# Optimizing a Trainium2 kernel written in Bass

```python
import numpy as np
import jax
import jax.numpy as jnp

def _softmax(x, axis=-1):
    return jax.nn.softmax(x, axis=axis)

def _gelu(x):
    return jax.nn.gelu(x, approximate=True)

def _silu(x):
    return jax.nn.silu(x)

def _sigmoid(x):
    return jax.nn.sigmoid(x)

def _layernorm(x, axis=-1, eps=1e-05):
    m = jnp.mean(x, axis=axis, keepdims=True)
    v = jnp.var(x, axis=axis, keepdims=True)
    return (x - m) / jnp.sqrt(v + eps)

def _scatter_add(tgt, idx, src, axis=0):
    return tgt.at[idx].add(src)

def _segment_sum(src, seg, n):
    return jax.ops.segment_sum(src, seg, n)
kernel_name = 'mk_decoder_postln_d1_seqx_r8_bb624a'

def setup_inputs(seed: int=0):
    np.random.seed(seed)
    _w = jnp.asarray

    def _rec_inputs():
        import jax
        import jax.numpy as jnp
        _rk = jax.random.key(seed)
        x = 0.000341 + 1 * jax.random.normal(jax.random.fold_in(_rk, 1), (8, 128, 256), jnp.float32)
        _lenS = 128 - jax.random.randint(jax.random.fold_in(_rk, 7), (8,), 0, max(1, 128 // 4) + 1, jnp.int32)
        _lenS2 = 128 - jax.random.randint(jax.random.fold_in(_rk, 8), (8,), 0, max(1, 128 // 4) + 1, jnp.int32)
        _ctx_2048P = jax.random.normal(jax.random.fold_in(_rk, 11), (8, 16, 256), jnp.float32)
        _ctx_2048c = jax.random.dirichlet(jax.random.fold_in(_rk, 511), 0.3 * jnp.ones((16,), jnp.float32), (8, 128))
        _ctx_2048t = jnp.einsum('bsk,bkd->bsd', _ctx_2048c, _ctx_2048P)
        _ctx_2048t = _ctx_2048t * jax.lax.rsqrt(jnp.mean(jnp.square(_ctx_2048t)) + 1e-12) * 0.953939
        ctx_2048 = -1.47943e-05 + 1.00017 * (_ctx_2048t + 0.3 * jax.random.normal(jax.random.fold_in(_rk, 611), (8, 128, 256), jnp.float32))
        return (x, ctx_2048)
    x, ctx_2048 = _rec_inputs()

    def _L0_attn_setup():
        import jax, jax.numpy as jnp
        import numpy as np
        import math
        B, L, D = (2, 256, 256)
        H, DH = (16, 128)
        R = 16
        WIN = 64
        EPS = 1e-06

        def _lora_proj(h, Wb, A, Bm, scale):
            return h @ Wb.T + h @ A.T @ Bm.T * scale

        def _rope_freqs(seq_len, d_head):
            half = d_head // 2
            theta = 1.0 / 10000.0 ** (jnp.arange(half, dtype=jnp.float32) / half)
            freqs = jnp.arange(seq_len, dtype=jnp.float32)[:, None] * theta[None, :]
            emb = jnp.concatenate([freqs, freqs], axis=-1)
            return (jnp.cos(emb), jnp.sin(emb))

        def _apply_rope(x, cos, sin):
            half = x.shape[-1] // 2
            x1, x2 = (x[..., :half], x[..., half:])
            rotated = jnp.concatenate([-x2, x1], axis=-1)
            return x * cos[None, None] + rotated * sin[None, None]
        key = jax.random.key(seed)
        ks = jax.random.split(key, 16)

        def rn(k, shape, s=1.0):
            return jax.random.normal(k, shape, dtype=jnp.float32) * s
        d_in_std = 1.0 / math.sqrt(D)
        return {'x': rn(ks[0], (B, L, D)), 'norm_w': jnp.ones((D,), jnp.float32), 'wq': rn(ks[1], (H * DH, D), d_in_std), 'wk': rn(ks[2], (H * DH, D), d_in_std), 'wv': rn(ks[3], (H * DH, D), d_in_std), 'wo': rn(ks[4], (D, H * DH), d_in_std), 'qA': rn(ks[5], (R, D), 0.02), 'qB': rn(ks[6], (H * DH, R), 0.02), 'kA': rn(ks[7], (R, D), 0.02), 'kB': rn(ks[8], (H * DH, R), 0.02), 'vA': rn(ks[9], (R, D), 0.02), 'vB': rn(ks[10], (H * DH, R), 0.02), 'oA': rn(ks[11], (R, H * DH), 0.02), 'oB': rn(ks[12], (D, R), 0.02)}
    _L0_attn_all = _L0_attn_setup()
    _L0_attn_in = {k: v for k, v in _L0_attn_all.items() if k in ('norm_w', 'wq', 'wk', 'wv', 'wo', 'qA', 'qB', 'kA', 'kB', 'vA', 'vB', 'oA', 'oB')}
    del _L0_attn_all

    def _L0_xattn_setup():
        import jax, jax.numpy as jnp
        import numpy as np

        def _wkv(time_decay, time_first, k, v):
            w = -jnp.exp(time_decay)
            u = time_first
            B, T, C = k.shape
            aa = jnp.zeros((B, C), dtype=k.dtype)
            bb = jnp.zeros((B, C), dtype=k.dtype)
            pp = jnp.full((B, C), -1e+38, dtype=k.dtype)

            def step(carry, kv_t):
                aa, bb, pp = carry
                kt, vt = kv_t
                ww = u + kt
                q = jnp.maximum(pp, ww)
                e1 = jnp.exp(pp - q)
                e2 = jnp.exp(ww - q)
                y_t = (e1 * aa + e2 * vt) / (e1 * bb + e2)
                ww2 = pp + w
                q2 = jnp.maximum(ww2, kt)
                e1b = jnp.exp(ww2 - q2)
                e2b = jnp.exp(kt - q2)
                new_carry = (e1b * aa + e2b * vt, e1b * bb + e2b, q2)
                return (new_carry, y_t)
            ks = jnp.transpose(k, (1, 0, 2))
            vs = jnp.transpose(v, (1, 0, 2))
            _, ys = jax.lax.scan(step, (aa, bb, pp), (ks, vs))
            return jnp.transpose(ys, (1, 0, 2))
        key = jax.random.key(seed)
        k1, k2, k3, k4 = jax.random.split(key, 4)
        B, T, C = (8, 128, 256)
        return {'batch_size': B, 'seq_len': T, 'embedding_dim': C, 'time_decay': jax.random.normal(k1, (C,), dtype=jnp.float32), 'time_first': jax.random.normal(k2, (C,), dtype=jnp.float32), 'k': jax.random.normal(k3, (B, T, C), dtype=jnp.float32), 'v': jax.random.normal(k4, (B, T, C), dtype=jnp.float32)}
    _L0_xattn_all = _L0_xattn_setup()
    _L0_xattn_in = {k: v for k, v in _L0_xattn_all.items() if k in ('time_decay', 'time_first')}
    del _L0_xattn_all

    def _L0_ffn_setup():
        import jax, jax.numpy as jnp
        import numpy as np
        HIDDEN = 256
        INTER = 1024
        COMPRESSION = 128.9

        def _n_ctrl(out_size, in_size):
            return max(16, int(out_size * in_size / COMPRESSION))

        def _catmull_rom_grid(n_ctrl, n_samples):
            t = np.linspace(0.0, n_ctrl - 1.0, n_samples, dtype=np.float64)
            i = np.clip(np.floor(t).astype(np.int64), 0, n_ctrl - 2)
            f = (t - i).astype(np.float32)
            idx = np.stack([np.clip(i + k, 0, n_ctrl - 1) for k in (-1, 0, 1, 2)], axis=0)
            return (jnp.asarray(idx.astype(np.int32)), jnp.asarray(f))

        def spline_reconstruct(control_points, out_size, in_size):
            n = out_size * in_size
            idx, f = _catmull_rom_grid(control_points.shape[0], n)
            p0, p1, p2, p3 = (control_points[idx[0]], control_points[idx[1]], control_points[idx[2]], control_points[idx[3]])
            f2 = f * f
            f3 = f2 * f
            w = 0.5 * (2.0 * p1 + (p2 - p0) * f + (2.0 * p0 - 5.0 * p1 + 4.0 * p2 - p3) * f2 + (3.0 * p1 - p0 - 3.0 * p2 + p3) * f3)
            return w.reshape(out_size, in_size)
        key = jax.random.key(seed)
        k0, k1, k2, k3 = jax.random.split(key, 4)
        hidden_states = jax.random.normal(k0, (4, 256, HIDDEN), dtype=jnp.float32)
        gate_cp = jax.random.normal(k1, (_n_ctrl(INTER, HIDDEN),), dtype=jnp.float32) * 0.02
        up_cp = jax.random.normal(k2, (_n_ctrl(INTER, HIDDEN),), dtype=jnp.float32) * 0.02
        down_cp = jax.random.normal(k3, (_n_ctrl(HIDDEN, INTER),), dtype=jnp.float32) * 0.02
        return {'hidden_states': hidden_states, 'gate_cp': gate_cp, 'up_cp': up_cp, 'down_cp': down_cp}
    _L0_ffn_all = _L0_ffn_setup()
    _L0_ffn_in = {k: v for k, v in _L0_ffn_all.items() if k in ('gate_cp', 'up_cp', 'down_cp')}
    del _L0_ffn_all
    return {'x': x, 'ctx_2048': ctx_2048, 'L0_attn_norm_w': _L0_attn_in['norm_w'], 'L0_attn_wq': _L0_attn_in['wq'], 'L0_attn_wk': _L0_attn_in['wk'], 'L0_attn_wv': _L0_attn_in['wv'], 'L0_attn_wo': _L0_attn_in['wo'], 'L0_attn_qA': _L0_attn_in['qA'], 'L0_attn_qB': _L0_attn_in['qB'], 'L0_attn_kA': _L0_attn_in['kA'], 'L0_attn_kB': _L0_attn_in['kB'], 'L0_attn_vA': _L0_attn_in['vA'], 'L0_attn_vB': _L0_attn_in['vB'], 'L0_attn_oA': _L0_attn_in['oA'], 'L0_attn_oB': _L0_attn_in['oB'], 'L0_xattn_time_decay': _L0_xattn_in['time_decay'], 'L0_xattn_time_first': _L0_xattn_in['time_first'], 'L0_ffn_gate_cp': _L0_ffn_in['gate_cp'], 'L0_ffn_up_cp': _L0_ffn_in['up_cp'], 'L0_ffn_down_cp': _L0_ffn_in['down_cp']}

def reference(x, ctx_2048, L0_attn_norm_w, L0_attn_wq, L0_attn_wk, L0_attn_wv, L0_attn_wo, L0_attn_qA, L0_attn_qB, L0_attn_kA, L0_attn_kB, L0_attn_vA, L0_attn_vB, L0_attn_oA, L0_attn_oB, L0_xattn_time_decay, L0_xattn_time_first, L0_ffn_gate_cp, L0_ffn_up_cp, L0_ffn_down_cp):
    import jax
    import jax.numpy as jnp

    def _L0_attn_ref(x, norm_w, wq, wk, wv, wo, qA, qB, kA, kB, vA, vB, oA, oB):
        import jax, jax.numpy as jnp
        import numpy as np
        import math
        B, L, D = (2, 256, 256)
        H, DH = (16, 128)
        R = 16
        WIN = 64
        EPS = 1e-06

        def _lora_proj(h, Wb, A, Bm, scale):
            return h @ Wb.T + h @ A.T @ Bm.T * scale

        def _rope_freqs(seq_len, d_head):
            half = d_head // 2
            theta = 1.0 / 10000.0 ** (jnp.arange(half, dtype=jnp.float32) / half)
            freqs = jnp.arange(seq_len, dtype=jnp.float32)[:, None] * theta[None, :]
            emb = jnp.concatenate([freqs, freqs], axis=-1)
            return (jnp.cos(emb), jnp.sin(emb))

        def _apply_rope(x, cos, sin):
            half = x.shape[-1] // 2
            x1, x2 = (x[..., :half], x[..., half:])
            rotated = jnp.concatenate([-x2, x1], axis=-1)
            return x * cos[None, None] + rotated * sin[None, None]
        lora_scale = 1.0 / qA.shape[0]
        residual = x
        h = x * jax.lax.rsqrt(jnp.mean(x * x, axis=-1, keepdims=True) + EPS) * norm_w
        Q = _lora_proj(h, wq, qA, qB, lora_scale)
        K = _lora_proj(h, wk, kA, kB, lora_scale)
        V = _lora_proj(h, wv, vA, vB, lora_scale)
        b, l, _ = x.shape
        Q = Q.reshape(b, l, H, DH).transpose(0, 2, 1, 3)
        K = K.reshape(b, l, H, DH).transpose(0, 2, 1, 3)
        V = V.reshape(b, l, H, DH).transpose(0, 2, 1, 3)
        cos, sin = _rope_freqs(l, DH)
        Q = _apply_rope(Q, cos, sin)
        K = _apply_rope(K, cos, sin)
        i = jnp.arange(l)[:, None]
        j = jnp.arange(l)[None, :]
        valid = (j <= i) & (j >= i - WIN + 1)
        mask = jnp.where(valid, 0.0, -jnp.inf).astype(x.dtype)
        scores = jnp.einsum('bhqd,bhkd->bhqk', Q, K) / math.sqrt(DH)
        attn = jax.nn.softmax(scores + mask[None, None], axis=-1)
        out = jnp.einsum('bhqk,bhkd->bhqd', attn, V)
        out = out.transpose(0, 2, 1, 3).reshape(b, l, H * DH)
        out = _lora_proj(out, wo, oA, oB, lora_scale)
        return residual + out

    def _L0_xattn_ref(batch_size, seq_len, embedding_dim, time_decay, time_first, k, v):
        import jax, jax.numpy as jnp
        import numpy as np

        def _wkv(time_decay, time_first, k, v):
            w = -jnp.exp(time_decay)
            u = time_first
            B, T, C = k.shape
            aa = jnp.zeros((B, C), dtype=k.dtype)
            bb = jnp.zeros((B, C), dtype=k.dtype)
            pp = jnp.full((B, C), -1e+38, dtype=k.dtype)

            def step(carry, kv_t):
                aa, bb, pp = carry
                kt, vt = kv_t
                ww = u + kt
                q = jnp.maximum(pp, ww)
                e1 = jnp.exp(pp - q)
                e2 = jnp.exp(ww - q)
                y_t = (e1 * aa + e2 * vt) / (e1 * bb + e2)
                ww2 = pp + w
                q2 = jnp.maximum(ww2, kt)
                e1b = jnp.exp(ww2 - q2)
                e2b = jnp.exp(kt - q2)
                new_carry = (e1b * aa + e2b * vt, e1b * bb + e2b, q2)
                return (new_carry, y_t)
            ks = jnp.transpose(k, (1, 0, 2))
            vs = jnp.transpose(v, (1, 0, 2))
            _, ys = jax.lax.scan(step, (aa, bb, pp), (ks, vs))
            return jnp.transpose(ys, (1, 0, 2))
        assert seq_len <= 128
        return _wkv(time_decay, time_first, k, v)

    def _L0_ffn_ref(hidden_states, gate_cp, up_cp, down_cp):
        import jax, jax.numpy as jnp
        import numpy as np
        HIDDEN = 256
        INTER = 1024
        COMPRESSION = 128.9

        def _n_ctrl(out_size, in_size):
            return max(16, int(out_size * in_size / COMPRESSION))

        def _catmull_rom_grid(n_ctrl, n_samples):
            t = np.linspace(0.0, n_ctrl - 1.0, n_samples, dtype=np.float64)
            i = np.clip(np.floor(t).astype(np.int64), 0, n_ctrl - 2)
            f = (t - i).astype(np.float32)
            idx = np.stack([np.clip(i + k, 0, n_ctrl - 1) for k in (-1, 0, 1, 2)], axis=0)
            return (jnp.asarray(idx.astype(np.int32)), jnp.asarray(f))

        def spline_reconstruct(control_points, out_size, in_size):
            n = out_size * in_size
            idx, f = _catmull_rom_grid(control_points.shape[0], n)
            p0, p1, p2, p3 = (control_points[idx[0]], control_points[idx[1]], control_points[idx[2]], control_points[idx[3]])
            f2 = f * f
            f3 = f2 * f
            w = 0.5 * (2.0 * p1 + (p2 - p0) * f + (2.0 * p0 - 5.0 * p1 + 4.0 * p2 - p3) * f2 + (3.0 * p1 - p0 - 3.0 * p2 + p3) * f3)
            return w.reshape(out_size, in_size)
        gate_w = spline_reconstruct(gate_cp, INTER, HIDDEN)
        up_w = spline_reconstruct(up_cp, INTER, HIDDEN)
        down_w = spline_reconstruct(down_cp, HIDDEN, INTER)
        gate = jnp.einsum('bsh,ih->bsi', hidden_states, gate_w)
        up = jnp.einsum('bsh,ih->bsi', hidden_states, up_w)
        inter = jax.nn.silu(gate) * up
        return jnp.einsum('bsi,hi->bsh', inter, down_w)
    x = _layernorm(x + _L0_attn_ref(x, L0_attn_norm_w, L0_attn_wq, L0_attn_wk, L0_attn_wv, L0_attn_wo, L0_attn_qA, L0_attn_qB, L0_attn_kA, L0_attn_kB, L0_attn_vA, L0_attn_vB, L0_attn_oA, L0_attn_oB), axis=-1)
    x = _layernorm(x + _L0_xattn_ref(8, 128, 256, L0_xattn_time_decay, L0_xattn_time_first, x, ctx_2048), axis=-1)
    x = _layernorm(x + _L0_ffn_ref(x, L0_ffn_gate_cp, L0_ffn_up_cp, L0_ffn_down_cp), axis=-1)
    return x

_drawn_inputs = setup_inputs


def setup_inputs(seed=0):
    import zlib

    import numpy as np

    out = dict(_drawn_inputs(seed))
    spreads = {'L0_attn_norm_w': (1.0, 0.2)}
    factors = {'L0_attn_qA': 8.0,
     'L0_attn_qB': 8.0,
     'L0_attn_kA': 8.0,
     'L0_attn_kB': 8.0,
     'L0_attn_vA': 8.0,
     'L0_attn_vB': 8.0,
     'L0_attn_oA': 8.0,
     'L0_attn_oB': 8.0,
     'L0_ffn_up_cp': 2.955,
     'L0_ffn_down_cp': 3.13}
    for name, (base, spread) in spreads.items():
        noise = np.random.default_rng([zlib.crc32(name.encode()), seed]).standard_normal(out[name].shape)
        drawn = base * np.exp(spread * noise) if base else spread * noise
        out[name] = jnp.asarray(drawn.astype(out[name].dtype))
    for name, factor in factors.items():
        out[name] = (out[name] * factor).astype(out[name].dtype)
    return out
```

```python
from contextlib import ExitStack

import concourse.bass as bass
from concourse import mybir

F32 = mybir.dt.float32
F32R = mybir.dt.float32r
BF16 = mybir.dt.bfloat16
I32 = mybir.dt.int32
ALU = mybir.AluOpType
ACT = mybir.ActivationFunctionType
AX = mybir.AxisListType

P = 128
B, T, D = 8, 128, 256
H, DH = 16, 128
RANK = 16
WINDOW = 64
INTER = 1024
PAIRS = H // 2
GROUPS = 2
GB = B // GROUPS
GT = GB * T
DC = D // P
UNITS = PAIRS * GROUPS * 2
IB = INTER // P
CHUNK = 256
COLUMNS = D * INTER // P
RMS_EPS = 1e-6
LN_EPS = 1e-5
LORA_SCALE = 1.0 / RANK
NO_STATE = -1e38
FORGET = -2e38
MASKED = -3e38

RING = 4
BLK_LQK1, BLK_Q0, BLK_K0, BLK_LV = 0, 1, 2, 3
BLK_Q1, BLK_K1, BLK_V0 = 4, 5, 6
BLK_Q2, BLK_K2, BLK_LWO, BLK_GEN = 8, 9, 10, 11
BLK_LQK0, BLK_Q3, BLK_K3, BLK_V1 = 14, 15, 16, 17
PAIR_BLOCKS = 19
FIRST_BLOCKS = 5
BLK_Q = [BLK_Q0, BLK_Q1, BLK_Q2, BLK_Q3]
BLK_K = [BLK_K0, BLK_K1, BLK_K2, BLK_K3]
MID = {BLK_Q0: 0, BLK_K0: 1, BLK_Q1: 2, BLK_K1: 3, 6: 4, 7: 5, BLK_Q2: 6, BLK_K2: 7, 11: 8, 12: 9, 13: 10,
       BLK_Q3: 11, BLK_K3: 12, 17: 13, 18: 14}
PAIR_MIDS = 15
WKV_DVE, WKV_POOL, WKV_ACT = 10, 6, 4
FIRST_MIDS = 4


def block_at(p, k):
    if isinstance(p, int) and p == PAIRS - 1 and k > BLK_LQK0:
        k -= 1
    return FIRST_BLOCKS + PAIR_BLOCKS * p + k


def mid_at(p, k):
    return FIRST_MIDS + PAIR_MIDS * p + MID[k]


def bank_user_before(p, k):
    if k >= RING:
        return block_at(p, k - RING)
    if isinstance(p, int) and p == 0:
        return [0, 1, 4, 3][k]
    return block_at(p, {0: 16, 1: 17, 2: 18, 3: 15}[k]) - PAIR_BLOCKS


def wait_for(engine, sem, count):
    if isinstance(count, int) and count <= 0:
        return
    engine.wait_ge(sem, count)


def decoder_layer(nc, x, ctx_t, small, consts, lora_a, lora_b, w_qkv, w_o, knots, spline, piece, out):
    with ExitStack() as stack:
        def sb(name, shape, dt=F32):
            return stack.enter_context(nc.sbuf_tensor(name, shape, dt))

        def ps(name):
            return stack.enter_context(nc.psum_tensor(name, [P, 512], F32))

        def sem(name):
            return stack.enter_context(nc.semaphore(name))

        x_raw = sb("x_raw", [P, B, D])
        acc = sb("acc", [P, B, D])
        xt_hi = sb("xt_hi", [P, DC, B * T], F32R)
        xt_lo = sb("xt_lo", [P, DC, B * T], F32R)
        v_t = sb("v_t", [P, DC, B * T])
        cst = sb("cst", [P, 9, P])
        sm = sb("sm", [P, 3, DC])
        ident_b = sb("ident_b", [P, P], BF16)
        mask_b = sb("mask_b", [P, P], BF16)
        phi = sb("phi", [P, 3, P], F32R)
        rope_cos = [cst[:, 0, :], cst[:, 2, :]]
        rope_sin = [cst[:, 1, :], cst[:, 3, :]]
        ident = cst[:, 4, :]

        la = sb("la", [96, 4, D], F32R)
        lb_raw = sb("lb_raw", [96, 3 * D])
        lb = sb("lb", [96, 3 * D], F32R)
        w_raw = sb("w_raw", [P, 3, 512])
        wo_raw = sb("wo_raw", [P, 512])
        w_sum = sb("w_sum", [P, 512])
        wqk = [[sb(f"wqk{hh}_{part}", [P, 4, P], F32R) for part in ("hi", "lo")] for hh in range(2)]
        wv = [sb(f"wv_{part}", [P, DC, 2 * DH], F32R) for part in ("hi", "lo")]
        wo = [sb(f"wo_{part}", [P, 2, D], F32R) for part in ("hi", "lo")]

        straight = [sb(f"straight{n}", [P, GB, T]) for n in range(2)]
        turned = [sb(f"turned{n}", [P, GB, T]) for n in range(2)]
        q_t = [sb(f"q_t{n}", [P, GB, T]) for n in range(2)]
        k_t = [sb(f"k_t{n}", [P, GB, T]) for n in range(2)]
        v_hi = [sb(f"v_hi{g}", [P, GB, 2 * DH], F32R) for g in range(GROUPS)]
        v_lo = [sb(f"v_lo{g}", [P, GB, 2 * DH], F32R) for g in range(GROUPS)]
        prob = [sb(f"prob{n}", [P, GB, T]) for n in range(2)]
        pt_hi = sb("pt_hi", [P, GB, T], F32R)
        pt_lo = sb("pt_lo", [P, GB, T], F32R)
        ot_hi = sb("ot_hi", [P, GB, T], F32R)
        ot_lo = sb("ot_lo", [P, GB, T], F32R)
        neg_max = sb("neg_max", [P, GB])
        row_sum = sb("row_sum", [P, GB])
        row_inv = sb("row_inv", [P, GB])

        knot_rows = sb("knot_rows", [96, CHUNK])
        spline_tab = sb("spline_tab", [96, 2, CHUNK])
        second = sb("second", [P, CHUNK], I32)
        coef = sb("coef", [96, 2, CHUNK])
        coef_hi = sb("coef_hi", [96, 2, CHUNK], F32R)
        coef_lo = sb("coef_lo", [96, 2, CHUNK], F32R)
        made = sb("made", [P, CHUNK])
        fw = [[sb(f"fw{w}_{part}", [P, COLUMNS], F32R) for part in ("hi", "lo")] for w in range(3)]

        squares = sb("squares", [P, D])
        sum_sq = sb("sum_sq", [P, B])
        mean_sq = sb("mean_sq", [P, B])
        rms_inv = sb("rms_inv", [P, B])
        half = sb("half", [P, B])
        stats = sb("stats", [P, GB, 6])
        mean_var = sb("mean_var", [P, GB, 2])
        var_eps = sb("var_eps", [P, GB])
        ln_inv = sb("ln_inv", [P, GB])

        decay = sb("decay", [P, DC])
        decay_tab = [sb(f"decay_tab{c}", [P, GB, T + 1]) for c in range(DC)]
        scan_bufs = sb("scan_bufs", [P, 7, GB * (T + 1)])
        k_ext, top, keep, add_k, add_v, aa, bb = [
            scan_bufs[:, n, :].rearrange("p (b t) -> p b t", b=GB) for n in range(7)]
        la_raw = scan_bufs[0:96, 0:2, :].rearrange("p a n -> p (a n)")[:, 0:4 * D].rearrange("p (k n) -> p k n", k=4)
        peak, e_old, e_new = q_t[0], q_t[1], k_t[0]
        y_t = [k_t[1], straight[0]]
        den_inv = straight[1]
        num = turned[0]
        den = turned[1]
        gated = [prob[0], prob[1]]
        th = [v_hi[0][:, 0:2, :], v_hi[0][:, 2:4, :]]

        ring = [ps(f"ring{n}") for n in range(RING)]
        s_bank = ps("s_bank")
        to_bank = ps("to_bank")
        wo_bank = [ps(f"wo_bank{n}") for n in range(2)]

        got_x, got_small, got_cst, got_la = sem("got_x"), sem("got_small"), sem("got_cst"), sem("got_la")
        got_lb, got_w, got_wo = sem("got_lb"), sem("got_w"), sem("got_wo")
        got_knots, got_tab, got_second, got_v = sem("got_knots"), sem("got_tab"), sem("got_second"), sem("got_v")
        stored = sem("stored")
        squared, rms_step, rms_ready, x_normed = sem("squared"), sem("rms_step"), sem("rms_ready"), sem("x_normed")
        half_set = sem("half_set")
        acc_set, small_cast, phi_cast = sem("acc_set"), sem("small_cast"), sem("phi_cast")
        la_hi_ready, la_ready = sem("la_hi_ready"), sem("la_ready")
        blk_full, blk_mid, blk_free = sem("blk_full"), sem("blk_mid"), sem("blk_free")
        lb_hi_ready, lb_ready = sem("lb_hi_ready"), sem("lb_ready")
        w_hi_ready, w_ready = sem("w_hi_ready"), sem("w_ready")
        coef_made, coef_hi_ready, coef_ready = sem("coef_made"), sem("coef_hi_ready"), sem("coef_ready")
        piece_due = sem("piece_due")
        fw_hi_ready, fw_ready = sem("fw_hi_ready"), sem("fw_ready")
        turned_ready, q_ready, k_ready = sem("turned_ready"), sem("q_ready"), sem("k_ready")
        scores_ready, max_ready, exp_ready = sem("scores_ready"), sem("max_ready"), sem("exp_ready")
        inv_ready, prob_ready = sem("inv_ready"), sem("prob_ready")
        pt_full, pt_hi_ready, pt_ready = sem("pt_full"), sem("pt_hi_ready"), sem("pt_ready")
        ot_full, ot_hi_ready, ot_ready = sem("ot_full"), sem("ot_hi_ready"), sem("ot_ready")
        wo_full, acc_added = sem("wo_full"), sem("acc_added")
        stats_step, stats_ready, ln_step, ln_inv_ready, ln_ready = (
            sem("stats_step"), sem("stats_ready"), sem("ln_step"), sem("ln_inv_ready"), sem("ln_ready"))
        tables_step, tables_ready = sem("tables_step"), sem("tables_ready")
        exts_set = sem("exts_set")
        decay_exp = sem("decay_exp")
        x1t_full, k_copied = sem("x1t_full"), sem("k_copied")
        wkv_dve, wkv_pool, wkv_act = sem("wkv_dve"), sem("wkv_pool"), sem("wkv_act")
        y_full, y_added = sem("y_full"), sem("y_added")
        x2t_full, x2t_hi, x2t_ready = sem("x2t_full"), sem("x2t_hi"), sem("x2t_ready")
        gate_full, up_full, tanh_ready = sem("gate_full"), sem("up_full"), sem("tanh_ready")
        gate_used, up_used = sem("gate_used"), sem("up_used")
        inter_hi, inter_ready, down_full, down_added = (
            sem("inter_hi"), sem("inter_ready"), sem("down_full"), sem("down_added"))

        def weight_views(w, p, part):
            if w < 2:
                dst = fw[w][part][:, bass.ds(CHUNK * p, CHUNK)].rearrange("p (h i) -> p h i", h=DC)
                return dst, made[:, :].rearrange("p (i h) -> p h i", h=DC)
            per = CHUNK // IB
            dst = fw[w][part][:, :].rearrange("p (i h) -> p i h", i=IB)[:, :, bass.ds(per * p, per)]
            return dst, made[:, :].rearrange("p (h i) -> p i h", i=IB)

        block = stack.enter_context(nc.Block())

        @block.sync
        def _(sp):
            def three_times(dst, src):
                for n in range(3):
                    ins = sp.dma_start(dst[32 * n:32 * n + 32], src)
                    yield ins

            def load_lora_b(e):
                for ins in three_times(lb_raw, lora_b[bass.ds(e, 1), :, :].rearrange("a r n -> (a r) n")):
                    ins.then_inc(got_lb, 16)

            def load_w(p):
                sp.dma_start(w_raw[:, :, :].rearrange("p k n -> p (k n)"),
                             w_qkv[bass.ds(p, 1), :, :].rearrange("a p n -> (a p) n")).then_inc(got_w, 16)

            def load_wo(p):
                sp.dma_start(wo_raw[:, :], w_o[bass.ds(p, 1), :, :].rearrange("a p n -> (a p) n")
                             ).then_inc(got_wo, 16)

            def load_spline(p):
                sp.dma_start(knot_rows[:, :], knots[bass.ds(p, 1), :, :].rearrange("a p n -> (a p) n")
                             ).then_inc(got_knots, 16)
                for n in range(3):
                    sp.dma_start(spline_tab[32 * n:32 * n + 32, :, :].rearrange("p k n -> p (k n)"),
                                 spline[bass.ds(p, 1), :, :].rearrange("a p n -> (a p) n")).then_inc(got_tab, 16)

            def load_piece(p):
                sp.dma_start(second[:, :], piece[bass.ds(p, 1), :, :].rearrange("a p n -> (a p) n")
                             ).then_inc(got_second, 16)

            x_view = x.rearrange("b t d -> t b d")
            for g in range(GROUPS):
                sp.dma_start(x_raw[:, GB * g:GB * g + GB, :], x_view[:, GB * g:GB * g + GB, :]).then_inc(got_x, 16)
            load_lora_b(0)
            for n in range(3):
                sp.dma_start(la_raw[32 * n:32 * n + 32, :, :].rearrange("p k n -> p (k n)"), lora_a).then_inc(got_la, 16)
            load_w(0)
            load_spline(0)
            load_piece(0)
            load_wo(0)
            sp.dma_start(v_t[:, :, :], ctx_t.rearrange("(c p) t -> p c t", p=P)).then_inc(got_v, 16)
            sp.wait_ge(lb_ready, 1)
            load_lora_b(1)

            with sp.Fori(0, PAIRS - 1) as i:
                sp.wait_ge(blk_free, block_at(i, BLK_LV) + 1)
                load_w(i + 1)
                sp.wait_ge(coef_made, i + 1)
                load_spline(i + 1)
                sp.wait_ge(lb_ready, i + 2)
                load_lora_b(i + 2)
                sp.wait_ge(blk_free, block_at(i, BLK_LWO) + 1)
                load_wo(i + 1)
                sp.wait_ge(blk_free, block_at(i, BLK_GEN + 2) + 1)
                load_piece(i + 1)

            out_view = out.rearrange("b t d -> t b d")
            for g in range(GROUPS):
                sp.wait_ge(ln_ready, GB * (4 + g + 1))
                sp.dma_start(out_view[:, GB * g:GB * g + GB, :], x_raw[:, GB * g:GB * g + GB, :]).then_inc(stored, 16)
            sp.wait_ge(stored, 16 * GROUPS)

        @block.tensor
        def _(pe):
            def product(dst, lhs, rhs, first, last):
                (lh, ll), (rh, rl) = lhs, rhs
                pe.matmul(dst, lh, rh, start=first, stop=False, skip_group_check=True)
                pe.matmul(dst, lh, rl, start=False, stop=False, skip_group_check=True)
                return pe.matmul(dst, ll, rh, start=False, stop=last, skip_group_check=True)

            def bank_for(p, k):
                wait_for(pe, blk_free, bank_user_before(p, k) + 1)
                return ring[k % RING]

            def lora_qk(p, hh, k):
                bank = bank_for(p, k)
                for m in range(2):
                    for dc in range(DC):
                        n = 2 * m + dc
                        mm = pe.matmul(bank[:, P * n:P * n + P], la[:, m, P * dc:P * dc + P],
                                       lb[:, P * hh:P * hh + P], start=True, stop=True)
                mm.then_inc(blk_full, 1)

            def lora_v(p):
                bank = bank_for(p, BLK_LV)
                for dc in range(DC):
                    mm = pe.matmul(bank[:, 256 * dc:256 * dc + 256], la[:, 2, P * dc:P * dc + P],
                                   lb[:, 256:512], start=True, stop=True)
                mm.then_inc(blk_full, 1)

            def lora_o(p):
                wait_for(pe, lb_ready, p + 2)
                bank = bank_for(p, BLK_LWO)
                for hh in range(2):
                    mm = pe.matmul(bank[:, 256 * hh:256 * hh + 256], lb[:, 512 + P * hh:512 + P * hh + P],
                                   la[:, 3, :], start=True, stop=True)
                mm.then_inc(blk_full, 1)

            def project(p, c, m):
                g, hh = c // 2, c % 2
                wait_for(pe, w_ready, 4 * p + 1 + hh)
                bank = bank_for(p, (BLK_Q, BLK_K)[m][c])
                cols = slice(GT * g, GT * g + GT)
                for dc in range(DC):
                    w = [wqk[hh][part][:, 2 * m + dc, :] for part in range(2)]
                    mm = product(bank[:, :], w, (xt_hi[:, dc, cols], xt_lo[:, dc, cols]), dc == 0, dc == DC - 1)
                mm.then_inc(blk_full, 1)

            def values(p, g):
                wait_for(pe, w_ready, 4 * p + 3)
                for j in range(2):
                    bank = bank_for(p, (BLK_V0, BLK_V1)[g] + j)
                    for n in range(2):
                        b = GB * g + 2 * j + n
                        for dc in range(DC):
                            xs = [t[:, dc, T * b:T * b + T] for t in (xt_hi, xt_lo)]
                            mm = product(bank[:, 256 * n:256 * n + 256], xs, [wv[part][:, dc, :] for part in range(2)],
                                         dc == 0, dc == DC - 1)
                    mm.then_inc(blk_full, 1)

            def spline_weights(p):
                wait_for(pe, coef_ready, p + 1)
                for w in range(3):
                    bank = bank_for(p, BLK_GEN + w)
                    pe.matmul(bank[:, :], phi[0:96, w, :], coef_hi[:, :, :].rearrange("p a n -> p (a n)"),
                              start=True, stop=False)
                    pe.matmul(bank[:, :], phi[0:96, w, :], coef_lo[:, :, :].rearrange("p a n -> p (a n)"),
                              start=False, stop=True).then_inc(blk_full, 1)

            def scores(u, par):
                wait_for(pe, q_ready, u + 1)
                wait_for(pe, k_ready, u + 1)
                wait_for(pe, exp_ready, u)
                pe.matmul(s_bank[:, :], ident_b[:, :], mask_b[:, :].unsqueeze(1).to_broadcast([P, GB, T]),
                          start=True, stop=False)
                for b in range(GB):
                    mm = pe.matmul(s_bank[:, T * b:T * b + T], q_t[par][:, b, :], k_t[par][:, b, :],
                                   start=False, stop=b == GB - 1)
                mm.then_inc(scores_ready, 1)

            def turn_probs(u, par):
                wait_for(pe, prob_ready, u + 1)
                wait_for(pe, ot_ready, u)
                for b in range(GB):
                    mm = pe.transpose(to_bank[:, T * b:T * b + T], prob[par][:, b, :], ident)
                mm.then_inc(pt_full, 1)

            def probs_v(u, p, c):
                g, hh = c // 2, c % 2
                wait_for(pe, pt_ready, u + 1)
                wait_for(pe, blk_free, block_at(p, (BLK_V0, BLK_V1)[g] + 1) + 1)
                for b in range(GB):
                    v = [t[g][:, b, DH * hh:DH * hh + DH] for t in (v_hi, v_lo)]
                    mm = product(to_bank[:, T * b:T * b + T], v, (pt_hi[:, b, :], pt_lo[:, b, :]), True, True)
                mm.then_inc(ot_full, 1)

            def out_project(u, p, c):
                g, hh = c // 2, c % 2
                wait_for(pe, ot_ready, u + 1)
                if hh == 0:
                    wait_for(pe, w_ready, 4 * p + 4)
                    wait_for(pe, acc_added, 4 * p + 2 * g)
                for b in range(GB):
                    o = (ot_hi[:, b, :], ot_lo[:, b, :])
                    mm = product(wo_bank[b // 2][:, 256 * (b % 2):256 * (b % 2) + 256], o,
                                 [wo[part][:, hh, :] for part in range(2)], hh == 0 and b % 2 == 0, hh == 1)
                mm.then_inc(wo_full, 1)

            def slot(s, p, c):
                static = isinstance(s, int)
                active = not static or s < UNITS
                if c == 3 and (not static or p + 1 < PAIRS):
                    lora_qk(p, 0, BLK_LQK0)
                if c == 0 and active:
                    lora_qk(p, 1, BLK_LQK1)
                if active:
                    project(p, c, 0)
                    project(p, c, 1)
                if not static or 0 <= s - 2 < UNITS:
                    turn_probs(s - 2, c % 2)
                if not static or 0 <= s - 3 < UNITS:
                    out_project(s - 3, p - (c < 3), (c + 1) % 4)
                if not static or 0 <= s - 1 < UNITS:
                    scores(s - 1, (c + 1) % 2)
                if active:
                    if c == 0:
                        lora_v(p)
                    if c == 1:
                        values(p, 0)
                    if c == 2:
                        lora_o(p)
                        spline_weights(p)
                    if c == 3:
                        values(p, 1)
                if not static or 0 <= s - 2 < UNITS:
                    probs_v(s - 2, p - (c < 2), (c + 2) % 4)

            pe.wait_ge(got_cst, 16)
            for n in range(4):
                dc, g = n // 2, n % 2
                for j in range(GB):
                    b = GB * g + j
                    wait_for(pe, x_normed, b + 1)
                    mm = pe.transpose(ring[n][:, T * j:T * j + T], acc[:, b, P * dc:P * dc + P], ident)
                mm.then_inc(blk_full, 1)
            pe.wait_ge(la_ready, 1)
            pe.wait_ge(lb_ready, 1)
            pe.wait_ge(blk_free, 3)
            for m in range(2):
                for dc in range(DC):
                    n = 2 * m + dc
                    mm = pe.matmul(ring[2][:, P * n:P * n + P], la[:, m, P * dc:P * dc + P], lb[:, 0:P],
                                   start=True, stop=True)
            mm.then_inc(blk_full, 1)
            pe.wait_ge(blk_free, 4)
            pe.wait_ge(small_cast, 2)
            pe.wait_ge(phi_cast, 1)
            for s in range(3):
                slot(s, 0, s)
            with pe.Fori(0, PAIRS - 1) as i:
                for j in range(4):
                    slot(4 * i + 3 + j, i + (j > 0), (3 + j) % 4)
            for s in range(UNITS - 1, UNITS + 3):
                slot(s, s // 4, s % 4)

            def x1_to_channels(g):
                wait_for(pe, ln_ready, GB * (g + 1))
                wait_for(pe, blk_free, block_at(PAIRS - 1, 18) + 1)
                for c in range(DC):
                    for j in range(GB):
                        mm = pe.transpose(ring[2 * g + c][:, T * j:T * j + T],
                                          x_raw[:, GB * g + j, P * c:P * c + P], ident)
                    mm.then_inc(x1t_full, 1)

            def y_to_tokens(g):
                wait_for(pe, wkv_dve, WKV_DVE * DC * (g + 1))
                if g == 0:
                    wait_for(pe, exp_ready, UNITS)
                    wait_for(pe, ot_ready, UNITS)
                else:
                    wait_for(pe, x2t_ready, DC * g)
                for j, bank in enumerate((s_bank, to_bank)):
                    for n in range(2):
                        b = 2 * j + n
                        for c in range(DC):
                            mm = pe.transpose(bank[:, 256 * n + P * c:256 * n + P * c + P], y_t[c][:, b, :], ident)
                    mm.then_inc(y_full, 1)

            def x2_to_features(g):
                wait_for(pe, ln_ready, GB * (2 + g + 1))
                for c, bank in enumerate((s_bank, to_bank)):
                    for j in range(GB):
                        mm = pe.transpose(bank[:, T * j:T * j + T], x_raw[:, GB * g + j, P * c:P * c + P], ident)
                    mm.then_inc(x2t_full, 1)

            def down(g, ib):
                n = IB * g + ib
                wait_for(pe, inter_ready, n + 1)
                if ib == 0:
                    wait_for(pe, acc_added if g == 0 else down_added, 4 * PAIRS if g == 0 else 2 * g)
                for b in range(GB):
                    a = (pt_hi[:, b, :], pt_lo[:, b, :]) if n % 2 == 0 else (ot_hi[:, b, :], ot_lo[:, b, :])
                    mm = product(wo_bank[b // 2][:, 256 * (b % 2):256 * (b % 2) + 256], a,
                                 [fw[2][part][:, 256 * ib:256 * ib + 256] for part in range(2)],
                                 ib == 0 and b % 2 == 0, ib == IB - 1)
                mm.then_inc(down_full, 1)

            def ffn(g):
                cols = slice(GT * g, GT * g + GT)
                wait_for(pe, x2t_ready, DC * (g + 1))
                for ib in range(IB):
                    n = IB * g + ib
                    for w, full, used in ((0, gate_full, gate_used), (1, up_full, up_used)):
                        wait_for(pe, used, n - 1)
                        if n < 2:
                            wait_for(pe, k_copied, DC * GROUPS)
                        for hb in range(DC):
                            at = 256 * ib + P * hb
                            mm = product(ring[2 * (n % 2) + w][:, :], [fw[w][part][:, at:at + P] for part in range(2)],
                                         (xt_hi[:, hb, cols], xt_lo[:, hb, cols]), hb == 0, hb == DC - 1)
                        mm.then_inc(full, 1)
                    if ib > 0:
                        down(g, ib - 1)
                down(g, IB - 1)

            x1_to_channels(0)
            x1_to_channels(1)
            y_to_tokens(0)
            x2_to_features(0)
            wait_for(pe, fw_ready, 3 * PAIRS)
            ffn(0)
            y_to_tokens(1)
            x2_to_features(1)
            ffn(1)

        @block.scalar
        def _(act):
            copy = nc.scalar.activation

            def halves(p, c, m):
                k = (BLK_Q, BLK_K)[m][c]
                s = 4 * p + c
                wait_for(act, blk_full, block_at(p, k) + 1)
                wait_for(act, (q_ready, k_ready)[m], s)
                bank = ring[k % RING]
                flat = turned[m][:, :, :].rearrange("p b t -> p (b t)")
                copy(flat[0:64, :], bank[64:128, :], ACT.Copy)
                copy(flat[64:128, :], bank[0:64, :], ACT.Copy).then_inc(blk_mid, 1)

            def high_weights(n, dst, free):
                wait_for(act, blk_free, free)
                copy(dst, w_sum[:, :], ACT.Copy).then_inc(w_hi_ready, 1)

            def lora_high(e):
                wait_for(act, got_lb, 48 * (e + 1))
                copy(lb[:, :], lb_raw[:, :], ACT.Copy).then_inc(lb_hi_ready, 1)

            def flat3(t):
                return t.rearrange("p a b -> p (a b)")

            def slot(s, p, c):
                static = isinstance(s, int)
                active = not static or s < UNITS
                if c == 3 and (not static or p + 1 < PAIRS):
                    wait_for(act, blk_full, block_at(p, BLK_LQK0) + 1)
                    high_weights(4 * p + 4, flat3(wqk[0][0][:, :, :]), block_at(p, BLK_LQK0) + 1)
                if c == 0 and active:
                    wait_for(act, blk_full, block_at(p, BLK_LQK1) + 1)
                    high_weights(4 * p + 1, flat3(wqk[1][0][:, :, :]), block_at(p, BLK_LQK1) + 1)
                if active:
                    halves(p, c, 0)
                    halves(p, c, 1)
                if not static or 0 <= s - 2 < UNITS:
                    u = s - 2
                    wait_for(act, pt_full, u + 1)
                    wait_for(act, ot_full, u)
                    copy(flat3(pt_hi[:, :, :]), to_bank[:, :], ACT.Copy).then_inc(pt_hi_ready, 1)
                if not static or 0 <= s - 1 < UNITS:
                    u = s - 1
                    par = (c + 1) % 2
                    wait_for(act, max_ready, u + 1)
                    wait_for(act, pt_full, u - 1)
                    wait_for(act, inv_ready, u)
                    for b in range(GB):
                        ins = copy(prob[par][:, b, :], s_bank[:, T * b:T * b + T], ACT.Exp,
                                   bias=neg_max[:, b:b + 1], scale=1.0, accum_out=row_sum[:, b:b + 1])
                    ins.then_inc(exp_ready, 1)
                if active:
                    if c == 0:
                        wait_for(act, blk_full, block_at(p, BLK_LV) + 1)
                        high_weights(4 * p + 2, flat3(wv[0][:, :, :]), block_at(p, BLK_LV) + 1)
                        wait_for(act, coef_made, p + 1)
                        if not static or p > 0:
                            wait_for(act, blk_full, block_at(p, BLK_GEN + 2) + 1 - PAIR_BLOCKS)
                        copy(flat3(coef_hi[:, :, :]), flat3(coef[:, :, :]), ACT.Copy).then_inc(coef_hi_ready, 1)
                    if c in (1, 3):
                        g = c // 2
                        wait_for(act, ot_full, 4 * p + 2 * g - 2)
                        for j in range(2):
                            k = (BLK_V0, BLK_V1)[g] + j
                            wait_for(act, blk_full, block_at(p, k) + 1)
                            copy(flat3(v_hi[g][:, 2 * j:2 * j + 2, :]), ring[k % RING][:, :], ACT.Copy
                                 ).then_inc(blk_mid, 1)
                    if c == 1:
                        wait_for(act, blk_full, block_at(p, BLK_LV) + 1)
                        lora_high(p + 1)
                    if c == 2:
                        wait_for(act, blk_full, block_at(p, BLK_LWO) + 1)
                        wait_for(act, wo_full, 4 * p)
                        high_weights(4 * p + 3, flat3(wo[0][:, :, :]), block_at(p, BLK_LWO) + 1)
                        for w in range(3):
                            k = BLK_GEN + w
                            wait_for(act, blk_full, block_at(p, k) + 1)
                            wait_for(act, fw_ready, 3 * p + w)
                            copy(made[:, :], ring[k % RING][:, 0:CHUNK], ACT.Copy).then_inc(blk_mid, 1)
                            wait_for(act, blk_free, block_at(p, k) + 1)
                            dst, src = weight_views(w, p, 0)
                            copy(dst, src, ACT.Copy).then_inc(fw_hi_ready, 1)
                if not static or 0 <= s - 2 < UNITS:
                    u = s - 2
                    wait_for(act, ot_full, u + 1)
                    wait_for(act, wo_full, u)
                    copy(flat3(ot_hi[:, :, :]), to_bank[:, :], ACT.Copy).then_inc(ot_hi_ready, 1)

            act.dma_start(sm[:, :, :], small).then_inc(got_small, 16)
            act.dma_start(cst[:, :, :], consts).then_inc(got_cst, 16)
            for b in range(B):
                wait_for(act, got_x, 32)
                if b:
                    act.wait_ge(squared, b)
                copy(squares[:, :], x_raw[:, b, :], ACT.Square, accum_out=sum_sq[:, b:b + 1]).then_inc(squared, 1)
            act.wait_ge(got_cst, 16)
            copy(phi[:, :, :], cst[:, 6:9, :], ACT.Copy).then_inc(phi_cast, 1)
            act.wait_ge(got_la, 48)
            copy(la[:, :, :], la_raw[:, :, :], ACT.Copy, scale=LORA_SCALE).then_inc(la_hi_ready, 1)
            lora_high(0)
            act.wait_ge(got_small, 16)
            for n in range(4):
                dc, g = n // 2, n % 2
                act.wait_ge(blk_full, n + 1)
                copy(xt_hi[:, dc, GT * g:GT * g + GT], ring[n][:, :], ACT.Copy, scale=sm[:, 0, dc:dc + 1]
                     ).then_inc(blk_mid, 1)
            copy(decay[:, :], sm[:, 1, :], ACT.Exp).then_inc(decay_exp, 1)
            act.wait_ge(blk_full, 5)
            high_weights(0, flat3(wqk[0][0][:, :, :]), 5)

            for s in range(3):
                slot(s, 0, s)
            with act.Fori(0, PAIRS - 1) as i:
                for j in range(4):
                    slot(4 * i + 3 + j, i + (j > 0), (3 + j) % 4)
            for s in range(UNITS - 1, UNITS + 3):
                slot(s, s // 4, s % 4)

            def wkv(g, c):
                n = DC * g + c
                wait_for(act, x1t_full, n + 1)
                wait_for(act, exts_set, 4)
                wait_for(act, wkv_dve, WKV_DVE * n)
                wait_for(act, wkv_pool, WKV_POOL * n)
                copy(k_ext[:, :, 1:], ring[n][:, :].rearrange("p (b t) -> p b t", b=GB), ACT.Copy).then_inc(k_copied, 1)
                for buf, engine_sem, count in ((e_old[:, :, :], wkv_pool, WKV_POOL * n + 1),
                                               (e_new[:, :, :], wkv_dve, WKV_DVE * n + 3),
                                               (add_k[:, :, 1:], wkv_pool, WKV_POOL * n + 2),
                                               (keep[:, :, 1:], wkv_dve, WKV_DVE * n + 4)):
                    wait_for(act, engine_sem, count)
                    copy(buf, buf, ACT.Exp).then_inc(wkv_act, 1)

            def x2_high(g):
                for c, bank in enumerate((s_bank, to_bank)):
                    wait_for(act, x2t_full, DC * g + c + 1)
                    copy(xt_hi[:, c, GT * g:GT * g + GT], bank[:, :], ACT.Copy).then_inc(x2t_hi, 1)

            def ffn(g):
                def high(n):
                    wait_for(act, up_used, n + 1)
                    wait_for(act, down_full, n - 1)
                    dst = pt_hi if n % 2 == 0 else ot_hi
                    copy(flat3(dst[:, :, :]), flat3(gated[n % 2][:, :, :]), ACT.Copy, scale=0.5).then_inc(inter_hi, 1)

                for ib in range(IB):
                    n = IB * g + ib
                    wait_for(act, gate_full, n + 1)
                    wait_for(act, gate_used, n - 1)
                    copy(flat3(th[n % 2]), ring[2 * (n % 2)][:, :], ACT.Tanh, scale=0.5).then_inc(tanh_ready, 1)
                    if ib:
                        high(n - 1)
                high(IB * g + IB - 1)

            wkv(0, 0)
            wkv(0, 1)
            x2_high(0)
            wkv(1, 0)
            wkv(1, 1)
            ffn(0)
            x2_high(1)
            ffn(1)

        @block.vector
        def _(dve):
            v = nc.vector

            def flat3(t):
                return t.rearrange("p a b -> p (a b)")

            def flat(t):
                return flat3(t[:, :, :])

            def low(dst, src, high):
                return v.tensor_tensor(dst, src, high.bitcast(F32), ALU.subtract)

            def cosine(p, c, m):
                k = (BLK_Q, BLK_K)[m][c]
                wait_for(dve, blk_mid, mid_at(p, k) + 1)
                wait_for(dve, (q_ready, k_ready)[m], 4 * p + c)
                v.tensor_tensor(straight[m][:, :, :], ring[k % RING][:, :].rearrange("p (b t) -> p b t", b=GB),
                                rope_cos[m].unsqueeze(1).to_broadcast([P, GB, T]), ALU.mult).then_inc(blk_free, 1)

            def sum_weights(n, k, blk, raw, got, count):
                wait_for(dve, blk_full, blk + 1)
                wait_for(dve, got, count)
                wait_for(dve, w_ready, n)
                v.tensor_tensor(w_sum[:, :], ring[k % RING][:, :], raw, ALU.add).then_inc(blk_free, 1)

            def lora_low(e):
                wait_for(dve, lb_hi_ready, e + 1)
                low(lb[32:64, :], lb_raw[32:64, :], lb[32:64, :]).then_inc(lb_ready, 1)

            def slot(s, p, c):
                static = isinstance(s, int)
                active = not static or s < UNITS
                if c == 3 and (not static or p + 1 < PAIRS):
                    sum_weights(4 * p + 4, BLK_LQK0, block_at(p, BLK_LQK0), w_raw[:, 0, :], got_w, 16 * (p + 2))
                if c == 0 and active:
                    sum_weights(4 * p + 1, BLK_LQK1, block_at(p, BLK_LQK1), w_raw[:, 1, :], got_w, 16 * (p + 1))
                if active:
                    cosine(p, c, 0)
                    cosine(p, c, 1)
                if not static or 0 <= s - 2 < UNITS:
                    wait_for(dve, pt_hi_ready, s - 1)
                    low(flat(pt_lo), to_bank[:, :], flat(pt_hi)).then_inc(pt_ready, 1)
                if active:
                    wait_for(dve, turned_ready, 2 * s + 1)
                    wait_for(dve, blk_free, block_at(p, BLK_Q[c]) + 1)
                    wait_for(dve, scores_ready, s - 1)
                    v.tensor_tensor(q_t[c % 2][:, :, :], straight[0][:, :, :], turned[0][:, :, :], ALU.add
                                    ).then_inc(q_ready, 1)
                if (not static or 0 <= s - 3 < UNITS) and (c + 1) % 2 == 1:
                    g = (c + 1) % 4 // 2
                    wait_for(dve, wo_full, s - 2)
                    wait_for(dve, acc_set, 1)
                    for j in range(2):
                        part = acc[:, GB * g + 2 * j:GB * g + 2 * j + 2, :]
                        wait_for(dve, acc_added, 4 * (p - (c < 3)))
                        v.tensor_tensor(flat3(part), wo_bank[j][:, :], flat3(part), ALU.add).then_inc(acc_added, 1)
                if not static or 0 <= s - 1 < UNITS:
                    u = s - 1
                    wait_for(dve, scores_ready, u + 1)
                    wait_for(dve, exp_ready, u)
                    v.tensor_reduce(neg_max[:, :], s_bank[:, :].rearrange("p (b t) -> p b t", b=GB), AX.X, ALU.max,
                                    negate=True).then_inc(max_ready, 1)
                if active:
                    if c == 0:
                        sum_weights(4 * p + 2, BLK_LV, block_at(p, BLK_LV), w_raw[:, 2, :], got_w, 16 * (p + 1))
                    if c in (1, 3):
                        g = c // 2
                        for j in range(2):
                            k = (BLK_V0, BLK_V1)[g] + j
                            wait_for(dve, blk_mid, mid_at(p, k) + 1)
                            low(flat3(v_lo[g][:, 2 * j:2 * j + 2, :]), ring[k % RING][:, :],
                                flat3(v_hi[g][:, 2 * j:2 * j + 2, :])).then_inc(blk_free, 1)
                if not static or 0 <= s - 1 < UNITS:
                    u = s - 1
                    wait_for(dve, exp_ready, u + 1)
                    wait_for(dve, prob_ready, u)
                    v.reciprocal(row_inv[:, :], row_sum[:, :]).then_inc(inv_ready, 1)
                if active:
                    if c == 1:
                        lora_low(p + 1)
                    if c == 2:
                        sum_weights(4 * p + 3, BLK_LWO, block_at(p, BLK_LWO), wo_raw[:, :], got_wo, 16 * (p + 1))
                        for w in range(3):
                            k = BLK_GEN + w
                            wait_for(dve, blk_mid, mid_at(p, k) + 1)
                            wait_for(dve, got_second, 16 * (p + 1))
                            dve.sem_inc(piece_due, 1)
                            v.copy_predicated(made[:, :], second[:, :], ring[k % RING][:, CHUNK:2 * CHUNK]
                                              ).then_inc(blk_free, 1)
                            wait_for(dve, fw_hi_ready, 3 * p + w + 1)
                            dst, src = weight_views(w, p, 1)
                            high, _ = weight_views(w, p, 0)
                            low(dst, src, high).then_inc(fw_ready, 1)
                if not static or 0 <= s - 2 < UNITS:
                    wait_for(dve, ot_hi_ready, s - 1)
                    low(flat(ot_lo), to_bank[:, :], flat(ot_hi)).then_inc(ot_ready, 1)

            dve.wait_ge(la_hi_ready, 1)
            v.scalar_tensor_tensor(la[64:96, :, :], la_raw[64:96, :, :], LORA_SCALE, la[64:96, :, :].bitcast(F32),
                                   ALU.mult, ALU.subtract).then_inc(la_ready, 1)
            lora_low(0)
            for b in range(B):
                wait_for(dve, rms_ready, 1)
                v.tensor_scalar(acc[:, b, :], x_raw[:, b, :], rms_inv[:, b:b + 1], None, ALU.mult).then_inc(x_normed, 1)
            dve.wait_ge(got_cst, 16)
            v.tensor_copy(ident_b[:, :], ident).then_inc(small_cast, 1)
            v.tensor_copy(mask_b[:, :], cst[:, 5, :]).then_inc(small_cast, 1)
            for n in range(4):
                dc, g = n // 2, n % 2
                cols = slice(GT * g, GT * g + GT)
                dve.wait_ge(blk_mid, n + 1)
                v.scalar_tensor_tensor(xt_lo[:, dc, cols], ring[n][:, :], sm[:, 0, dc:dc + 1],
                                       xt_hi[:, dc, cols].bitcast(F32), ALU.mult, ALU.subtract).then_inc(blk_free, 1)
            sum_weights(0, 2, 4, w_raw[:, 0, :], got_w, 16)
            dve.wait_ge(blk_full, 4)
            v.tensor_scalar(acc[:, :, :], x_raw[:, :, :], 2.0, None, ALU.mult).then_inc(acc_set, 1)

            for s in range(3):
                slot(s, 0, s)
            with dve.Fori(0, PAIRS - 1) as i:
                for j in range(4):
                    slot(4 * i + 3 + j, i + (j > 0), (3 + j) % 4)
            for s in range(UNITS - 1, UNITS + 3):
                slot(s, s // 4, s % 4)

            def layer_norm(n, g, src):
                for j in range(GB):
                    b = GB * g + j
                    wait_for(dve, ln_ready, GB * n)
                    v.bn_stats(stats[:, j, :], src[:, b, :]).then_inc(stats_step, 1)
                for j in range(GB):
                    wait_for(dve, stats_step, GB * n + j + 1)
                    v.bn_aggr(mean_var[:, j, :], stats[:, j, :]).then_inc(stats_ready, 1)
                wait_for(dve, ln_inv_ready, n + 1)
                wait_for(dve, stats_ready, GB * n + GB)
                for j in range(GB):
                    b = GB * g + j
                    v.tensor_scalar(x_raw[:, b, :], src[:, b, :], mean_var[:, j, 0:1], ln_inv[:, j:j + 1],
                                    ALU.subtract, ALU.mult).then_inc(ln_ready, 1)

            def wkv(g, c):
                n = DC * g + c
                done = WKV_DVE * n
                decay_c, first_c = decay[:, c:c + 1], sm[:, 2, c:c + 1]
                k_now = k_ext[:, :, 1:]
                before, now = top[:, :, 0:T], top[:, :, 1:]
                wait_for(dve, k_copied, n + 1)
                wait_for(dve, wkv_dve, done)
                wait_for(dve, wkv_pool, WKV_POOL * n)
                v.tensor_tensor_scan(flat(top), flat(decay_tab[c]), flat(k_ext), NO_STATE, ALU.add, ALU.max
                                     ).then_inc(wkv_dve, 1)
                dve.wait_ge(wkv_dve, done + 1)
                v.scalar_tensor_tensor(peak[:, :, :], k_now, first_c, before, ALU.add, ALU.max).then_inc(wkv_dve, 1)
                dve.wait_ge(wkv_dve, done + 2)
                v.scalar_tensor_tensor(e_new[:, :, :], k_now, first_c, peak[:, :, :], ALU.add, ALU.subtract
                                       ).then_inc(wkv_dve, 1)
                v.scalar_tensor_tensor(keep[:, :, 1:], before, decay_c, now, ALU.add, ALU.subtract
                                       ).then_inc(wkv_dve, 1)
                dve.wait_ge(wkv_act, WKV_ACT * n + 4)
                v.tensor_tensor_scan(flat(bb), flat(keep), flat(add_k), 0.0, ALU.mult, ALU.add).then_inc(wkv_dve, 1)
                dve.wait_ge(wkv_pool, WKV_POOL * n + 3)
                v.tensor_tensor_scan(flat(aa), flat(keep), flat(add_v), 0.0, ALU.mult, ALU.add).then_inc(wkv_dve, 1)
                dve.wait_ge(wkv_pool, WKV_POOL * n + 4)
                v.tensor_tensor(den[:, :, :], den[:, :, :], e_new[:, :, :], ALU.add).then_inc(wkv_dve, 1)
                dve.wait_ge(wkv_dve, done + 7)
                v.reciprocal(den_inv[:, :, :], den[:, :, :]).then_inc(wkv_dve, 1)
                dve.wait_ge(wkv_pool, WKV_POOL * n + 6)
                v.tensor_tensor(num[:, :, :], num[:, :, :], peak[:, :, :], ALU.add).then_inc(wkv_dve, 1)
                dve.wait_ge(wkv_dve, done + 9)
                wait_for(dve, y_full, 2 * g)
                v.tensor_tensor(y_t[c][:, :, :], num[:, :, :], den_inv[:, :, :], ALU.mult).then_inc(wkv_dve, 1)

            def add_y(g):
                for j, bank in enumerate((s_bank, to_bank)):
                    part = flat3(x_raw[:, GB * g + 2 * j:GB * g + 2 * j + 2, :])
                    wait_for(dve, y_full, 2 * g + j + 1)
                    v.tensor_tensor(part, bank[:, :], part, ALU.add).then_inc(y_added, 1)
                dve.wait_ge(y_added, 2 * g + 2)

            def x2_low(g):
                for c, bank in enumerate((s_bank, to_bank)):
                    cols = slice(GT * g, GT * g + GT)
                    wait_for(dve, x2t_hi, DC * g + c + 1)
                    low(xt_lo[:, c, cols], bank[:, :], xt_hi[:, c, cols]).then_inc(x2t_ready, 1)

            def ffn(g):
                def low_half(n):
                    wait_for(dve, inter_hi, n + 1)
                    hi, lo = (pt_hi, pt_lo) if n % 2 == 0 else (ot_hi, ot_lo)
                    v.scalar_tensor_tensor(flat(lo), flat(gated[n % 2]), 0.5, flat(hi).bitcast(F32),
                                           ALU.mult, ALU.subtract).then_inc(inter_ready, 1)

                for ib in range(IB):
                    n = IB * g + ib
                    wait_for(dve, tanh_ready, n + 1)
                    wait_for(dve, inter_ready, n - 1)
                    v.scalar_tensor_tensor(flat(gated[n % 2]), flat3(th[n % 2]).bitcast(F32), 1.0, ring[2 * (n % 2)][:, :],
                                           ALU.add, ALU.mult).then_inc(gate_used, 1)
                    if ib:
                        low_half(n - 1)
                    wait_for(dve, gate_used, n + 1)
                    wait_for(dve, up_full, n + 1)
                    v.tensor_tensor(flat(gated[n % 2]), ring[2 * (n % 2) + 1][:, :], flat(gated[n % 2]), ALU.mult
                                    ).then_inc(up_used, 1)
                low_half(IB * g + IB - 1)

            def add_down(g):
                wait_for(dve, down_full, IB * (g + 1))
                for j in range(2):
                    part = flat3(x_raw[:, GB * g + 2 * j:GB * g + 2 * j + 2, :])
                    v.tensor_tensor(part, wo_bank[j][:, :], part, ALU.add).then_inc(down_added, 1)
                dve.wait_ge(down_added, 2 * g + 2)

            dve.wait_ge(decay_exp, 1)
            v.tensor_scalar(decay[:, :], decay[:, :], -1.0, None, ALU.mult).then_inc(tables_step, 1)
            for c in range(DC):
                v.memset(decay_tab[c][:, :, :], 0.0).then_inc(tables_step, 1)
            dve.wait_ge(tables_step, 1 + DC)
            for c in range(DC):
                v.tensor_scalar(decay_tab[c][:, :, :], decay_tab[c][:, :, :], decay[:, c:c + 1], None, ALU.add
                                ).then_inc(tables_step, 1)
            dve.wait_ge(tables_step, 1 + 2 * DC)
            for c in range(DC):
                v.memset(decay_tab[c][:, :, 0:1], FORGET).then_inc(tables_step, 1)
            v.memset(k_ext[:, :, 0:1], NO_STATE).then_inc(exts_set, 1)
            for t in (keep, add_k, add_v):
                v.memset(t[:, :, 0:1], 0.0).then_inc(exts_set, 1)
            dve.wait_ge(tables_step, 1 + 3 * DC)
            dve.wait_ge(exts_set, 4)
            for g in range(GROUPS):
                dve.wait_ge(acc_added, 4 * (PAIRS - 1) + 2 * g + 2)
                layer_norm(g, g, acc)
            dve.wait_ge(got_v, 16)
            wkv(0, 0)
            wkv(0, 1)
            add_y(0)
            layer_norm(2, 0, x_raw)
            x2_low(0)
            wkv(1, 0)
            wkv(1, 1)
            ffn(0)
            add_y(1)
            layer_norm(3, 1, x_raw)
            x2_low(1)
            add_down(0)
            layer_norm(4, 0, x_raw)
            ffn(1)
            add_down(1)
            layer_norm(5, 1, x_raw)

        @block.gpsimd
        def _(pool):
            gp = nc.gpsimd

            def flat3(t):
                return t.rearrange("p a b -> p (a b)")

            def sine(p, c, m):
                s = 4 * p + c
                wait_for(pool, blk_mid, mid_at(p, (BLK_Q, BLK_K)[m][c]) + 1)
                gp.tensor_tensor(turned[m][:, :, :], turned[m][:, :, :],
                                 rope_sin[m].unsqueeze(1).to_broadcast([P, GB, T]), ALU.mult).then_inc(turned_ready, 1)

            def low_weights(n, dst, high):
                wait_for(pool, w_hi_ready, n + 1)
                gp.tensor_tensor(dst, w_sum[:, :], high.bitcast(F32), ALU.subtract).then_inc(w_ready, 1)

            def slot(s, p, c):
                static = isinstance(s, int)
                active = not static or s < UNITS
                if c == 3 and (not static or p + 1 < PAIRS):
                    low_weights(4 * p + 4, flat3(wqk[0][1][:, :, :]), flat3(wqk[0][0][:, :, :]))
                if c == 0 and active:
                    low_weights(4 * p + 1, flat3(wqk[1][1][:, :, :]), flat3(wqk[1][0][:, :, :]))
                if active:
                    sine(p, c, 0)
                    sine(p, c, 1)
                    wait_for(pool, turned_ready, 2 * s + 2)
                    wait_for(pool, blk_free, block_at(p, BLK_K[c]) + 1)
                    wait_for(pool, scores_ready, s - 1)
                    gp.tensor_tensor(k_t[c % 2][:, :, :], straight[1][:, :, :], turned[1][:, :, :], ALU.add
                                     ).then_inc(k_ready, 1)
                if not static or 0 <= s - 1 < UNITS:
                    u = s - 1
                    par = (c + 1) % 2
                    wait_for(pool, inv_ready, u + 1)
                    gp.tensor_tensor(prob[par][:, :, :], prob[par][:, :, :],
                                     row_inv[:, :].unsqueeze(2).to_broadcast([P, GB, T]), ALU.mult
                                     ).then_inc(prob_ready, 1)
                if active and c == 0:
                    low_weights(4 * p + 2, flat3(wv[1][:, :, :]), flat3(wv[0][:, :, :]))
                    wait_for(pool, got_knots, 16 * (p + 1))
                    wait_for(pool, got_tab, 48 * (p + 1))
                    wait_for(pool, coef_ready, p)
                    gp.tensor_tensor(coef[:, :, :], spline_tab[:, :, :],
                                     knot_rows[:, :].unsqueeze(1).to_broadcast([96, 2, CHUNK]), ALU.mult
                                     ).then_inc(coef_made, 1)
                    wait_for(pool, coef_hi_ready, p + 1)
                    gp.tensor_tensor(flat3(coef_lo[:, :, :]), flat3(coef[:, :, :]),
                                     flat3(coef_hi[:, :, :]).bitcast(F32), ALU.subtract).then_inc(coef_ready, 1)
                if active and c == 2:
                    low_weights(4 * p + 3, flat3(wo[1][:, :, :]), flat3(wo[0][:, :, :]))

            gp.memset(half[:, :], -0.5).then_inc(half_set, 1)
            pool.wait_ge(squared, B)
            gp.tensor_scalar(mean_sq[:, :], sum_sq[:, :], 1.0 / D, RMS_EPS, ALU.mult, ALU.add).then_inc(rms_step, 1)
            pool.wait_ge(rms_step, 1)
            pool.wait_ge(half_set, 1)
            gp.tensor_tensor(rms_inv[:, :], mean_sq[:, :], half[:, :], ALU.pow).then_inc(rms_ready, 1)
            low_weights(0, flat3(wqk[0][1][:, :, :]), flat3(wqk[0][0][:, :, :]))
            pool.wait_ge(got_cst, 16)

            for s in range(3):
                slot(s, 0, s)
            with pool.Fori(0, PAIRS - 1) as i:
                for j in range(4):
                    slot(4 * i + 3 + j, i + (j > 0), (3 + j) % 4)
            for s in range(UNITS - 1, UNITS + 3):
                slot(s, s // 4, s % 4)

            def layer_norm(n):
                wait_for(pool, stats_ready, GB * (n + 1))
                gp.tensor_scalar(var_eps[:, :], mean_var[:, :, 1], LN_EPS, None, ALU.add).then_inc(ln_step, 1)
                wait_for(pool, ln_step, n + 1)
                wait_for(pool, ln_ready, GB * n)
                gp.tensor_tensor(ln_inv[:, :], var_eps[:, :], half[:, 0:GB], ALU.pow).then_inc(ln_inv_ready, 1)

            def wkv(g, c):
                n = DC * g + c
                v_now = v_t[:, c, GT * g:GT * g + GT].rearrange("p (b t) -> p b t", b=GB)
                before, now = top[:, :, 0:T], top[:, :, 1:]
                pool.wait_ge(wkv_dve, WKV_DVE * n + 2)
                gp.tensor_tensor(e_old[:, :, :], before, peak[:, :, :], ALU.subtract).then_inc(wkv_pool, 1)
                gp.tensor_tensor(add_k[:, :, 1:], k_ext[:, :, 1:], now, ALU.subtract).then_inc(wkv_pool, 1)
                pool.wait_ge(wkv_act, WKV_ACT * n + 3)
                gp.tensor_tensor(add_v[:, :, 1:], add_k[:, :, 1:], v_now, ALU.mult).then_inc(wkv_pool, 1)
                pool.wait_ge(wkv_dve, WKV_DVE * n + 5)
                gp.tensor_tensor(den[:, :, :], e_old[:, :, :], bb[:, :, 0:T], ALU.mult).then_inc(wkv_pool, 1)
                gp.tensor_tensor(peak[:, :, :], e_new[:, :, :], v_now, ALU.mult).then_inc(wkv_pool, 1)
                pool.wait_ge(wkv_dve, WKV_DVE * n + 6)
                gp.tensor_tensor(num[:, :, :], e_old[:, :, :], aa[:, :, 0:T], ALU.mult).then_inc(wkv_pool, 1)

            pool.wait_ge(got_v, 16)
            layer_norm(0)
            layer_norm(1)
            wkv(0, 0)
            wkv(0, 1)
            layer_norm(2)
            wkv(1, 0)
            wkv(1, 1)
            layer_norm(3)
            layer_norm(4)
            layer_norm(5)


def spline_tables():
    import numpy as np

    knots_n = max(16, int(INTER * D / 128.9))
    t = np.linspace(0.0, knots_n - 1.0, D * INTER, dtype=np.float64)
    interval = np.clip(np.floor(t).astype(np.int64), 0, knots_n - 2).reshape(COLUMNS, P)
    j = np.arange(COLUMNS)
    base = 127 * (j // P) + j % P - 2
    first = interval[:, 0]
    second = (interval != first[:, None]).T.astype(np.int32)
    catmull = 0.5 * np.array([[0, -1, 2, -1], [2, 0, -5, 3], [0, 1, 4, -3], [0, 0, -1, 1]], np.float64)
    table = np.zeros((32, 2, COLUMNS))
    for side in (0, 1):
        a = t.reshape(COLUMNS, P)[:, 64] - first - side
        s = 64 * t[1]
        powers = np.zeros((4, 4, COLUMNS))
        powers[0, 0] = 1
        powers[1, 0], powers[1, 1] = a, s
        powers[2, 0], powers[2, 1], powers[2, 2] = a ** 2, 2 * a * s, s * s
        powers[3, 0], powers[3, 1], powers[3, 2], powers[3, 3] = a ** 3, 3 * a ** 2 * s, 3 * a * s * s, s ** 3
        for k in range(4):
            kk = np.clip(first + side - 1 + k, 0, knots_n - 1) - base
            co = np.einsum("m,mrj->rj", catmull[k], powers)
            ok = (kk >= 0) & (kk < 6)
            for r in range(5):
                np.add.at(table[:, side], (np.where(ok, kk * 5 + r, 31), j), np.where(ok, co[min(r, 3)], 0))
    q = (np.arange(P) - 64) / 64.0
    mantissa, exponent = np.frexp(q ** 3)
    high = np.ldexp(np.rint(mantissa * 4096) / 4096, exponent)
    phi = np.zeros((32, P))
    for kk in range(6):
        phi[5 * kk:5 * kk + 5] = [q ** 0, q, q * q, high, q ** 3 - high]
    return table.astype(np.float32), second, phi.astype(np.float32)


def constant_tables(phi):
    import numpy as np

    half = DH // 2
    theta = (1.0 / 10000.0 ** (np.arange(half) / half)).astype(np.float32)
    angle = (np.arange(T, dtype=np.float32)[:, None] * theta[None, :]).astype(np.float64).T
    cos = np.concatenate([np.cos(angle), np.cos(angle)])
    sin = np.concatenate([-np.sin(angle), np.sin(angle)])
    consts = np.zeros((P, 9, P), np.float32)
    scale = DH ** -0.5
    consts[:, 0], consts[:, 1], consts[:, 2], consts[:, 3] = cos * scale, sin * scale, cos, sin
    consts[:, 4] = np.eye(P)
    i, j = np.arange(T)[:, None], np.arange(T)[None, :]
    consts[:, 5] = np.where((j <= i) & (j >= i - WINDOW + 1), 0.0, MASKED)
    for w in range(3):
        consts[32 * w:32 * w + 32, 6 + w] = phi
    return consts


def lay_out(inputs):
    import numpy as np

    a = {k.replace("L0_", "").replace("attn_", ""): np.asarray(v) for k, v in inputs.items()}
    f = np.float32
    table, second, phi = spline_tables()
    arrays = {"x": a["x"], "ctx_t": np.ascontiguousarray(a["ctx_2048"].reshape(B * T, D).T)}
    arrays["small"] = np.ascontiguousarray(np.stack(
        [a["norm_w"], a["xtime_decay"], a["xtime_first"]]).reshape(3, DC, P).transpose(2, 0, 1))
    arrays["consts"] = constant_tables(phi)

    lora_a = np.zeros((32, 4, D), f)
    lora_a[0:16, 0], lora_a[16:32, 1], lora_a[0:16, 2] = a["qA"], a["kA"], a["vA"]
    lora_a[0:16, 3] = a["oB"].T
    arrays["lora_a"] = lora_a.reshape(32, 4 * D)
    lora_b = np.zeros((PAIRS + 1, 32, 3, 2 * DH), f)
    by_pair = lambda m: m.reshape(RANK, PAIRS, 2 * DH).transpose(1, 0, 2)
    lora_b[:PAIRS, 0:16, 0], lora_b[:PAIRS, 16:32, 0] = by_pair(a["qB"].T), by_pair(a["kB"].T)
    lora_b[:PAIRS, 0:16, 1] = by_pair(a["vB"].T)
    lora_b[1:, 0:16, 2] = by_pair(a["oA"])
    arrays["lora_b"] = lora_b.reshape(PAIRS + 1, 32, 3 * 2 * DH)

    w_qkv = np.zeros((PAIRS, P, 3, 512), f)
    q = a["wq"].reshape(PAIRS, 2, DH, DC, P).transpose(0, 4, 1, 3, 2)
    k = a["wk"].reshape(PAIRS, 2, DH, DC, P).transpose(0, 4, 1, 3, 2)
    w_qkv[:, :, 0:2, 0:256] = q.reshape(PAIRS, P, 2, 256)
    w_qkv[:, :, 0:2, 256:512] = k.reshape(PAIRS, P, 2, 256)
    v = a["wv"].reshape(PAIRS, 2 * DH, DC, P).transpose(0, 3, 2, 1)
    w_qkv[:, :, 2] = v.reshape(PAIRS, P, 512)
    arrays["w_qkv"] = w_qkv.reshape(PAIRS, P, 3 * 512)
    arrays["w_o"] = np.ascontiguousarray(
        a["wo"].reshape(D, PAIRS, 2, DH).transpose(1, 3, 2, 0)).reshape(PAIRS, DH, 512)

    knots = np.zeros((3, 32, 16, P), f)
    for w, name in enumerate(("ffn_gate_cp", "ffn_up_cp", "ffn_down_cp")):
        padded = np.pad(a[name], (2, 8))
        for kk in range(6):
            for jb in range(16):
                knots[w, 5 * kk:5 * kk + 5, jb] = padded[127 * jb + kk:127 * jb + kk + P]
    arrays["knots"] = np.ascontiguousarray(
        knots.reshape(96, PAIRS, CHUNK).transpose(1, 0, 2))
    arrays["spline"] = np.ascontiguousarray(
        table.reshape(32, 2, PAIRS, CHUNK).transpose(2, 0, 1, 3)).reshape(PAIRS, 32, 2 * CHUNK)
    arrays["piece"] = np.ascontiguousarray(second.reshape(P, PAIRS, CHUNK).transpose(1, 0, 2))
    return arrays


def kernel(**inputs):
    import numpy as _np
    import concourse.bacc as _bacc
    from concourse import mybir as _mybir
    from concourse.bass_utils import run_bass_kernel_spmd as _run

    nc = _bacc.Bacc("TRN2", target_bir_lowering=False, num_devices=1)
    arrays, args = {}, []
    for name, a in lay_out(inputs).items():
        a = _np.ascontiguousarray(a)
        arrays[f"in_{name}_dram"] = a
        args.append(nc.dram_tensor(f"in_{name}_dram", a.shape, _mybir.dt.from_np(a.dtype), kind="ExternalInput").ap())
    args.append(nc.dram_tensor("out_0_dram", (B, T, D), F32, kind="ExternalOutput").ap())
    decoder_layer(nc, *args)
    r = _run(nc, [arrays], core_ids=[0])
    return r.results[0]["out_0_dram"]
```

```python
from contextlib import ExitStack

import concourse.bass as bass
from concourse import mybir

F32 = mybir.dt.float32
F32R = mybir.dt.float32r
BF16 = mybir.dt.bfloat16
I32 = mybir.dt.int32
ALU = mybir.AluOpType
ACT = mybir.ActivationFunctionType
AX = mybir.AxisListType

P = 128
B, T, D = 8, 128, 256
H, DH = 16, 128
RANK = 16
WINDOW = 64
INTER = 1024
PAIRS = H // 2
GROUPS = 2
GB = B // GROUPS
GT = GB * T
DC = D // P
UNITS = PAIRS * GROUPS * 2
IB = INTER // P
CHUNK = 256
COLUMNS = D * INTER // P
RMS_EPS = 1e-6
LN_EPS = 1e-5
LORA_SCALE = 1.0 / RANK
NO_STATE = -1e38
FORGET = -2e38
MASKED = -3e38

RING = 4
BLK_Q0, BLK_K0, BLK_LV = 0, 1, 2
BLK_Q1, BLK_K1, BLK_V0 = 3, 4, 5
BLK_Q2, BLK_K2, BLK_LWO, BLK_GEN = 7, 8, 9, 10
BLK_LQK0, BLK_Q3, BLK_K3, BLK_V1, BLK_LQK1 = 13, 14, 15, 16, 18
PAIR_BLOCKS = 19
FIRST_BLOCKS = 6
BLK_Q = [BLK_Q0, BLK_Q1, BLK_Q2, BLK_Q3]
BLK_K = [BLK_K0, BLK_K1, BLK_K2, BLK_K3]
MID = {BLK_Q0: 0, BLK_K0: 1, BLK_Q1: 2, BLK_K1: 3, BLK_Q2: 4, BLK_K2: 5, BLK_GEN: 6, BLK_GEN + 1: 7,
       BLK_GEN + 2: 8, BLK_Q3: 9, BLK_K3: 10}
PAIR_MIDS = 11
WKV_DVE, WKV_POOL, WKV_ACT = 10, 6, 4
FIRST_MIDS = 4


def block_at(p, k):
    if isinstance(p, int) and p == PAIRS - 1 and k > BLK_LQK0:
        k -= 1
    return FIRST_BLOCKS + PAIR_BLOCKS * p + k


def mid_at(p, k):
    return FIRST_MIDS + PAIR_MIDS * p + MID[k]


def bank_user_before(p, k):
    if k >= RING:
        return block_at(p, k - RING)
    if isinstance(p, int) and p == 0:
        return [0, 4, 5, 3][k]
    return block_at(p - 1, {0: BLK_V1, 1: BLK_V1 + 1, 2: BLK_LQK1, 3: BLK_K3}[k])


def wait_for(engine, sem, count):
    if isinstance(count, int) and count <= 0:
        return
    engine.wait_ge(sem, count)


def decoder_layer(nc, x, ctx_t, small, consts, lora_a, lora_b, w_qkv, w_o, knots, spline, piece, out):
    with ExitStack() as stack:
        def sb(name, shape, dt=F32):
            return stack.enter_context(nc.sbuf_tensor(name, shape, dt))

        def ps(name):
            return stack.enter_context(nc.psum_tensor(name, [P, 512], F32))

        def sem(name):
            return stack.enter_context(nc.semaphore(name))

        x_raw = sb("x_raw", [P, B, D])
        acc = sb("acc", [P, B, D])
        xt_hi = sb("xt_hi", [P, DC, B * T], F32R)
        xt_lo = sb("xt_lo", [P, DC, B * T], F32R)
        v_t = sb("v_t", [P, DC, B * T])
        cst = sb("cst", [P, 9, P])
        sm = sb("sm", [P, 3, DC])
        ident_b = sb("ident_b", [P, P], BF16)
        mask_b = sb("mask_b", [P, P], BF16)
        phi = sb("phi", [P, 3, P], F32R)
        rope_cos = [cst[:, 0, :], cst[:, 2, :]]
        rope_sin = [cst[:, 1, :], cst[:, 3, :]]
        ident = cst[:, 4, :]

        la = sb("la", [96, 4, D], F32R)
        lb_raw = sb("lb_raw", [96, 3 * D])
        lb = sb("lb", [96, 3 * D], F32R)
        w_raw = sb("w_raw", [P, 3, 512])
        wo_raw = sb("wo_raw", [P, 512])
        w_sum = sb("w_sum", [P, 2, 512])
        wqk = [[sb(f"wqk{hh}_{part}", [P, 4, P], F32R) for part in ("hi", "lo")] for hh in range(2)]
        wv = [sb(f"wv_{part}", [P, DC, 2 * DH], F32R) for part in ("hi", "lo")]
        wo = [sb(f"wo_{part}", [P, 2, D], F32R) for part in ("hi", "lo")]

        straight = [sb(f"straight{n}", [P, GB, T]) for n in range(2)]
        turned = [sb(f"turned{n}", [P, GB, T]) for n in range(2)]
        q_t = [sb(f"q_t{n}", [P, GB, T]) for n in range(2)]
        k_t = [sb(f"k_t{n}", [P, GB, T]) for n in range(2)]
        v_now = [sb(f"v_now{g}", [P, GB, 2 * DH]) for g in range(GROUPS)]
        prob = [sb(f"prob{n}", [P, GB, T]) for n in range(2)]
        pt = sb("pt", [P, GB, T])
        ot_hi = sb("ot_hi", [P, GB, T], F32R)
        ot_lo = sb("ot_lo", [P, GB, T], F32R)
        inner_parts = [(sb("inner_hi", [P, GB, T], F32R), sb("inner_lo", [P, GB, T], F32R)), (ot_hi, ot_lo)]
        neg_max = sb("neg_max", [P, GB])
        row_sum = sb("row_sum", [P, GB])
        row_inv = sb("row_inv", [P, GB])

        knot_rows = sb("knot_rows", [96, CHUNK])
        spline_tab = sb("spline_tab", [96, 2, CHUNK])
        second = sb("second", [P, CHUNK], I32)
        coef = sb("coef", [96, 2, CHUNK])
        coef_hi = sb("coef_hi", [96, 2, CHUNK], F32R)
        coef_lo = sb("coef_lo", [96, 2, CHUNK], F32R)
        made = sb("made", [P, 3, CHUNK])
        fw = [[sb(f"fw{w}_{part}", [P, COLUMNS], F32R) for part in ("hi", "lo")] for w in range(3)]

        squares = sb("squares", [P, D])
        sum_sq = sb("sum_sq", [P, B])
        mean_sq = sb("mean_sq", [P, B])
        rms_inv = sb("rms_inv", [P, B])
        half = sb("half", [P, B])
        stats = sb("stats", [P, GB, 6])
        mean_var = sb("mean_var", [P, GB, 2])
        var_eps = sb("var_eps", [P, GB])
        ln_inv = sb("ln_inv", [P, GB])

        decay = sb("decay", [P, DC])
        decay_tab = [sb(f"decay_tab{c}", [P, GB, T + 1]) for c in range(DC)]
        scan_bufs = sb("scan_bufs", [P, 7, GB * (T + 1)])
        k_ext, top, keep, add_k, add_v, aa, bb = [
            scan_bufs[:, n, :].rearrange("p (b t) -> p b t", b=GB) for n in range(7)]
        la_raw = scan_bufs[0:96, 0:2, :].rearrange("p a n -> p (a n)")[:, 0:4 * D].rearrange("p (k n) -> p k n", k=4)
        peak, e_old, e_new = q_t[0], q_t[1], k_t[0]
        y_t = [k_t[1], straight[0]]
        den_inv = straight[1]
        num = turned[0]
        den = turned[1]
        gated = [prob[0], prob[1]]
        th = [v_now[0][:, 0:2, :], v_now[0][:, 2:4, :]]

        ring = [ps(f"ring{n}") for n in range(RING)]
        s_bank = ps("s_bank")
        to_bank = ps("to_bank")
        wo_bank = [ps(f"wo_bank{n}") for n in range(2)]

        got_x, got_small, got_cst, got_la = sem("got_x"), sem("got_small"), sem("got_cst"), sem("got_la")
        got_lb, got_w, got_wo = sem("got_lb"), sem("got_w"), sem("got_wo")
        got_knots, got_tab, got_second, got_v = sem("got_knots"), sem("got_tab"), sem("got_second"), sem("got_v")
        stored = sem("stored")
        squared, rms_step, rms_ready, x_normed = sem("squared"), sem("rms_step"), sem("rms_ready"), sem("x_normed")
        half_set = sem("half_set")
        small_cast, phi_cast = sem("small_cast"), sem("phi_cast")
        la_hi_ready, la_ready = sem("la_hi_ready"), sem("la_ready")
        blk_full, blk_mid, blk_free = sem("blk_full"), sem("blk_mid"), sem("blk_free")
        lb_hi_ready, lb_ready = sem("lb_hi_ready"), sem("lb_ready")
        w_hi_ready, w_ready = sem("w_hi_ready"), sem("w_ready")
        coef_made, coef_hi_ready, coef_ready = sem("coef_made"), sem("coef_hi_ready"), sem("coef_ready")
        piece_due = sem("piece_due")
        fw_hi_ready, fw_ready = sem("fw_hi_ready"), sem("fw_ready")
        turned_ready, q_ready, k_ready = sem("turned_ready"), sem("q_ready"), sem("k_ready")
        scores_ready, max_ready, exp_ready = sem("scores_ready"), sem("max_ready"), sem("exp_ready")
        inv_ready, prob_ready = sem("inv_ready"), sem("prob_ready")
        pt_full, pt_ready = sem("pt_full"), sem("pt_ready")
        ot_full, ot_hi_ready, ot_ready = sem("ot_full"), sem("ot_hi_ready"), sem("ot_ready")
        wo_full, acc_added = sem("wo_full"), sem("acc_added")
        stats_step, stats_ready, ln_step, ln_inv_ready, ln_ready = (
            sem("stats_step"), sem("stats_ready"), sem("ln_step"), sem("ln_inv_ready"), sem("ln_ready"))
        tables_step, tables_ready = sem("tables_step"), sem("tables_ready")
        exts_set = sem("exts_set")
        decay_exp = sem("decay_exp")
        x1t_full, k_copied = sem("x1t_full"), sem("k_copied")
        wkv_dve, wkv_pool, wkv_act = sem("wkv_dve"), sem("wkv_pool"), sem("wkv_act")
        y_full, y_added = sem("y_full"), sem("y_added")
        x2t_full, x2t_hi, x2t_ready = sem("x2t_full"), sem("x2t_hi"), sem("x2t_ready")
        gate_full, up_full, tanh_ready = sem("gate_full"), sem("up_full"), sem("tanh_ready")
        gate_used, up_used = sem("gate_used"), sem("up_used")
        inter_hi, inter_ready, down_full, down_added = (
            sem("inter_hi"), sem("inter_ready"), sem("down_full"), sem("down_added"))

        def weight_views(w, p, part):
            if w < 2:
                dst = fw[w][part][:, bass.ds(CHUNK * p, CHUNK)].rearrange("p (h i) -> p h i", h=DC)
                return dst, made[:, w, :].rearrange("p (i h) -> p h i", h=DC)
            per = CHUNK // IB
            dst = fw[w][part][:, :].rearrange("p (i h) -> p i h", i=IB)[:, :, bass.ds(per * p, per)]
            return dst, made[:, w, :].rearrange("p (h i) -> p i h", i=IB)

        block = stack.enter_context(nc.Block())

        @block.sync
        def _(sp):
            def three_times(dst, src):
                for n in range(3):
                    ins = sp.dma_start(dst[32 * n:32 * n + 32], src)
                    yield ins

            def load_lora_b(e):
                for ins in three_times(lb_raw, lora_b[bass.ds(e, 1), :, :].rearrange("a r n -> (a r) n")):
                    ins.then_inc(got_lb, 16)

            def load_w(p):
                sp.dma_start(w_raw[:, :, :].rearrange("p k n -> p (k n)"),
                             w_qkv[bass.ds(p, 1), :, :].rearrange("a p n -> (a p) n")).then_inc(got_w, 16)

            def load_wo(p):
                sp.dma_start(wo_raw[:, :], w_o[bass.ds(p, 1), :, :].rearrange("a p n -> (a p) n")
                             ).then_inc(got_wo, 16)

            def load_spline(p):
                sp.dma_start(knot_rows[:, :], knots[bass.ds(p, 1), :, :].rearrange("a p n -> (a p) n")
                             ).then_inc(got_knots, 16)
                for n in range(3):
                    sp.dma_start(spline_tab[32 * n:32 * n + 32, :, :].rearrange("p k n -> p (k n)"),
                                 spline[bass.ds(p, 1), :, :].rearrange("a p n -> (a p) n")).then_inc(got_tab, 16)

            def load_piece(p):
                sp.dma_start(second[:, :], piece[bass.ds(p, 1), :, :].rearrange("a p n -> (a p) n")
                             ).then_inc(got_second, 16)

            x_view = x.rearrange("b t d -> t b d")
            for g in range(GROUPS):
                sp.dma_start(x_raw[:, GB * g:GB * g + GB, :], x_view[:, GB * g:GB * g + GB, :]).then_inc(got_x, 16)
            load_lora_b(0)
            for n in range(3):
                sp.dma_start(la_raw[32 * n:32 * n + 32, :, :].rearrange("p k n -> p (k n)"), lora_a).then_inc(got_la, 16)
            load_w(0)
            load_spline(0)
            load_piece(0)
            load_wo(0)
            sp.dma_start(v_t[:, :, :], ctx_t.rearrange("(c p) t -> p c t", p=P)).then_inc(got_v, 16)
            sp.wait_ge(lb_ready, 1)
            load_lora_b(1)

            with sp.Fori(0, PAIRS - 1) as i:
                sp.wait_ge(blk_free, block_at(i, BLK_LV) + 1)
                load_w(i + 1)
                sp.wait_ge(coef_made, i + 1)
                load_spline(i + 1)
                sp.wait_ge(lb_ready, i + 2)
                load_lora_b(i + 2)
                sp.wait_ge(blk_free, block_at(i, BLK_LWO) + 1)
                load_wo(i + 1)
                sp.wait_ge(blk_free, block_at(i, BLK_GEN + 2) + 1)
                load_piece(i + 1)

            out_view = out.rearrange("b t d -> t b d")
            for g in range(GROUPS):
                sp.wait_ge(ln_ready, GB * (4 + g + 1))
                sp.dma_start(out_view[:, GB * g:GB * g + GB, :], x_raw[:, GB * g:GB * g + GB, :]).then_inc(stored, 16)
            sp.wait_ge(stored, 16 * GROUPS)

        @block.tensor
        def _(pe):
            def product(dst, lhs, rhs, first, last):
                (lh, ll), (rh, rl) = lhs, rhs
                pe.matmul(dst, lh, rh, start=first, stop=False, skip_group_check=True)
                pe.matmul(dst, lh, rl, start=False, stop=False, skip_group_check=True)
                return pe.matmul(dst, ll, rh, start=False, stop=last, skip_group_check=True)

            def bank_for(p, k):
                wait_for(pe, blk_free, bank_user_before(p, k) + 1)
                return ring[k % RING]

            def lora_qk(p, hh, k):
                bank = bank_for(p, k)
                for m in range(2):
                    for dc in range(DC):
                        n = 2 * m + dc
                        mm = pe.matmul(bank[:, P * n:P * n + P], la[:, m, P * dc:P * dc + P],
                                       lb[:, P * hh:P * hh + P], start=True, stop=True)
                mm.then_inc(blk_full, 1)

            def lora_v(p):
                bank = bank_for(p, BLK_LV)
                for dc in range(DC):
                    mm = pe.matmul(bank[:, 256 * dc:256 * dc + 256], la[:, 2, P * dc:P * dc + P],
                                   lb[:, 256:512], start=True, stop=True)
                mm.then_inc(blk_full, 1)

            def lora_o(p):
                wait_for(pe, lb_ready, p + 2)
                bank = bank_for(p, BLK_LWO)
                for hh in range(2):
                    mm = pe.matmul(bank[:, 256 * hh:256 * hh + 256], lb[:, 512 + P * hh:512 + P * hh + P],
                                   la[:, 3, :], start=True, stop=True)
                mm.then_inc(blk_full, 1)

            def project(p, c, m):
                g, hh = c // 2, c % 2
                wait_for(pe, w_ready, 4 * p + 1 + hh)
                bank = bank_for(p, (BLK_Q, BLK_K)[m][c])
                cols = slice(GT * g, GT * g + GT)
                for dc in range(DC):
                    w = [wqk[hh][part][:, 2 * m + dc, :] for part in range(2)]
                    mm = product(bank[:, :], w, (xt_hi[:, dc, cols], xt_lo[:, dc, cols]), dc == 0, dc == DC - 1)
                mm.then_inc(blk_full, 1)

            def values(p, g):
                wait_for(pe, w_ready, 4 * p + 3)
                for j in range(2):
                    bank = bank_for(p, (BLK_V0, BLK_V1)[g] + j)
                    for n in range(2):
                        b = GB * g + 2 * j + n
                        for dc in range(DC):
                            xs = [t[:, dc, T * b:T * b + T] for t in (xt_hi, xt_lo)]
                            mm = product(bank[:, 256 * n:256 * n + 256], xs, [wv[part][:, dc, :] for part in range(2)],
                                         dc == 0, dc == DC - 1)
                    mm.then_inc(blk_full, 1)

            def spline_weights(p, w):
                wait_for(pe, coef_ready, p + 1)
                bank = bank_for(p, BLK_GEN + w)
                pe.matmul(bank[:, :], phi[0:96, w, :], coef_hi[:, :, :].rearrange("p a n -> p (a n)"),
                          start=True, stop=False)
                pe.matmul(bank[:, :], phi[0:96, w, :], coef_lo[:, :, :].rearrange("p a n -> p (a n)"),
                          start=False, stop=True).then_inc(blk_full, 1)

            def scores(u, par):
                wait_for(pe, q_ready, u + 1)
                wait_for(pe, k_ready, u + 1)
                wait_for(pe, exp_ready, u)
                pe.matmul(s_bank[:, :], ident_b[:, :], mask_b[:, :].unsqueeze(1).to_broadcast([P, GB, T]),
                          start=True, stop=False)
                for b in range(GB):
                    mm = pe.matmul(s_bank[:, T * b:T * b + T], q_t[par][:, b, :], k_t[par][:, b, :],
                                   start=False, stop=b == GB - 1)
                mm.then_inc(scores_ready, 1)

            def turn_probs(u, par):
                wait_for(pe, prob_ready, u + 1)
                wait_for(pe, ot_ready, u)
                for b in range(GB):
                    mm = pe.transpose(to_bank[:, T * b:T * b + T], prob[par][:, b, :], ident)
                mm.then_inc(pt_full, 1)

            def probs_v(u, p, c):
                g, hh = c // 2, c % 2
                wait_for(pe, pt_ready, u + 1)
                wait_for(pe, blk_free, block_at(p, (BLK_V0, BLK_V1)[g] + 1) + 1)
                for b in range(GB):
                    mm = pe.matmul(to_bank[:, T * b:T * b + T], v_now[g][:, b, DH * hh:DH * hh + DH], pt[:, b, :],
                                   start=True, stop=True)
                mm.then_inc(ot_full, 1)

            def out_project(u, p, c):
                g, hh = c // 2, c % 2
                wait_for(pe, ot_ready, u + 1)
                if hh == 0:
                    wait_for(pe, w_ready, 4 * p + 4)
                    wait_for(pe, acc_added, 1 + 4 * p + 2 * g)
                for b in range(GB):
                    o = (ot_hi[:, b, :], ot_lo[:, b, :])
                    mm = product(wo_bank[b // 2][:, 256 * (b % 2):256 * (b % 2) + 256], o,
                                 [wo[part][:, hh, :] for part in range(2)], hh == 0 and b % 2 == 0, hh == 1)
                mm.then_inc(wo_full, 1)

            def slot(s, p, c):
                static = isinstance(s, int)
                active = not static or s < UNITS
                if c == 3 and (not static or p + 1 < PAIRS):
                    lora_qk(p, 0, BLK_LQK0)
                if active:
                    project(p, c, 0)
                if not static or 0 <= s - 1 < UNITS:
                    scores(s - 1, (c + 1) % 2)
                if active:
                    project(p, c, 1)
                if not static or 0 <= s - 2 < UNITS:
                    turn_probs(s - 2, c % 2)
                if not static or 0 <= s - 3 < UNITS:
                    out_project(s - 3, p - (c < 3), (c + 1) % 4)
                if active:
                    if c == 0:
                        lora_v(p)
                    if c == 1:
                        values(p, 0)
                    if c == 2:
                        lora_o(p)
                        spline_weights(p, 0)
                        spline_weights(p, 1)
                    if c == 3:
                        values(p, 1)
                        if not static or p + 1 < PAIRS:
                            lora_qk(p, 1, BLK_LQK1)
                if not static or 0 <= s - 2 < UNITS:
                    probs_v(s - 2, p - (c < 2), (c + 2) % 4)
                if active and c == 2:
                    spline_weights(p, 2)

            pe.wait_ge(got_cst, 16)
            for n in range(4):
                dc, g = n // 2, n % 2
                for j in range(GB):
                    b = GB * g + j
                    wait_for(pe, x_normed, b + 1)
                    mm = pe.transpose(ring[n][:, T * j:T * j + T], acc[:, b, P * dc:P * dc + P], ident)
                mm.then_inc(blk_full, 1)
            pe.wait_ge(la_ready, 1)
            pe.wait_ge(lb_ready, 1)
            for hh in range(2):
                pe.wait_ge(blk_free, 2 + hh)
                for m in range(2):
                    for dc in range(DC):
                        n = 2 * m + dc
                        mm = pe.matmul(ring[1 + hh][:, P * n:P * n + P], la[:, m, P * dc:P * dc + P],
                                       lb[:, P * hh:P * hh + P], start=True, stop=True)
                mm.then_inc(blk_full, 1)
            pe.wait_ge(blk_free, 4)
            pe.wait_ge(small_cast, 2)
            pe.wait_ge(phi_cast, 1)
            for s in range(4):
                slot(s, 0, s)
            with pe.Fori(1, PAIRS - 1) as pair:
                for c in range(4):
                    slot(4 * pair + c, pair, c)
            for s in range(UNITS - 4, UNITS + 3):
                slot(s, s // 4, s % 4)

            def x1_to_channels(g):
                wait_for(pe, ln_ready, GB * (g + 1))
                wait_for(pe, blk_free, block_at(PAIRS - 1, BLK_V1 + 1) + 1)
                for c in range(DC):
                    for j in range(GB):
                        mm = pe.transpose(ring[2 * g + c][:, T * j:T * j + T],
                                          x_raw[:, GB * g + j, P * c:P * c + P], ident)
                    mm.then_inc(x1t_full, 1)

            def y_to_tokens(g):
                wait_for(pe, wkv_dve, WKV_DVE * DC * (g + 1))
                if g == 0:
                    wait_for(pe, exp_ready, UNITS)
                    wait_for(pe, ot_ready, UNITS)
                else:
                    wait_for(pe, x2t_ready, DC * g)
                for j, bank in enumerate((s_bank, to_bank)):
                    for n in range(2):
                        b = 2 * j + n
                        for c in range(DC):
                            mm = pe.transpose(bank[:, 256 * n + P * c:256 * n + P * c + P], y_t[c][:, b, :], ident)
                    mm.then_inc(y_full, 1)

            def x2_to_features(g):
                wait_for(pe, ln_ready, GB * (2 + g + 1))
                for c, bank in enumerate((s_bank, to_bank)):
                    for j in range(GB):
                        mm = pe.transpose(bank[:, T * j:T * j + T], x_raw[:, GB * g + j, P * c:P * c + P], ident)
                    mm.then_inc(x2t_full, 1)

            def down(g, ib):
                n = IB * g + ib
                wait_for(pe, inter_ready, n + 1)
                if ib == 0:
                    wait_for(pe, acc_added if g == 0 else down_added, 1 + 4 * PAIRS if g == 0 else 2 * g)
                for b in range(GB):
                    a = [part[:, b, :] for part in inner_parts[n % 2]]
                    mm = product(wo_bank[b // 2][:, 256 * (b % 2):256 * (b % 2) + 256], a,
                                 [fw[2][part][:, 256 * ib:256 * ib + 256] for part in range(2)],
                                 ib == 0 and b % 2 == 0, ib == IB - 1)
                mm.then_inc(down_full, 1)

            def ffn(g):
                cols = slice(GT * g, GT * g + GT)
                wait_for(pe, x2t_ready, DC * (g + 1))
                for ib in range(IB):
                    n = IB * g + ib
                    for w, full, used in ((0, gate_full, gate_used), (1, up_full, up_used)):
                        wait_for(pe, used, n - 1)
                        if n < 2:
                            wait_for(pe, k_copied, DC * GROUPS)
                        for hb in range(DC):
                            at = 256 * ib + P * hb
                            mm = product(ring[2 * (n % 2) + w][:, :], [fw[w][part][:, at:at + P] for part in range(2)],
                                         (xt_hi[:, hb, cols], xt_lo[:, hb, cols]), hb == 0, hb == DC - 1)
                        mm.then_inc(full, 1)
                    if ib > 0:
                        down(g, ib - 1)
                down(g, IB - 1)

            x1_to_channels(0)
            x1_to_channels(1)
            y_to_tokens(0)
            x2_to_features(0)
            wait_for(pe, fw_ready, 3 * PAIRS)
            ffn(0)
            y_to_tokens(1)
            x2_to_features(1)
            ffn(1)

        @block.scalar
        def _(act):
            copy = nc.scalar.activation

            def halves(p, c, m):
                k = (BLK_Q, BLK_K)[m][c]
                s = 4 * p + c
                wait_for(act, blk_full, block_at(p, k) + 1)
                wait_for(act, (q_ready, k_ready)[m], s)
                bank = ring[k % RING]
                flat = turned[m][:, :, :].rearrange("p b t -> p (b t)")
                copy(flat[0:64, :], bank[64:128, :], ACT.Copy)
                copy(flat[64:128, :], bank[0:64, :], ACT.Copy).then_inc(blk_mid, 1)

            def high_weights(n_parity, dst, free):
                wait_for(act, blk_free, free)
                copy(dst, w_sum[:, n_parity, :], ACT.Copy).then_inc(w_hi_ready, 1)

            def lora_high(e):
                wait_for(act, got_lb, 48 * (e + 1))
                copy(lb[:, :], lb_raw[:, :], ACT.Copy).then_inc(lb_hi_ready, 1)

            def flat3(t):
                return t.rearrange("p a b -> p (a b)")

            def exponentials(u, par):
                wait_for(act, max_ready, u + 1)
                wait_for(act, pt_full, u - 1)
                wait_for(act, inv_ready, u)
                for b in range(GB):
                    ins = copy(prob[par][:, b, :], s_bank[:, T * b:T * b + T], ACT.Exp,
                               bias=neg_max[:, b:b + 1], scale=1.0, accum_out=row_sum[:, b:b + 1])
                ins.then_inc(exp_ready, 1)

            def first_piece(p, w):
                k = BLK_GEN + w
                wait_for(act, blk_full, block_at(p, k) + 1)
                wait_for(act, fw_ready, 3 * p - 2 + w)
                copy(made[:, w, :], ring[k % RING][:, 0:CHUNK], ACT.Copy).then_inc(blk_mid, 1)

            def high_spline(p, w):
                wait_for(act, blk_free, block_at(p, BLK_GEN + w) + 1)
                dst, src = weight_views(w, p, 0)
                copy(dst, src, ACT.Copy).then_inc(fw_hi_ready, 1)

            def high_out(u):
                wait_for(act, ot_full, u + 1)
                wait_for(act, wo_full, u)
                copy(flat3(ot_hi[:, :, :]), to_bank[:, :], ACT.Copy).then_inc(ot_hi_ready, 1)

            def slot(s, p, c):
                static = isinstance(s, int)
                active = not static or s < UNITS
                if active:
                    halves(p, c, 0)
                if c == 3 and (not static or p + 1 < PAIRS):
                    wait_for(act, blk_full, block_at(p, BLK_LQK0) + 1)
                    high_weights(0, flat3(wqk[0][0][:, :, :]), block_at(p, BLK_LQK0) + 1)
                if not static or 0 <= s - 1 < UNITS:
                    exponentials(s - 1, (c + 1) % 2)
                if not static or 0 <= s - 2 < UNITS:
                    wait_for(act, pt_full, s - 1)
                    wait_for(act, ot_full, s - 2)
                    copy(flat3(pt[:, :, :]), to_bank[:, :], ACT.Copy).then_inc(pt_ready, 1)
                if active:
                    halves(p, c, 1)
                if active and c == 0:
                    wait_for(act, blk_full, block_at(p, BLK_LV) + 1)
                    high_weights(0, flat3(wv[0][:, :, :]), block_at(p, BLK_LV) + 1)
                if active and c == 1:
                    wait_for(act, blk_full, block_at(p, BLK_LV) + 1)
                    lora_high(p + 1)
                    wait_for(act, coef_made, p + 1)
                    if not static or p > 0:
                        wait_for(act, blk_full, block_at(p, BLK_GEN + 2) + 1 - PAIR_BLOCKS)
                    copy(flat3(coef_hi[:, :, :]), flat3(coef[:, :, :]), ACT.Copy).then_inc(coef_hi_ready, 1)
                if active and c == 2:
                    wait_for(act, blk_full, block_at(p, BLK_LWO) + 1)
                    wait_for(act, wo_full, 4 * p)
                    high_weights(1, flat3(wo[0][:, :, :]), block_at(p, BLK_LWO) + 1)
                    for w in range(3):
                        first_piece(p, w)
                if not static or 0 <= s - 2 < UNITS:
                    high_out(s - 2)
                if c == 3 and (not static or p + 1 < PAIRS):
                    wait_for(act, blk_full, block_at(p, BLK_LQK1) + 1)
                    high_weights(1, flat3(wqk[1][0][:, :, :]), block_at(p, BLK_LQK1) + 1)
                if active and c == 2:
                    for w in range(3):
                        high_spline(p, w)

            act.dma_start(sm[:, :, :], small).then_inc(got_small, 16)
            act.dma_start(cst[:, :, :], consts).then_inc(got_cst, 16)
            for b in range(B):
                wait_for(act, got_x, 32)
                if b:
                    act.wait_ge(squared, b)
                copy(squares[:, :], x_raw[:, b, :], ACT.Square, accum_out=sum_sq[:, b:b + 1]).then_inc(squared, 1)
            act.wait_ge(got_cst, 16)
            copy(phi[:, :, :], cst[:, 6:9, :], ACT.Copy).then_inc(phi_cast, 1)
            act.wait_ge(got_la, 48)
            copy(la[:, :, :], la_raw[:, :, :], ACT.Copy, scale=LORA_SCALE).then_inc(la_hi_ready, 1)
            lora_high(0)
            act.wait_ge(got_small, 16)
            for n in range(4):
                dc, g = n // 2, n % 2
                act.wait_ge(blk_full, n + 1)
                copy(xt_hi[:, dc, GT * g:GT * g + GT], ring[n][:, :], ACT.Copy, scale=sm[:, 0, dc:dc + 1]
                     ).then_inc(blk_mid, 1)
            copy(decay[:, :], sm[:, 1, :], ACT.Exp).then_inc(decay_exp, 1)
            for hh in range(2):
                act.wait_ge(blk_full, 5 + hh)
                high_weights(hh, flat3(wqk[hh][0][:, :, :]), 5 + hh)

            for s in range(4):
                slot(s, 0, s)
            with act.Fori(1, PAIRS - 1) as pair:
                for c in range(4):
                    slot(4 * pair + c, pair, c)
            for s in range(UNITS - 4, UNITS + 3):
                slot(s, s // 4, s % 4)

            def wkv(g, c):
                n = DC * g + c
                wait_for(act, x1t_full, n + 1)
                wait_for(act, exts_set, 4)
                wait_for(act, wkv_dve, WKV_DVE * n)
                wait_for(act, wkv_pool, WKV_POOL * n)
                copy(k_ext[:, :, 1:], ring[n][:, :].rearrange("p (b t) -> p b t", b=GB), ACT.Copy).then_inc(k_copied, 1)
                for buf, engine_sem, count in ((e_old[:, :, :], wkv_pool, WKV_POOL * n + 1),
                                               (e_new[:, :, :], wkv_dve, WKV_DVE * n + 3),
                                               (add_k[:, :, 1:], wkv_pool, WKV_POOL * n + 2),
                                               (keep[:, :, 1:], wkv_dve, WKV_DVE * n + 4)):
                    wait_for(act, engine_sem, count)
                    copy(buf, buf, ACT.Exp).then_inc(wkv_act, 1)

            def x2_high(g):
                for c, bank in enumerate((s_bank, to_bank)):
                    wait_for(act, x2t_full, DC * g + c + 1)
                    copy(xt_hi[:, c, GT * g:GT * g + GT], bank[:, :], ACT.Copy).then_inc(x2t_hi, 1)

            def ffn(g):
                def high(n):
                    wait_for(act, up_used, n + 1)
                    wait_for(act, down_full, n - 1)
                    copy(flat3(inner_parts[n % 2][0][:, :, :]), flat3(gated[n % 2][:, :, :]), ACT.Copy, scale=0.5).then_inc(inter_hi, 1)

                for ib in range(IB):
                    n = IB * g + ib
                    wait_for(act, gate_full, n + 1)
                    wait_for(act, gate_used, n - 1)
                    copy(flat3(th[n % 2]), ring[2 * (n % 2)][:, :], ACT.Tanh, scale=0.5).then_inc(tanh_ready, 1)
                    if ib:
                        high(n - 1)
                high(IB * g + IB - 1)

            wkv(0, 0)
            wkv(0, 1)
            x2_high(0)
            wkv(1, 0)
            wkv(1, 1)
            ffn(0)
            x2_high(1)
            ffn(1)

        @block.vector
        def _(dve):
            v = nc.vector

            def flat3(t):
                return t.rearrange("p a b -> p (a b)")

            def flat(t):
                return flat3(t[:, :, :])

            def low(dst, src, high):
                return v.tensor_tensor(dst, src, high.bitcast(F32), ALU.subtract)

            def cosine(p, c, m):
                k = (BLK_Q, BLK_K)[m][c]
                wait_for(dve, blk_mid, mid_at(p, k) + 1)
                wait_for(dve, (q_ready, k_ready)[m], 4 * p + c)
                v.tensor_tensor(straight[m][:, :, :], ring[k % RING][:, :].rearrange("p (b t) -> p b t", b=GB),
                                rope_cos[m].unsqueeze(1).to_broadcast([P, GB, T]), ALU.mult).then_inc(blk_free, 1)

            def sum_weights(n, parity, k, blk, raw, got, count):
                wait_for(dve, blk_full, blk + 1)
                wait_for(dve, got, count)
                wait_for(dve, w_ready, n - 1)
                v.tensor_tensor(w_sum[:, parity, :], ring[k % RING][:, :], raw, ALU.add).then_inc(blk_free, 1)

            def lora_low(e):
                wait_for(dve, lb_hi_ready, e + 1)
                low(lb[32:64, :], lb_raw[32:64, :], lb[32:64, :]).then_inc(lb_ready, 1)

            def add_rotated(u, p, c, m, ready):
                dst = (q_t, k_t)[m][c % 2]
                wait_for(dve, turned_ready, 2 * u + m + 1)
                wait_for(dve, blk_free, block_at(p, (BLK_Q, BLK_K)[m][c]) + 1)
                wait_for(dve, scores_ready, u - 1)
                v.tensor_tensor(dst[:, :, :], straight[m][:, :, :], turned[m][:, :, :], ALU.add).then_inc(ready, 1)

            def add_to_acc(u, p, g):
                wait_for(dve, wo_full, u + 1)
                wait_for(dve, acc_added, 1 + 4 * p)
                for j in range(2):
                    part = acc[:, GB * g + 2 * j:GB * g + 2 * j + 2, :]
                    v.tensor_tensor(flat3(part), wo_bank[j][:, :], flat3(part), ALU.add).then_inc(acc_added, 1)

            def new_values(p, g, j):
                k = (BLK_V0, BLK_V1)[g] + j
                wait_for(dve, blk_full, block_at(p, k) + 1)
                v.tensor_copy(flat3(v_now[g][:, 2 * j:2 * j + 2, :]), ring[k % RING][:, :]).then_inc(blk_free, 1)

            def second_piece(p, w):
                k = BLK_GEN + w
                wait_for(dve, blk_mid, mid_at(p, k) + 1)
                wait_for(dve, got_second, 16 * (p + 1))
                dve.sem_inc(piece_due, 1)
                v.copy_predicated(made[:, w, :], second[:, :], ring[k % RING][:, CHUNK:2 * CHUNK]
                                  ).then_inc(blk_free, 1)

            def low_spline(p, w):
                wait_for(dve, fw_hi_ready, 3 * p + w + 1)
                dst, src = weight_views(w, p, 1)
                low(dst, src, weight_views(w, p, 0)[0]).then_inc(fw_ready, 1)

            def slot(s, p, c):
                static = isinstance(s, int)
                active = not static or s < UNITS
                if c == 3 and (not static or p + 1 < PAIRS):
                    sum_weights(4 * p + 4, 0, BLK_LQK0, block_at(p, BLK_LQK0), w_raw[:, 0, :], got_w, 16 * (p + 2))
                if active and c % 2 == 1 and (not static or s >= 4):
                    add_to_acc(s - 4, p - 1, c // 2)
                if not static or 0 <= s - 1 < UNITS:
                    wait_for(dve, scores_ready, s)
                    wait_for(dve, exp_ready, s - 1)
                    v.tensor_reduce(neg_max[:, :], s_bank[:, :].rearrange("p (b t) -> p b t", b=GB), AX.X, ALU.max,
                                    negate=True).then_inc(max_ready, 1)
                if active:
                    cosine(p, c, 0)
                if not static or 0 <= s - 1 < UNITS:
                    wait_for(dve, exp_ready, s)
                    wait_for(dve, prob_ready, s - 1)
                    v.reciprocal(row_inv[:, :], row_sum[:, :]).then_inc(inv_ready, 1)
                if active:
                    cosine(p, c, 1)
                if static and s >= UNITS and c % 2 == 0:
                    add_to_acc(s - 3, p - 1, (c + 1) % 4 // 2)
                if active:
                    if c in (1, 3):
                        new_values(p, c // 2, 0)
                    add_rotated(s, p, c, 0, q_ready)
                    if c == 0:
                        sum_weights(4 * p + 2, 0, BLK_LV, block_at(p, BLK_LV), w_raw[:, 2, :], got_w, 16 * (p + 1))
                    if c in (1, 3):
                        new_values(p, c // 2, 1)
                    if c == 2:
                        sum_weights(4 * p + 3, 1, BLK_LWO, block_at(p, BLK_LWO), wo_raw[:, :], got_wo, 16 * (p + 1))
                    add_rotated(s, p, c, 1, k_ready)
                    if c == 1:
                        lora_low(p + 1)
                    if c == 2:
                        for w in range(3):
                            second_piece(p, w)
                    if c == 3 and (not static or p + 1 < PAIRS):
                        sum_weights(4 * p + 5, 1, BLK_LQK1, block_at(p, BLK_LQK1), w_raw[:, 1, :], got_w, 16 * (p + 2))
                if not static or 0 <= s - 2 < UNITS:
                    wait_for(dve, ot_hi_ready, s - 1)
                    low(flat(ot_lo), to_bank[:, :], flat(ot_hi)).then_inc(ot_ready, 1)
                if active and c == 2:
                    for w in range(3):
                        low_spline(p, w)

            dve.wait_ge(la_hi_ready, 1)
            v.scalar_tensor_tensor(la[64:96, :, :], la_raw[64:96, :, :], LORA_SCALE, la[64:96, :, :].bitcast(F32),
                                   ALU.mult, ALU.subtract).then_inc(la_ready, 1)
            lora_low(0)
            for b in range(B):
                wait_for(dve, rms_ready, 1)
                v.tensor_scalar(acc[:, b, :], x_raw[:, b, :], rms_inv[:, b:b + 1], None, ALU.mult).then_inc(x_normed, 1)
            dve.wait_ge(got_cst, 16)
            v.tensor_copy(ident_b[:, :], ident).then_inc(small_cast, 1)
            v.tensor_copy(mask_b[:, :], cst[:, 5, :]).then_inc(small_cast, 1)
            for n in range(4):
                dc, g = n // 2, n % 2
                cols = slice(GT * g, GT * g + GT)
                dve.wait_ge(blk_mid, n + 1)
                v.scalar_tensor_tensor(xt_lo[:, dc, cols], ring[n][:, :], sm[:, 0, dc:dc + 1],
                                       xt_hi[:, dc, cols].bitcast(F32), ALU.mult, ALU.subtract).then_inc(blk_free, 1)
            sum_weights(0, 0, 1, 4, w_raw[:, 0, :], got_w, 16)
            sum_weights(1, 1, 2, 5, w_raw[:, 1, :], got_w, 16)
            dve.wait_ge(blk_full, 4)
            v.tensor_scalar(acc[:, :, :], x_raw[:, :, :], 2.0, None, ALU.mult).then_inc(acc_added, 1)

            for s in range(4):
                slot(s, 0, s)
            with dve.Fori(1, PAIRS - 1) as pair:
                for c in range(4):
                    slot(4 * pair + c, pair, c)
            for s in range(UNITS - 4, UNITS + 3):
                slot(s, s // 4, s % 4)

            def layer_norm(n, g, src):
                for j in range(GB):
                    b = GB * g + j
                    wait_for(dve, ln_ready, GB * n)
                    v.bn_stats(stats[:, j, :], src[:, b, :]).then_inc(stats_step, 1)
                for j in range(GB):
                    wait_for(dve, stats_step, GB * n + j + 1)
                    v.bn_aggr(mean_var[:, j, :], stats[:, j, :]).then_inc(stats_ready, 1)
                wait_for(dve, ln_inv_ready, n + 1)
                wait_for(dve, stats_ready, GB * n + GB)
                for j in range(GB):
                    b = GB * g + j
                    v.tensor_scalar(x_raw[:, b, :], src[:, b, :], mean_var[:, j, 0:1], ln_inv[:, j:j + 1],
                                    ALU.subtract, ALU.mult).then_inc(ln_ready, 1)

            def wkv(g, c):
                n = DC * g + c
                done = WKV_DVE * n
                decay_c, first_c = decay[:, c:c + 1], sm[:, 2, c:c + 1]
                k_now = k_ext[:, :, 1:]
                before, now = top[:, :, 0:T], top[:, :, 1:]
                wait_for(dve, k_copied, n + 1)
                wait_for(dve, wkv_dve, done)
                wait_for(dve, wkv_pool, WKV_POOL * n)
                v.tensor_tensor_scan(flat(top), flat(decay_tab[c]), flat(k_ext), NO_STATE, ALU.add, ALU.max
                                     ).then_inc(wkv_dve, 1)
                dve.wait_ge(wkv_dve, done + 1)
                v.scalar_tensor_tensor(peak[:, :, :], k_now, first_c, before, ALU.add, ALU.max).then_inc(wkv_dve, 1)
                dve.wait_ge(wkv_dve, done + 2)
                v.scalar_tensor_tensor(e_new[:, :, :], k_now, first_c, peak[:, :, :], ALU.add, ALU.subtract
                                       ).then_inc(wkv_dve, 1)
                v.scalar_tensor_tensor(keep[:, :, 1:], before, decay_c, now, ALU.add, ALU.subtract
                                       ).then_inc(wkv_dve, 1)
                dve.wait_ge(wkv_act, WKV_ACT * n + 4)
                v.tensor_tensor_scan(flat(bb), flat(keep), flat(add_k), 0.0, ALU.mult, ALU.add).then_inc(wkv_dve, 1)
                dve.wait_ge(wkv_pool, WKV_POOL * n + 3)
                v.tensor_tensor_scan(flat(aa), flat(keep), flat(add_v), 0.0, ALU.mult, ALU.add).then_inc(wkv_dve, 1)
                dve.wait_ge(wkv_pool, WKV_POOL * n + 4)
                v.tensor_tensor(den[:, :, :], den[:, :, :], e_new[:, :, :], ALU.add).then_inc(wkv_dve, 1)
                dve.wait_ge(wkv_dve, done + 7)
                v.reciprocal(den_inv[:, :, :], den[:, :, :]).then_inc(wkv_dve, 1)
                dve.wait_ge(wkv_pool, WKV_POOL * n + 6)
                v.tensor_tensor(num[:, :, :], num[:, :, :], peak[:, :, :], ALU.add).then_inc(wkv_dve, 1)
                dve.wait_ge(wkv_dve, done + 9)
                wait_for(dve, y_full, 2 * g)
                v.tensor_tensor(y_t[c][:, :, :], num[:, :, :], den_inv[:, :, :], ALU.mult).then_inc(wkv_dve, 1)

            def add_y(g):
                for j, bank in enumerate((s_bank, to_bank)):
                    part = flat3(x_raw[:, GB * g + 2 * j:GB * g + 2 * j + 2, :])
                    wait_for(dve, y_full, 2 * g + j + 1)
                    v.tensor_tensor(part, bank[:, :], part, ALU.add).then_inc(y_added, 1)
                dve.wait_ge(y_added, 2 * g + 2)

            def x2_low(g):
                for c, bank in enumerate((s_bank, to_bank)):
                    cols = slice(GT * g, GT * g + GT)
                    wait_for(dve, x2t_hi, DC * g + c + 1)
                    low(xt_lo[:, c, cols], bank[:, :], xt_hi[:, c, cols]).then_inc(x2t_ready, 1)

            def ffn(g):
                def low_half(n):
                    wait_for(dve, inter_hi, n + 1)
                    hi, lo = inner_parts[n % 2]
                    v.scalar_tensor_tensor(flat(lo), flat(gated[n % 2]), 0.5, flat(hi).bitcast(F32),
                                           ALU.mult, ALU.subtract).then_inc(inter_ready, 1)

                for ib in range(IB):
                    n = IB * g + ib
                    wait_for(dve, tanh_ready, n + 1)
                    wait_for(dve, inter_ready, n - 1)
                    v.scalar_tensor_tensor(flat(gated[n % 2]), flat3(th[n % 2]), 1.0, ring[2 * (n % 2)][:, :],
                                           ALU.add, ALU.mult).then_inc(gate_used, 1)
                    if ib:
                        low_half(n - 1)
                    wait_for(dve, gate_used, n + 1)
                    wait_for(dve, up_full, n + 1)
                    v.tensor_tensor(flat(gated[n % 2]), ring[2 * (n % 2) + 1][:, :], flat(gated[n % 2]), ALU.mult
                                    ).then_inc(up_used, 1)
                low_half(IB * g + IB - 1)

            def add_down(g):
                wait_for(dve, down_full, IB * (g + 1))
                for j in range(2):
                    part = flat3(x_raw[:, GB * g + 2 * j:GB * g + 2 * j + 2, :])
                    v.tensor_tensor(part, wo_bank[j][:, :], part, ALU.add).then_inc(down_added, 1)
                dve.wait_ge(down_added, 2 * g + 2)

            dve.wait_ge(decay_exp, 1)
            v.tensor_scalar(decay[:, :], decay[:, :], -1.0, None, ALU.mult).then_inc(tables_step, 1)
            for c in range(DC):
                v.memset(decay_tab[c][:, :, :], 0.0).then_inc(tables_step, 1)
            dve.wait_ge(tables_step, 1 + DC)
            for c in range(DC):
                v.tensor_scalar(decay_tab[c][:, :, :], decay_tab[c][:, :, :], decay[:, c:c + 1], None, ALU.add
                                ).then_inc(tables_step, 1)
            dve.wait_ge(tables_step, 1 + 2 * DC)
            for c in range(DC):
                v.memset(decay_tab[c][:, :, 0:1], FORGET).then_inc(tables_step, 1)
            v.memset(k_ext[:, :, 0:1], NO_STATE).then_inc(exts_set, 1)
            for t in (keep, add_k, add_v):
                v.memset(t[:, :, 0:1], 0.0).then_inc(exts_set, 1)
            dve.wait_ge(tables_step, 1 + 3 * DC)
            dve.wait_ge(exts_set, 4)
            for g in range(GROUPS):
                dve.wait_ge(acc_added, 1 + 4 * (PAIRS - 1) + 2 * g + 2)
                layer_norm(g, g, acc)
            dve.wait_ge(got_v, 16)
            wkv(0, 0)
            wkv(0, 1)
            add_y(0)
            layer_norm(2, 0, x_raw)
            x2_low(0)
            wkv(1, 0)
            wkv(1, 1)
            ffn(0)
            add_y(1)
            layer_norm(3, 1, x_raw)
            x2_low(1)
            add_down(0)
            layer_norm(4, 0, x_raw)
            ffn(1)
            add_down(1)
            layer_norm(5, 1, x_raw)

        @block.gpsimd
        def _(pool):
            gp = nc.gpsimd

            def flat3(t):
                return t.rearrange("p a b -> p (a b)")

            def sine(p, c, m):
                s = 4 * p + c
                wait_for(pool, blk_mid, mid_at(p, (BLK_Q, BLK_K)[m][c]) + 1)
                gp.tensor_tensor(turned[m][:, :, :], turned[m][:, :, :],
                                 rope_sin[m].unsqueeze(1).to_broadcast([P, GB, T]), ALU.mult).then_inc(turned_ready, 1)

            def low_weights(n, parity, dst, high):
                wait_for(pool, w_hi_ready, n + 1)
                gp.tensor_tensor(dst, w_sum[:, parity, :], high.bitcast(F32), ALU.subtract).then_inc(w_ready, 1)

            def slot(s, p, c):
                static = isinstance(s, int)
                active = not static or s < UNITS
                if active and c == 1:
                    wait_for(pool, got_knots, 16 * (p + 1))
                    wait_for(pool, got_tab, 48 * (p + 1))
                    wait_for(pool, coef_ready, p)
                    gp.tensor_tensor(coef[:, :, :], spline_tab[:, :, :],
                                     knot_rows[:, :].unsqueeze(1).to_broadcast([96, 2, CHUNK]), ALU.mult
                                     ).then_inc(coef_made, 1)
                if active and c == 0 and (not static or p > 0):
                    low_weights(4 * p + 1, 1, flat3(wqk[1][1][:, :, :]), flat3(wqk[1][0][:, :, :]))
                if active:
                    sine(p, c, 0)
                if c == 3 and (not static or p + 1 < PAIRS):
                    low_weights(4 * p + 4, 0, flat3(wqk[0][1][:, :, :]), flat3(wqk[0][0][:, :, :]))
                if not static or 0 <= s - 1 < UNITS:
                    par = (c + 1) % 2
                    wait_for(pool, inv_ready, s)
                    gp.tensor_tensor(prob[par][:, :, :], prob[par][:, :, :],
                                     row_inv[:, :].unsqueeze(2).to_broadcast([P, GB, T]), ALU.mult
                                     ).then_inc(prob_ready, 1)
                if active:
                    sine(p, c, 1)
                if active and c == 0:
                    low_weights(4 * p + 2, 0, flat3(wv[1][:, :, :]), flat3(wv[0][:, :, :]))
                if active and c == 1:
                    wait_for(pool, coef_hi_ready, p + 1)
                    gp.tensor_tensor(flat3(coef_lo[:, :, :]), flat3(coef[:, :, :]),
                                     flat3(coef_hi[:, :, :]).bitcast(F32), ALU.subtract).then_inc(coef_ready, 1)
                if active and c == 2:
                    low_weights(4 * p + 3, 1, flat3(wo[1][:, :, :]), flat3(wo[0][:, :, :]))

            gp.memset(half[:, :], -0.5).then_inc(half_set, 1)
            pool.wait_ge(squared, B)
            gp.tensor_scalar(mean_sq[:, :], sum_sq[:, :], 1.0 / D, RMS_EPS, ALU.mult, ALU.add).then_inc(rms_step, 1)
            pool.wait_ge(rms_step, 1)
            pool.wait_ge(half_set, 1)
            gp.tensor_tensor(rms_inv[:, :], mean_sq[:, :], half[:, :], ALU.pow).then_inc(rms_ready, 1)
            for hh in range(2):
                low_weights(hh, hh, flat3(wqk[hh][1][:, :, :]), flat3(wqk[hh][0][:, :, :]))
            pool.wait_ge(got_cst, 16)

            for s in range(4):
                slot(s, 0, s)
            with pool.Fori(1, PAIRS - 1) as pair:
                for c in range(4):
                    slot(4 * pair + c, pair, c)
            for s in range(UNITS - 4, UNITS + 3):
                slot(s, s // 4, s % 4)

            def layer_norm(n):
                wait_for(pool, stats_ready, GB * (n + 1))
                gp.tensor_scalar(var_eps[:, :], mean_var[:, :, 1], LN_EPS, None, ALU.add).then_inc(ln_step, 1)
                wait_for(pool, ln_step, n + 1)
                wait_for(pool, ln_ready, GB * n)
                gp.tensor_tensor(ln_inv[:, :], var_eps[:, :], half[:, 0:GB], ALU.pow).then_inc(ln_inv_ready, 1)

            def wkv(g, c):
                n = DC * g + c
                v_now = v_t[:, c, GT * g:GT * g + GT].rearrange("p (b t) -> p b t", b=GB)
                before, now = top[:, :, 0:T], top[:, :, 1:]
                pool.wait_ge(wkv_dve, WKV_DVE * n + 2)
                gp.tensor_tensor(e_old[:, :, :], before, peak[:, :, :], ALU.subtract).then_inc(wkv_pool, 1)
                gp.tensor_tensor(add_k[:, :, 1:], k_ext[:, :, 1:], now, ALU.subtract).then_inc(wkv_pool, 1)
                pool.wait_ge(wkv_act, WKV_ACT * n + 3)
                gp.tensor_tensor(add_v[:, :, 1:], add_k[:, :, 1:], v_now, ALU.mult).then_inc(wkv_pool, 1)
                pool.wait_ge(wkv_dve, WKV_DVE * n + 5)
                gp.tensor_tensor(den[:, :, :], e_old[:, :, :], bb[:, :, 0:T], ALU.mult).then_inc(wkv_pool, 1)
                gp.tensor_tensor(peak[:, :, :], e_new[:, :, :], v_now, ALU.mult).then_inc(wkv_pool, 1)
                pool.wait_ge(wkv_dve, WKV_DVE * n + 6)
                gp.tensor_tensor(num[:, :, :], e_old[:, :, :], aa[:, :, 0:T], ALU.mult).then_inc(wkv_pool, 1)

            pool.wait_ge(got_v, 16)
            layer_norm(0)
            layer_norm(1)
            wkv(0, 0)
            wkv(0, 1)
            layer_norm(2)
            wkv(1, 0)
            wkv(1, 1)
            layer_norm(3)
            layer_norm(4)
            layer_norm(5)


def spline_tables():
    import numpy as np

    knots_n = max(16, int(INTER * D / 128.9))
    t = np.linspace(0.0, knots_n - 1.0, D * INTER, dtype=np.float64)
    interval = np.clip(np.floor(t).astype(np.int64), 0, knots_n - 2).reshape(COLUMNS, P)
    j = np.arange(COLUMNS)
    base = 127 * (j // P) + j % P - 2
    first = interval[:, 0]
    second = (interval != first[:, None]).T.astype(np.int32)
    catmull = 0.5 * np.array([[0, -1, 2, -1], [2, 0, -5, 3], [0, 1, 4, -3], [0, 0, -1, 1]], np.float64)
    table = np.zeros((32, 2, COLUMNS))
    for side in (0, 1):
        a = t.reshape(COLUMNS, P)[:, 64] - first - side
        s = 64 * t[1]
        powers = np.zeros((4, 4, COLUMNS))
        powers[0, 0] = 1
        powers[1, 0], powers[1, 1] = a, s
        powers[2, 0], powers[2, 1], powers[2, 2] = a ** 2, 2 * a * s, s * s
        powers[3, 0], powers[3, 1], powers[3, 2], powers[3, 3] = a ** 3, 3 * a ** 2 * s, 3 * a * s * s, s ** 3
        for k in range(4):
            kk = np.clip(first + side - 1 + k, 0, knots_n - 1) - base
            co = np.einsum("m,mrj->rj", catmull[k], powers)
            ok = (kk >= 0) & (kk < 6)
            for r in range(5):
                np.add.at(table[:, side], (np.where(ok, kk * 5 + r, 31), j), np.where(ok, co[min(r, 3)], 0))
    q = (np.arange(P) - 64) / 64.0
    mantissa, exponent = np.frexp(q ** 3)
    high = np.ldexp(np.rint(mantissa * 4096) / 4096, exponent)
    phi = np.zeros((32, P))
    for kk in range(6):
        phi[5 * kk:5 * kk + 5] = [q ** 0, q, q * q, high, q ** 3 - high]
    return table.astype(np.float32), second, phi.astype(np.float32)


def constant_tables(phi):
    import numpy as np

    half = DH // 2
    theta = (1.0 / 10000.0 ** (np.arange(half) / half)).astype(np.float32)
    angle = (np.arange(T, dtype=np.float32)[:, None] * theta[None, :]).astype(np.float64).T
    cos = np.concatenate([np.cos(angle), np.cos(angle)])
    sin = np.concatenate([-np.sin(angle), np.sin(angle)])
    consts = np.zeros((P, 9, P), np.float32)
    scale = DH ** -0.5
    consts[:, 0], consts[:, 1], consts[:, 2], consts[:, 3] = cos * scale, sin * scale, cos, sin
    consts[:, 4] = np.eye(P)
    i, j = np.arange(T)[:, None], np.arange(T)[None, :]
    consts[:, 5] = np.where((j <= i) & (j >= i - WINDOW + 1), 0.0, MASKED)
    for w in range(3):
        consts[32 * w:32 * w + 32, 6 + w] = phi
    return consts


def lay_out(inputs):
    import numpy as np

    a = {k.replace("L0_", "").replace("attn_", ""): np.asarray(v) for k, v in inputs.items()}
    f = np.float32
    table, second, phi = spline_tables()
    arrays = {"x": a["x"], "ctx_t": np.ascontiguousarray(a["ctx_2048"].reshape(B * T, D).T)}
    arrays["small"] = np.ascontiguousarray(np.stack(
        [a["norm_w"], a["xtime_decay"], a["xtime_first"]]).reshape(3, DC, P).transpose(2, 0, 1))
    arrays["consts"] = constant_tables(phi)

    lora_a = np.zeros((32, 4, D), f)
    lora_a[0:16, 0], lora_a[16:32, 1], lora_a[0:16, 2] = a["qA"], a["kA"], a["vA"]
    lora_a[0:16, 3] = a["oB"].T
    arrays["lora_a"] = lora_a.reshape(32, 4 * D)
    lora_b = np.zeros((PAIRS + 1, 32, 3, 2 * DH), f)
    by_pair = lambda m: m.reshape(RANK, PAIRS, 2 * DH).transpose(1, 0, 2)
    lora_b[:PAIRS, 0:16, 0], lora_b[:PAIRS, 16:32, 0] = by_pair(a["qB"].T), by_pair(a["kB"].T)
    lora_b[:PAIRS, 0:16, 1] = by_pair(a["vB"].T)
    lora_b[1:, 0:16, 2] = by_pair(a["oA"])
    arrays["lora_b"] = lora_b.reshape(PAIRS + 1, 32, 3 * 2 * DH)

    w_qkv = np.zeros((PAIRS, P, 3, 512), f)
    q = a["wq"].reshape(PAIRS, 2, DH, DC, P).transpose(0, 4, 1, 3, 2)
    k = a["wk"].reshape(PAIRS, 2, DH, DC, P).transpose(0, 4, 1, 3, 2)
    w_qkv[:, :, 0:2, 0:256] = q.reshape(PAIRS, P, 2, 256)
    w_qkv[:, :, 0:2, 256:512] = k.reshape(PAIRS, P, 2, 256)
    v = a["wv"].reshape(PAIRS, 2 * DH, DC, P).transpose(0, 3, 2, 1)
    w_qkv[:, :, 2] = v.reshape(PAIRS, P, 512)
    arrays["w_qkv"] = w_qkv.reshape(PAIRS, P, 3 * 512)
    arrays["w_o"] = np.ascontiguousarray(
        a["wo"].reshape(D, PAIRS, 2, DH).transpose(1, 3, 2, 0)).reshape(PAIRS, DH, 512)

    knots = np.zeros((3, 32, 16, P), f)
    for w, name in enumerate(("ffn_gate_cp", "ffn_up_cp", "ffn_down_cp")):
        padded = np.pad(a[name], (2, 8))
        for kk in range(6):
            for jb in range(16):
                knots[w, 5 * kk:5 * kk + 5, jb] = padded[127 * jb + kk:127 * jb + kk + P]
    arrays["knots"] = np.ascontiguousarray(
        knots.reshape(96, PAIRS, CHUNK).transpose(1, 0, 2))
    arrays["spline"] = np.ascontiguousarray(
        table.reshape(32, 2, PAIRS, CHUNK).transpose(2, 0, 1, 3)).reshape(PAIRS, 32, 2 * CHUNK)
    arrays["piece"] = np.ascontiguousarray(second.reshape(P, PAIRS, CHUNK).transpose(1, 0, 2))
    return arrays


def kernel(**inputs):
    import numpy as _np
    import concourse.bacc as _bacc
    from concourse import mybir as _mybir
    from concourse.bass_utils import run_bass_kernel_spmd as _run

    nc = _bacc.Bacc("TRN2", target_bir_lowering=False, num_devices=1)
    arrays, args = {}, []
    for name, a in lay_out(inputs).items():
        a = _np.ascontiguousarray(a)
        arrays[f"in_{name}_dram"] = a
        args.append(nc.dram_tensor(f"in_{name}_dram", a.shape, _mybir.dt.from_np(a.dtype), kind="ExternalInput").ap())
    args.append(nc.dram_tensor("out_0_dram", (B, T, D), F32, kind="ExternalOutput").ap())
    decoder_layer(nc, *args)
    r = _run(nc, [arrays], core_ids=[0])
    return r.results[0]["out_0_dram"]
```

```python
from contextlib import ExitStack

import concourse.bass as bass
from concourse import mybir

F32 = mybir.dt.float32
F32R = mybir.dt.float32r
I32 = mybir.dt.int32
ALU = mybir.AluOpType
ACT = mybir.ActivationFunctionType
AX = mybir.AxisListType

P = 128
B, T, D = 8, 128, 256
H, DH = 16, 128
RANK = 16
WINDOW = 64
INTER = 1024
PAIRS = H // 2
GROUPS = 2
GB = B // GROUPS
GT = GB * T
DC = D // P
UNITS = PAIRS * GROUPS * 2
IB = INTER // P
CHUNK = 256
COLUMNS = D * INTER // P
RMS_EPS = 1e-6
LN_EPS = 1e-5
LORA_SCALE = 1.0 / RANK
NO_STATE = -1e38
FORGET = -2e38
MASKED = -3e38

RING = 4
BLK_Q0, BLK_K0, BLK_LV = 0, 1, 2
BLK_Q1, BLK_K1, BLK_V0 = 3, 4, 5
BLK_Q2, BLK_K2, BLK_LWO, BLK_GEN = 7, 8, 9, 10
BLK_LQK0, BLK_Q3, BLK_K3, BLK_V1, BLK_LQK1 = 13, 14, 15, 16, 18
PAIR_BLOCKS = 19
FIRST_BLOCKS = 4
BLK_Q = [BLK_Q0, BLK_Q1, BLK_Q2, BLK_Q3]
BLK_K = [BLK_K0, BLK_K1, BLK_K2, BLK_K3]
MID = {BLK_Q0: 0, BLK_K0: 1, BLK_Q1: 2, BLK_K1: 3, BLK_Q2: 4, BLK_K2: 5, BLK_GEN: 6, BLK_GEN + 1: 7,
       BLK_GEN + 2: 8, BLK_Q3: 9, BLK_K3: 10}
PAIR_MIDS = 11
CHUNKS = GROUPS * DC
FIRST_MIDS = 2


def block_at(p, k):
    if isinstance(p, int) and p == PAIRS - 1 and k > BLK_LQK0:
        k -= 1
    return FIRST_BLOCKS + PAIR_BLOCKS * p + k


def mid_at(p, k):
    return FIRST_MIDS + PAIR_MIDS * p + MID[k]


def bank_user_before(p, k):
    if k >= RING:
        return block_at(p, k - RING)
    if isinstance(p, int) and p == 0:
        return [2, 0, 1, 3][k]
    return block_at(p - 1, {0: BLK_V1, 1: BLK_V1 + 1, 2: BLK_LQK1, 3: BLK_K3}[k])


def wait_for(engine, sem, count):
    if isinstance(count, int) and count <= 0:
        return
    engine.wait_ge(sem, count)


def decoder_layer(nc, x, ctx_t, small, consts, lora_a, lora_b, w_qkv, w_o, knots, spline, piece, out):
    with ExitStack() as stack:
        def sb(name, shape, dt=F32):
            return stack.enter_context(nc.sbuf_tensor(name, shape, dt))

        def ps(name):
            return stack.enter_context(nc.psum_tensor(name, [P, 512], F32))

        def sem(name):
            return stack.enter_context(nc.semaphore(name))

        x_raw = sb("x_raw", [P, B, D])
        acc = sb("acc", [P, B, D])
        xt_hi = sb("xt_hi", [P, DC, B * T], F32R)
        xt_lo = sb("xt_lo", [P, DC, B * T], F32R)
        v_t = sb("v_t", [P, DC, B * T])
        cst = sb("cst", [P, 9, P])
        sm = sb("sm", [P, 3, DC])
        phi = sb("phi", [P, 3, P], F32R)
        ident = cst[:, 0, :]
        rope_cos = [cst[:, 2, :], cst[:, 4, :]]
        rope_sin = [cst[:, 3, :], cst[:, 5, :]]

        la = sb("la", [96, 4, D], F32R)
        lb_raw = sb("lb_raw", [96, 3 * D])
        lb = sb("lb", [96, 3 * D], F32R)
        w_raw = sb("w_raw", [P, 3, 512])
        wo_raw = sb("wo_raw", [P, 512])
        w_sum = sb("w_sum", [P, 2, 512])
        wqk = [[sb(f"wqk{hh}_{part}", [P, 4, P], F32R) for part in ("hi", "lo")] for hh in range(2)]
        wv = [sb(f"wv_{part}", [P, DC, 2 * DH], F32R) for part in ("hi", "lo")]
        wo = [sb(f"wo_{part}", [P, 2, D], F32R) for part in ("hi", "lo")]

        straight = [sb(f"straight{n}", [P, GB, T]) for n in range(2)]
        turned = [sb(f"turned{n}", [P, GB, T]) for n in range(2)]
        q_t = [sb(f"q_t{n}", [P, GB, T]) for n in range(2)]
        k_t = [sb(f"k_t{n}", [P, GB, T]) for n in range(2)]
        v_now = [sb(f"v_now{g}", [P, GB, 2 * DH]) for g in range(GROUPS)]
        prob = [sb(f"prob{n}", [P, GB, T]) for n in range(2)]
        pt = sb("pt", [P, GB, T])
        ot_hi = sb("ot_hi", [P, GB, T], F32R)
        ot_lo = sb("ot_lo", [P, GB, T], F32R)
        inner_parts = [(sb("inner_hi", [P, GB, T], F32R), sb("inner_lo", [P, GB, T], F32R)), (ot_hi, ot_lo)]
        neg_max = sb("neg_max", [P, GB])
        row_sum = sb("row_sum", [P, GB])
        row_inv = sb("row_inv", [P, GB])

        knot_rows = sb("knot_rows", [96, CHUNK])
        spline_tab = sb("spline_tab", [96, 2, CHUNK])
        second = sb("second", [P, CHUNK], I32)
        coef = sb("coef", [96, 2, CHUNK])
        coef_hi = sb("coef_hi", [96, 2, CHUNK], F32R)
        coef_lo = sb("coef_lo", [96, 2, CHUNK], F32R)
        made = sb("made", [P, 3, CHUNK])
        fw = [[sb(f"fw{w}_{part}", [P, COLUMNS], F32R) for part in ("hi", "lo")] for w in range(3)]

        squares = sb("squares", [P, D])
        sum_sq = sb("sum_sq", [P, B])
        mean_sq = sb("mean_sq", [P, B])
        rms_inv = sb("rms_inv", [P, B])
        half = sb("half", [P, B])
        stats = sb("stats", [P, 2, GB, 6])
        mean_var = sb("mean_var", [P, 2, GB, 2])
        var_eps = sb("var_eps", [P, 2, GB])
        ln_inv = sb("ln_inv", [P, 2, GB])

        decay = sb("decay", [P, DC])
        decay_tab = [sb(f"decay_tab{c}", [P, GB, T + 1]) for c in range(DC)]
        scan_bufs = sb("scan_bufs", [P, 7, GB * (T + 1)])
        k_first, top_first, keep, add_k, add_v, aa, bb = [
            scan_bufs[:, n, :].rearrange("p (b t) -> p b t", b=GB) for n in range(7)]
        k_second = w_sum[:, :, :].rearrange("p a n -> p (a n)")[:, 0:GB * (T + 1)].rearrange("p (b t) -> p b t", b=GB)
        k_ext = [k_first, k_second]
        top_second = acc[:, 0:GB, :].rearrange("p b d -> p (b d)")[:, 0:GB * (T + 1)].rearrange("p (b t) -> p b t", b=GB)
        top = [top_first, top_second]
        la_raw = scan_bufs[0:96, 0:2, :].rearrange("p a n -> p (a n)")[:, 0:4 * D].rearrange("p (k n) -> p k n", k=4)
        raw_part = [w_raw[:, n, :].rearrange("p (b t) -> p b t", b=GB) for n in range(3)]
        out_gap, e_old, e_new = [q_t[0], raw_part[0]], [q_t[1], raw_part[1]], [k_t[0], raw_part[2]]
        state_gap = [v_now[n // DC][:, 2 * (n % DC):2 * (n % DC) + 2, :].rearrange("p a n -> p (a n)")
                     .rearrange("p (b t) -> p b t", b=GB) for n in range(GROUPS * DC)]
        y_t = [k_t[1], straight[0]]
        den_inv = straight[1]
        num = turned[0]
        den = turned[1]
        new_v = pt
        gated = [prob[0], prob[1]]
        th = [v_now[0][:, 0:2, :], v_now[0][:, 2:4, :]]

        ring = [ps(f"ring{n}") for n in range(RING)]
        s_bank = ps("s_bank")
        to_bank = ps("to_bank")
        wo_bank = [ps(f"wo_bank{n}") for n in range(2)]

        x1_bank = [[ring[0], ring[1]], [ring[2], ring[3]]]

        got_x0, got_x1, got_small, got_la = sem("got_x0"), sem("got_x1"), sem("got_small"), sem("got_la")
        got_ident, got_cst = sem("got_ident"), sem("got_cst")
        got_lb, got_w, got_wo = sem("got_lb"), sem("got_w"), sem("got_wo")
        got_knots, got_tab, got_second, got_v = sem("got_knots"), sem("got_tab"), sem("got_second"), sem("got_v")
        stored = sem("stored")
        xt1_full, xt1_hi_ready, xt1_ready = sem("xt1_full"), sem("xt1_hi_ready"), sem("xt1_ready")
        squared, rms_step, rms_ready, x_normed = sem("squared"), sem("rms_step"), sem("rms_ready"), sem("x_normed")
        half_set = sem("half_set")
        phi_cast = sem("phi_cast")
        la_hi_ready, la_ready = sem("la_hi_ready"), sem("la_ready")
        blk_full, blk_mid, blk_free = sem("blk_full"), sem("blk_mid"), sem("blk_free")
        lb_hi_ready, lb_ready = sem("lb_hi_ready"), sem("lb_ready")
        w_hi_ready, w_ready = sem("w_hi_ready"), sem("w_ready")
        coef_made, coef_hi_ready, coef_ready = sem("coef_made"), sem("coef_hi_ready"), sem("coef_ready")
        piece_due = sem("piece_due")
        fw_hi_ready, fw_ready = sem("fw_hi_ready"), sem("fw_ready")
        turned_ready, q_ready, k_ready = sem("turned_ready"), sem("q_ready"), sem("k_ready")
        scores_ready, masked, max_ready, exp_ready = sem("scores_ready"), sem("masked"), sem("max_ready"), sem("exp_ready")
        inv_ready, prob_ready = sem("inv_ready"), sem("prob_ready")
        pt_full, pt_ready = sem("pt_full"), sem("pt_ready")
        ot_full, ot_hi_ready, ot_ready = sem("ot_full"), sem("ot_hi_ready"), sem("ot_ready")
        wo_full, acc_added = sem("wo_full"), sem("acc_added")
        stats_step, stats_ready, ln_step, ln_inv_ready, ln_ready = (
            sem("stats_step"), sem("stats_ready"), sem("ln_step"), sem("ln_inv_ready"), sem("ln_ready"))
        tables_step = sem("tables_step")
        exts_set = sem("exts_set")
        decay_exp = sem("decay_exp")
        x1t_full, k_copied = sem("x1t_full"), sem("k_copied")
        top_ready, aa_ready, bb_ready = sem("top_ready"), sem("aa_ready"), sem("bb_ready")
        out_gap_ready, state_gap_ready = sem("out_gap_ready"), sem("state_gap_ready")
        e_old_arg, e_new_arg, keep_arg, add_k_arg = sem("e_old_arg"), sem("e_new_arg"), sem("keep_arg"), sem("add_k_arg")
        e_old_ready, e_new_ready, keep_ready, add_k_ready, add_v_ready = (
            sem("e_old_ready"), sem("e_new_ready"), sem("keep_ready"), sem("add_k_ready"), sem("add_v_ready"))
        den_old_ready, num_old_ready, new_v_ready = sem("den_old_ready"), sem("num_old_ready"), sem("new_v_ready")
        den_ready, den_inv_ready, num_ready, y_ready = (
            sem("den_ready"), sem("den_inv_ready"), sem("num_ready"), sem("y_ready"))
        y_full, y_added = sem("y_full"), sem("y_added")
        x2t_full, x2t_hi, x2t_ready = sem("x2t_full"), sem("x2t_hi"), sem("x2t_ready")
        gate_full, up_full, tanh_ready = sem("gate_full"), sem("up_full"), sem("tanh_ready")
        gate_used, up_used = sem("gate_used"), sem("up_used")
        inner_hi_ready, inner_ready, down_half_full, down_full, down_added = (
            sem("inner_hi_ready"), sem("inner_ready"), sem("down_half_full"), sem("down_full"), sem("down_added"))

        def weight_views(w, p, part):
            if w < 2:
                dst = fw[w][part][:, bass.ds(CHUNK * p, CHUNK)].rearrange("p (h i) -> p h i", h=DC)
                return dst, made[:, w, :].rearrange("p (i h) -> p h i", h=DC)
            per = CHUNK // IB
            dst = fw[w][part][:, :].rearrange("p (i h) -> p i h", i=IB)[:, :, bass.ds(per * p, per)]
            return dst, made[:, w, :].rearrange("p (h i) -> p i h", i=IB)

        block = stack.enter_context(nc.Block())

        @block.sync
        def _(sp):
            def three_times(dst, src):
                for n in range(3):
                    ins = sp.dma_start(dst[32 * n:32 * n + 32], src)
                    yield ins

            def load_lora_b(e):
                for ins in three_times(lb_raw, lora_b[bass.ds(e, 1), :, :].rearrange("a r n -> (a r) n")):
                    ins.then_inc(got_lb, 16)

            def load_w(p):
                sp.dma_start(w_raw[:, :, :].rearrange("p k n -> p (k n)"),
                             w_qkv[bass.ds(p, 1), :, :].rearrange("a p n -> (a p) n")).then_inc(got_w, 16)

            def load_wo(p):
                sp.dma_start(wo_raw[:, :], w_o[bass.ds(p, 1), :, :].rearrange("a p n -> (a p) n")
                             ).then_inc(got_wo, 16)

            def load_spline(p):
                sp.dma_start(knot_rows[:, :], knots[bass.ds(p, 1), :, :].rearrange("a p n -> (a p) n")
                             ).then_inc(got_knots, 16)
                for n in range(3):
                    sp.dma_start(spline_tab[32 * n:32 * n + 32, :, :].rearrange("p k n -> p (k n)"),
                                 spline[bass.ds(p, 1), :, :].rearrange("a p n -> (a p) n")).then_inc(got_tab, 16)

            def load_piece(p):
                sp.dma_start(second[:, :], piece[bass.ds(p, 1), :, :].rearrange("a p n -> (a p) n")
                             ).then_inc(got_second, 16)

            x_view = x.rearrange("b t d -> t b d")
            for g in range(GROUPS):
                sp.dma_start(x_raw[:, GB * g:GB * g + GB, :], x_view[:, GB * g:GB * g + GB, :]
                             ).then_inc((got_x0, got_x1)[g], 16)
                if g == 0:
                    for n in range(3):
                        sp.dma_start(la_raw[32 * n:32 * n + 32, :, :].rearrange("p k n -> p (k n)"), lora_a
                                     ).then_inc(got_la, 16)
                    load_lora_b(0)
                    load_w(0)
            load_spline(0)
            load_piece(0)
            load_wo(0)
            sp.dma_start(v_t[:, :, :], ctx_t.rearrange("(c p) t -> p c t", p=P)).then_inc(got_v, 16)
            sp.wait_ge(lb_ready, 1)
            load_lora_b(1)

            with sp.Fori(0, PAIRS - 1) as i:
                sp.wait_ge(blk_free, block_at(i, BLK_LV) + 1)
                load_w(i + 1)
                sp.wait_ge(coef_made, i + 1)
                load_spline(i + 1)
                sp.wait_ge(lb_ready, i + 2)
                load_lora_b(i + 2)
                sp.wait_ge(blk_free, block_at(i, BLK_LWO) + 1)
                load_wo(i + 1)
                sp.wait_ge(blk_free, block_at(i, BLK_GEN + 2) + 1)
                load_piece(i + 1)

            out_view = out.rearrange("b t d -> t b d")
            for b, batches in ((0, GB), (GB, 2), (GB + 2, 2)):
                sp.wait_ge(ln_ready, 2 * B + b + batches)
                sp.dma_start(out_view[:, b:b + batches, :], x_raw[:, b:b + batches, :]).then_inc(stored, 16)
            sp.wait_ge(stored, 16 * 3)

        @block.tensor
        def _(pe):
            def product(dst, lhs, rhs, first, last):
                (lh, ll), (rh, rl) = lhs, rhs
                pe.matmul(dst, lh, rh, start=first, stop=False, skip_group_check=True)
                pe.matmul(dst, lh, rl, start=False, stop=False, skip_group_check=True)
                return pe.matmul(dst, ll, rh, start=False, stop=last, skip_group_check=True)

            def bank_for(p, k):
                wait_for(pe, blk_free, bank_user_before(p, k) + 1)
                return ring[k % RING]

            def lora_qk(p, hh, k):
                bank = bank_for(p, k)
                for m in range(2):
                    for dc in range(DC):
                        n = 2 * m + dc
                        mm = pe.matmul(bank[:, P * n:P * n + P], la[:, m, P * dc:P * dc + P],
                                       lb[:, P * hh:P * hh + P], start=True, stop=True)
                mm.then_inc(blk_full, 1)

            def lora_v(p):
                bank = bank_for(p, BLK_LV)
                for dc in range(DC):
                    mm = pe.matmul(bank[:, 256 * dc:256 * dc + 256], la[:, 2, P * dc:P * dc + P],
                                   lb[:, 256:512], start=True, stop=True)
                mm.then_inc(blk_full, 1)

            def lora_o(p):
                wait_for(pe, lb_ready, p + 2)
                bank = bank_for(p, BLK_LWO)
                for hh in range(2):
                    mm = pe.matmul(bank[:, 256 * hh:256 * hh + 256], lb[:, 512 + P * hh:512 + P * hh + P],
                                   la[:, 3, :], start=True, stop=True)
                mm.then_inc(blk_full, 1)

            def project(p, c, m):
                g, hh = c // 2, c % 2
                wait_for(pe, w_ready, 4 * p + 1 + hh)
                bank = bank_for(p, (BLK_Q, BLK_K)[m][c])
                cols = slice(GT * g, GT * g + GT)
                for dc in range(DC):
                    w = [wqk[hh][part][:, 2 * m + dc, :] for part in range(2)]
                    mm = product(bank[:, :], w, (xt_hi[:, dc, cols], xt_lo[:, dc, cols]), dc == 0, dc == DC - 1)
                mm.then_inc(blk_full, 1)

            def values(p, g):
                wait_for(pe, w_ready, 4 * p + 3)
                for j in range(2):
                    bank = bank_for(p, (BLK_V0, BLK_V1)[g] + j)
                    for n in range(2):
                        b = GB * g + 2 * j + n
                        for dc in range(DC):
                            xs = [t[:, dc, T * b:T * b + T] for t in (xt_hi, xt_lo)]
                            mm = product(bank[:, 256 * n:256 * n + 256], xs, [wv[part][:, dc, :] for part in range(2)],
                                         dc == 0, dc == DC - 1)
                    mm.then_inc(blk_full, 1)

            def spline_weights(p, w):
                wait_for(pe, coef_ready, p + 1)
                bank = bank_for(p, BLK_GEN + w)
                pe.matmul(bank[:, :], phi[0:96, w, :], coef_hi[:, :, :].rearrange("p a n -> p (a n)"),
                          start=True, stop=False)
                pe.matmul(bank[:, :], phi[0:96, w, :], coef_lo[:, :, :].rearrange("p a n -> p (a n)"),
                          start=False, stop=True).then_inc(blk_full, 1)

            def scores(u, par):
                wait_for(pe, q_ready, u + 1)
                wait_for(pe, k_ready, u + 1)
                wait_for(pe, masked, u)
                for b in range(GB):
                    mm = pe.matmul(s_bank[:, T * b:T * b + T], q_t[par][:, b, :], k_t[par][:, b, :],
                                   start=True, stop=True)
                mm.then_inc(scores_ready, 1)

            def turn_probs(u, par):
                wait_for(pe, prob_ready, u + 1)
                wait_for(pe, ot_ready, u)
                for b in range(GB):
                    mm = pe.transpose(to_bank[:, T * b:T * b + T], prob[par][:, b, :], ident)
                mm.then_inc(pt_full, 1)

            def probs_v(u, p, c):
                g, hh = c // 2, c % 2
                wait_for(pe, pt_ready, u + 1)
                wait_for(pe, blk_free, block_at(p, (BLK_V0, BLK_V1)[g] + 1) + 1)
                for b in range(GB):
                    mm = pe.matmul(to_bank[:, T * b:T * b + T], v_now[g][:, b, DH * hh:DH * hh + DH], pt[:, b, :],
                                   start=True, stop=True)
                mm.then_inc(ot_full, 1)

            def out_project(u, p, c):
                g, hh = c // 2, c % 2
                wait_for(pe, ot_ready, u + 1)
                if hh == 0:
                    wait_for(pe, w_ready, 4 * p + 4)
                    if not (isinstance(u, int) and u == 0):
                        wait_for(pe, acc_added, 1 + 4 * p + 2 * g)
                for b in range(GB):
                    o = (ot_hi[:, b, :], ot_lo[:, b, :])
                    mm = product(wo_bank[b // 2][:, 256 * (b % 2):256 * (b % 2) + 256], o,
                                 [wo[part][:, hh, :] for part in range(2)], hh == 0 and b % 2 == 0, hh == 1)
                mm.then_inc(wo_full, 1)

            def slot(s, p, c):
                static = isinstance(s, int)
                active = not static or s < UNITS
                if active:
                    project(p, c, 0)
                    project(p, c, 1)
                if not static or 0 <= s - 1 < UNITS:
                    scores(s - 1, (c + 1) % 2)
                if not static or 0 <= s - 2 < UNITS:
                    turn_probs(s - 2, c % 2)
                if not static or 0 <= s - 3 < UNITS:
                    out_project(s - 3, p - (c < 3), (c + 1) % 4)
                if active:
                    if c == 0:
                        lora_v(p)
                    if c == 1:
                        values(p, 0)
                    if c == 2:
                        lora_o(p)
                        spline_weights(p, 0)
                        spline_weights(p, 1)
                    if static and s == UNITS - 1:
                        probs_v(s - 2, p, 1)
                    if c == 3:
                        values(p, 1)
                        if not static or p + 1 < PAIRS:
                            lora_qk(p, 1, BLK_LQK1)
                if not static or 0 <= s - 2 < UNITS - 3:
                    probs_v(s - 2, p - (c < 2), (c + 2) % 4)
                if active and c == 2:
                    spline_weights(p, 2)
                    if not static or p + 1 < PAIRS:
                        lora_qk(p, 0, BLK_LQK0)

            def x_to_features(g, banks, full):
                for dc in range(DC):
                    for j in range(GB):
                        b = GB * g + j
                        wait_for(pe, x_normed, b + 1)
                        mm = pe.transpose(banks[dc][:, T * j:T * j + T], acc[:, b, P * dc:P * dc + P], ident)
                    mm.then_inc(full, 1)

            pe.wait_ge(got_ident, 16)
            x_to_features(0, (ring[0], ring[3]), blk_full)
            pe.wait_ge(la_ready, 1)
            pe.wait_ge(lb_ready, 1)
            for hh in range(2):
                for m in range(2):
                    for dc in range(DC):
                        n = 2 * m + dc
                        mm = pe.matmul(ring[1 + hh][:, P * n:P * n + P], la[:, m, P * dc:P * dc + P],
                                       lb[:, P * hh:P * hh + P], start=True, stop=True)
                mm.then_inc(blk_full, 1)
            pe.wait_ge(blk_free, 4)
            slot(0, 0, 0)
            x_to_features(1, wo_bank, xt1_full)
            pe.wait_ge(phi_cast, 1)
            slot(1, 0, 1)
            pe.wait_ge(xt1_ready, DC)
            slot(2, 0, 2)
            slot(3, 0, 3)
            with pe.Fori(1, PAIRS - 1) as pair:
                for c in range(4):
                    slot(4 * pair + c, pair, c)
            for s in range(UNITS - 4, UNITS):
                slot(s, s // 4, s % 4)

            def x1_to_channels(g):
                wait_for(pe, ln_ready, GB * (2 * g + 1))
                wait_for(pe, blk_free, block_at(PAIRS - 1, BLK_V1 + 1) + 1)
                for c in range(DC):
                    for j in range(GB):
                        mm = pe.transpose(x1_bank[g][c][:, T * j:T * j + T],
                                          x_raw[:, GB * g + j, P * c:P * c + P], ident)
                    mm.then_inc(x1t_full, 1)

            def y_to_tokens(g):
                wait_for(pe, y_ready, DC * (g + 1))
                if g == 0:
                    wait_for(pe, masked, UNITS)
                    wait_for(pe, ot_ready, UNITS)
                for j, bank in enumerate((s_bank, to_bank)):
                    for n in range(2):
                        b = 2 * j + n
                        for c in range(DC):
                            mm = pe.transpose(bank[:, 256 * n + P * c:256 * n + P * c + P], y_t[c][:, b, :], ident)
                    mm.then_inc(y_full, 1)

            def x2_to_features(g):
                wait_for(pe, ln_ready, GB * (2 * g + 2))
                for c, bank in enumerate((s_bank, to_bank)):
                    for j in range(GB):
                        mm = pe.transpose(bank[:, T * j:T * j + T], x_raw[:, GB * g + j, P * c:P * c + P], ident)
                    mm.then_inc(x2t_full, 1)

            def down(g, ib):
                n = IB * g + ib
                wait_for(pe, inner_ready, n + 1)
                if ib == 0:
                    wait_for(pe, acc_added if g == 0 else down_added, 1 + 4 * PAIRS if g == 0 else 2 * g)
                for b in range(GB):
                    if b == 2 and ib == IB - 1:
                        mm.then_inc(down_half_full, 1)
                    a = [part[:, b, :] for part in inner_parts[n % 2]]
                    mm = product(wo_bank[b // 2][:, 256 * (b % 2):256 * (b % 2) + 256], a,
                                 [fw[2][part][:, 256 * ib:256 * ib + 256] for part in range(2)],
                                 ib == 0 and b % 2 == 0, ib == IB - 1)
                mm.then_inc(down_full, 1)

            def ffn(g, after_down):
                cols = slice(GT * g, GT * g + GT)
                wait_for(pe, x2t_ready, DC * (g + 1))
                for ib in range(IB):
                    n = IB * g + ib
                    for w, full, used in ((0, gate_full, gate_used), (1, up_full, up_used)):
                        wait_for(pe, used, n - 1)
                        if n < 2:
                            wait_for(pe, k_copied, DC * (n + 1))
                        for hb in range(DC):
                            at = 256 * ib + P * hb
                            mm = product(ring[2 * (n % 2) + w][:, :], [fw[w][part][:, at:at + P] for part in range(2)],
                                         (xt_hi[:, hb, cols], xt_lo[:, hb, cols]), hb == 0, hb == DC - 1)
                        mm.then_inc(full, 1)
                    if ib > 1:
                        down(g, ib - 2)
                        if ib - 2 in after_down:
                            after_down[ib - 2](1)
                for ib in (IB - 2, IB - 1):
                    down(g, ib)
                    if ib in after_down:
                        after_down[ib](1)

            scores(UNITS - 1, 1)
            out_project(UNITS - 3, PAIRS - 1, 1)
            turn_probs(UNITS - 2, 0)
            probs_v(UNITS - 2, PAIRS - 1, 2)
            out_project(UNITS - 2, PAIRS - 1, 2)
            x1_to_channels(0)
            turn_probs(UNITS - 1, 1)
            probs_v(UNITS - 1, PAIRS - 1, 3)
            out_project(UNITS - 1, PAIRS - 1, 3)
            y_to_tokens(0)
            x2_to_features(0)
            x1_to_channels(1)
            wait_for(pe, fw_ready, 3 * PAIRS)
            ffn(0, {IB - 4: y_to_tokens, IB - 2: x2_to_features})
            ffn(1, {})

        @block.scalar
        def _(act):
            copy = nc.scalar.activation

            def halves(p, c, m):
                k = (BLK_Q, BLK_K)[m][c]
                s = 4 * p + c
                wait_for(act, blk_full, block_at(p, k) + 1)
                wait_for(act, (q_ready, k_ready)[m], s)
                bank = ring[k % RING]
                flat = turned[m][:, :, :].rearrange("p b t -> p (b t)")
                copy(flat[0:64, :], bank[64:128, :], ACT.Copy)
                copy(flat[64:128, :], bank[0:64, :], ACT.Copy).then_inc(blk_mid, 1)

            def high_weights(n_parity, dst, free):
                wait_for(act, blk_free, free)
                copy(dst, w_sum[:, n_parity, :], ACT.Copy).then_inc(w_hi_ready, 1)

            def lora_high(e):
                wait_for(act, got_lb, 48 * (e + 1))
                copy(lb[:, :], lb_raw[:, :], ACT.Copy).then_inc(lb_hi_ready, 1)

            def flat3(t):
                return t.rearrange("p a b -> p (a b)")

            def exponentials(u, par):
                wait_for(act, max_ready, u + 1)
                wait_for(act, inv_ready, u)
                for b in range(GB):
                    ins = copy(prob[par][:, b, :], prob[par][:, b, :], ACT.Exp,
                               bias=neg_max[:, b:b + 1], scale=1.0, accum_out=row_sum[:, b:b + 1])
                ins.then_inc(exp_ready, 1)

            def first_piece(p, w):
                k = BLK_GEN + w
                wait_for(act, blk_full, block_at(p, k) + 1)
                wait_for(act, fw_ready, 3 * p - 2 + w)
                copy(made[:, w, :], ring[k % RING][:, 0:CHUNK], ACT.Copy).then_inc(blk_mid, 1)

            def high_spline(p, w):
                wait_for(act, blk_free, block_at(p, BLK_GEN + w) + 1)
                dst, src = weight_views(w, p, 0)
                copy(dst, src, ACT.Copy).then_inc(fw_hi_ready, 1)

            def copy_probs(u):
                wait_for(act, pt_full, u + 1)
                wait_for(act, ot_full, u)
                copy(flat3(pt[:, :, :]), to_bank[:, :], ACT.Copy).then_inc(pt_ready, 1)

            def high_out(u):
                wait_for(act, ot_full, u + 1)
                wait_for(act, wo_full, u)
                copy(flat3(ot_hi[:, :, :]), to_bank[:, :], ACT.Copy).then_inc(ot_hi_ready, 1)

            def slot(s, p, c):
                static = isinstance(s, int)
                active = not static or s < UNITS
                if active:
                    halves(p, c, 0)
                    halves(p, c, 1)
                if not static or 0 <= s - 2 < UNITS:
                    copy_probs(s - 2)
                if not static or 0 <= s - 1 < UNITS:
                    exponentials(s - 1, (c + 1) % 2)
                if active and c == 0:
                    wait_for(act, blk_full, block_at(p, BLK_LV) + 1)
                    high_weights(0, flat3(wv[0][:, :, :]), block_at(p, BLK_LV) + 1)
                if active and c == 1:
                    wait_for(act, blk_full, block_at(p, BLK_LV) + 1)
                    lora_high(p + 1)
                    wait_for(act, coef_made, p + 1)
                    if not static or p > 0:
                        wait_for(act, blk_full, block_at(p, BLK_GEN + 2) + 1 - PAIR_BLOCKS)
                    copy(flat3(coef_hi[:, :, :]), flat3(coef[:, :, :]), ACT.Copy).then_inc(coef_hi_ready, 1)
                if active and c == 2:
                    first_piece(p, 0)
                    first_piece(p, 1)
                    wait_for(act, blk_full, block_at(p, BLK_LWO) + 1)
                    wait_for(act, wo_full, 4 * p)
                    high_weights(1, flat3(wo[0][:, :, :]), block_at(p, BLK_LWO) + 1)
                    first_piece(p, 2)
                if not static or 0 <= s - 2 < UNITS:
                    high_out(s - 2)
                if c == 3 and (not static or p + 1 < PAIRS):
                    wait_for(act, blk_full, block_at(p, BLK_LQK1) + 1)
                    high_weights(1, flat3(wqk[1][0][:, :, :]), block_at(p, BLK_LQK1) + 1)
                if active and c == 2:
                    for w in range(3):
                        high_spline(p, w)
                    if not static or p + 1 < PAIRS:
                        wait_for(act, blk_full, block_at(p, BLK_LQK0) + 1)
                        high_weights(0, flat3(wqk[0][0][:, :, :]), block_at(p, BLK_LQK0) + 1)

            act.dma_start(cst[:, 0:2, :], consts[:, 0:2, :]).then_inc(got_ident, 16)
            act.dma_start(sm[:, :, :], small).then_inc(got_small, 16)

            def sum_squares(g):
                wait_for(act, (got_x0, got_x1)[g], 16)
                for b in range(GB * g, GB * g + GB):
                    if b:
                        act.wait_ge(squared, b)
                    copy(squares[:, :], x_raw[:, b, :], ACT.Square, accum_out=sum_sq[:, b:b + 1]).then_inc(squared, 1)

            def x_high(g, banks, full, full_before, ready):
                act.wait_ge(got_small, 16)
                for dc in range(DC):
                    act.wait_ge(full, full_before + dc + 1)
                    copy(xt_hi[:, dc, GT * g:GT * g + GT], banks[dc][:, :], ACT.Copy, scale=sm[:, 0, dc:dc + 1]
                         ).then_inc(ready, 1)

            sum_squares(0)
            act.wait_ge(got_la, 48)
            copy(la[:, :, :], la_raw[:, :, :], ACT.Copy).then_inc(la_hi_ready, 1)
            lora_high(0)
            act.dma_start(cst[:, 2:9, :], consts[:, 2:9, :]).then_inc(got_cst, 16)
            x_high(0, (ring[0], ring[3]), blk_full, 0, blk_mid)
            for hh in range(2):
                act.wait_ge(blk_full, 3 + hh)
                high_weights(hh, flat3(wqk[hh][0][:, :, :]), 3 + hh)
            sum_squares(1)
            act.wait_ge(got_cst, 16)
            copy(phi[:, :, :], cst[:, 6:9, :], ACT.Copy).then_inc(phi_cast, 1)
            copy(decay[:, :], sm[:, 1, :], ACT.Exp).then_inc(decay_exp, 1)

            slot(0, 0, 0)
            x_high(1, wo_bank, xt1_full, 0, xt1_hi_ready)
            for s in range(1, 4):
                slot(s, 0, s)
            with act.Fori(1, PAIRS - 1) as pair:
                for c in range(4):
                    slot(4 * pair + c, pair, c)
            for s in range(UNITS - 4, UNITS):
                slot(s, s // 4, s % 4)

            def copy_k(n):
                g, c = n // DC, n % DC
                wait_for(act, x1t_full, n + 1)
                wait_for(act, exts_set, 5)
                wait_for(act, out_gap_ready, n - 1)
                wait_for(act, state_gap_ready, n - 1)
                copy(k_ext[n % 2][:, :, 1:], x1_bank[g][c][:, :].rearrange("p (b t) -> p b t", b=GB), ACT.Copy
                     ).then_inc(k_copied, 1)

            def exponential(n, buf, argument, ready, scale=1.0):
                wait_for(act, argument, n + 1)
                copy(buf, buf, ACT.Exp, scale=scale).then_inc(ready, 1)

            def exp_keep(n):
                exponential(n, keep[:, :, 1:], keep_arg, keep_ready)

            def exp_add_k(n):
                wait_for(act, state_gap_ready, n + 1)
                wait_for(act, add_v_ready, n)
                wait_for(act, bb_ready, n)
                copy(add_k[:, :, 1:], state_gap[n], ACT.Relu).then_inc(add_k_arg, 1)
                exponential(n, add_k[:, :, 1:], add_k_arg, add_k_ready, scale=-1.0)

            def exp_old(n):
                wait_for(act, out_gap_ready, n + 1)
                wait_for(act, den_old_ready, n - 1)
                wait_for(act, num_old_ready, n - 1)
                copy(e_old[n % 2][:, :, :], out_gap[n % 2][:, :, :], ACT.Relu).then_inc(e_old_arg, 1)
                exponential(n, e_old[n % 2][:, :, :], e_old_arg, e_old_ready, scale=-1.0)

            def exp_new(n):
                wait_for(act, out_gap_ready, n + 1)
                wait_for(act, new_v_ready, n - 1)
                wait_for(act, den_ready, n - 1)
                copy(e_new[n % 2][:, :, :], out_gap[n % 2][:, :, :], ACT.Relu, scale=-1.0).then_inc(e_new_arg, 1)
                exponential(n, e_new[n % 2][:, :, :], e_new_arg, e_new_ready, scale=-1.0)

            def x2_high(g):
                for c, bank in enumerate((s_bank, to_bank)):
                    wait_for(act, x2t_full, DC * g + c + 1)
                    copy(xt_hi[:, c, GT * g:GT * g + GT], bank[:, :], ACT.Copy).then_inc(x2t_hi, 1)

            def ffn(g, between):
                def high(n):
                    wait_for(act, up_used, n + 1)
                    wait_for(act, down_full, n - 1)
                    copy(flat3(inner_parts[n % 2][0][:, :, :]), flat3(gated[n % 2][:, :, :]), ACT.Copy
                         ).then_inc(inner_hi_ready, 1)

                for ib in range(IB):
                    n = IB * g + ib
                    wait_for(act, gate_full, n + 1)
                    wait_for(act, gate_used, n - 1)
                    copy(flat3(th[n % 2]), ring[2 * (n % 2)][:, :], ACT.Tanh, scale=0.5).then_inc(tanh_ready, 1)
                    if ib:
                        high(n - 1)
                    for step, chunk in between[ib]:
                        step(chunk)
                high(IB * g + IB - 1)

            copy_probs(UNITS - 2)
            exponentials(UNITS - 1, 1)
            high_out(UNITS - 2)
            copy_k(0)
            copy_k(1)
            copy_probs(UNITS - 1)
            high_out(UNITS - 1)
            for n in range(DC):
                for step in (exp_keep, exp_add_k, exp_old, exp_new):
                    step(n)
            x2_high(0)
            copy_k(2)
            copy_k(3)
            ffn(0, [[(exp_keep, 2), (exp_add_k, 2), (exp_old, 2)], [(exp_new, 2)],
                    [(exp_keep, 3), (exp_add_k, 3)], [(exp_old, 3), (exp_new, 3)], [], [], [], []])
            x2_high(1)
            ffn(1, [[]] * IB)

        @block.vector
        def _(dve):
            v = nc.vector

            def flat3(t):
                return t.rearrange("p a b -> p (a b)")

            def flat(t):
                return flat3(t[:, :, :])

            def low(dst, src, high):
                return v.tensor_tensor(dst, src, high.bitcast(F32), ALU.subtract)

            def cosine(p, c, m):
                k = (BLK_Q, BLK_K)[m][c]
                wait_for(dve, blk_mid, mid_at(p, k) + 1)
                wait_for(dve, (q_ready, k_ready)[m], 4 * p + c)
                v.tensor_tensor(straight[m][:, :, :], ring[k % RING][:, :].rearrange("p (b t) -> p b t", b=GB),
                                rope_cos[m].unsqueeze(1).to_broadcast([P, GB, T]), ALU.mult).then_inc(blk_free, 1)

            def sum_weights(n, parity, k, blk, raw, got, count):
                wait_for(dve, blk_full, blk + 1)
                wait_for(dve, got, count)
                wait_for(dve, w_ready, n - 1)
                v.scalar_tensor_tensor(w_sum[:, parity, :], ring[k % RING][:, :], LORA_SCALE, raw, ALU.mult, ALU.add
                                       ).then_inc(blk_free, 1)

            def lora_low(e):
                wait_for(dve, lb_hi_ready, e + 1)
                low(lb[32:64, :], lb_raw[32:64, :], lb[32:64, :]).then_inc(lb_ready, 1)

            def add_rotated(u, p, c, m, ready):
                dst = (q_t, k_t)[m][c % 2]
                wait_for(dve, turned_ready, 2 * u + m + 1)
                wait_for(dve, blk_free, block_at(p, (BLK_Q, BLK_K)[m][c]) + 1)
                wait_for(dve, scores_ready, u - 1)
                v.tensor_tensor(dst[:, :, :], straight[m][:, :, :], turned[m][:, :, :], ALU.add).then_inc(ready, 1)

            def add_to_acc(u, p, g):
                wait_for(dve, wo_full, u + 1)
                wait_for(dve, acc_added, 1 + 4 * p)
                for j in range(2):
                    part = acc[:, GB * g + 2 * j:GB * g + 2 * j + 2, :]
                    v.tensor_tensor(flat3(part), wo_bank[j][:, :], flat3(part), ALU.add).then_inc(acc_added, 1)

            def new_values(p, g, j):
                k = (BLK_V0, BLK_V1)[g] + j
                wait_for(dve, blk_full, block_at(p, k) + 1)
                v.tensor_copy(flat3(v_now[g][:, 2 * j:2 * j + 2, :]), ring[k % RING][:, :]).then_inc(blk_free, 1)

            def second_piece(p, w):
                k = BLK_GEN + w
                wait_for(dve, blk_mid, mid_at(p, k) + 1)
                wait_for(dve, got_second, 16 * (p + 1))
                dve.sem_inc(piece_due, 1)
                v.copy_predicated(made[:, w, :], second[:, :], ring[k % RING][:, CHUNK:2 * CHUNK]
                                  ).then_inc(blk_free, 1)

            def low_spline(p, w):
                wait_for(dve, fw_hi_ready, 3 * p + w + 1)
                dst, src = weight_views(w, p, 1)
                low(dst, src, weight_views(w, p, 0)[0]).then_inc(fw_ready, 1)

            def mask_scores(u, par):
                wait_for(dve, scores_ready, u + 1)
                wait_for(dve, pt_full, u - 1)
                v.tensor_tensor(prob[par][:, :, :], s_bank[:, :].rearrange("p (b t) -> p b t", b=GB),
                                cst[:, 1, :].unsqueeze(1).to_broadcast([P, GB, T]), ALU.add).then_inc(masked, 1)
                wait_for(dve, masked, u + 1)
                wait_for(dve, exp_ready, u)
                v.tensor_reduce(neg_max[:, :], prob[par][:, :, :], AX.X, ALU.max, negate=True
                                ).then_inc(max_ready, 1)

            def invert_sums(u):
                wait_for(dve, exp_ready, u + 1)
                wait_for(dve, prob_ready, u)
                v.reciprocal(row_inv[:, :], row_sum[:, :]).then_inc(inv_ready, 1)

            def low_out(u):
                wait_for(dve, ot_hi_ready, u + 1)
                low(flat(ot_lo), to_bank[:, :], flat(ot_hi)).then_inc(ot_ready, 1)

            def slot(s, p, c):
                static = isinstance(s, int)
                active = not static or s < UNITS
                last = static and s == UNITS - 1
                if active:
                    cosine(p, c, 0)
                if not static or 0 <= s - 1 < UNITS:
                    mask_scores(s - 1, (c + 1) % 2)
                if active:
                    cosine(p, c, 1)
                    add_rotated(s, p, c, 0, q_ready)
                    add_rotated(s, p, c, 1, k_ready)
                if not static or 0 <= s - 1 < UNITS:
                    invert_sums(s - 1)
                if last:
                    low_out(s - 2)
                if active:
                    if c == 0:
                        sum_weights(4 * p + 2, 0, BLK_LV, block_at(p, BLK_LV), w_raw[:, 2, :], got_w, 16 * (p + 1))
                    if c in (1, 3):
                        new_values(p, c // 2, 0)
                        new_values(p, c // 2, 1)
                    if c == 2:
                        sum_weights(4 * p + 3, 1, BLK_LWO, block_at(p, BLK_LWO), wo_raw[:, :], got_wo, 16 * (p + 1))
                    if c == 1:
                        lora_low(p + 1)
                    if c == 2:
                        for w in range(3):
                            second_piece(p, w)
                    if c == 3 and (not static or p + 1 < PAIRS):
                        sum_weights(4 * p + 5, 1, BLK_LQK1, block_at(p, BLK_LQK1), w_raw[:, 1, :], got_w, 16 * (p + 2))
                if c == 0 and (not static or s >= 4):
                    add_to_acc(s - 3, p - 1, 0)
                if (not static or 0 <= s - 2) and not last:
                    low_out(s - 2)
                if active and c == 2 and (not static or p + 1 < PAIRS):
                    sum_weights(4 * p + 4, 0, BLK_LQK0, block_at(p, BLK_LQK0), w_raw[:, 0, :], got_w, 16 * (p + 2))
                if c == 2 and (not static or s >= 4):
                    add_to_acc(s - 3, p - 1, 1)
                if active and c == 2:
                    for w in range(3):
                        low_spline(p, w)

            def norm_stats(n, g, src, batches=range(GB)):
                half_at = n % 2
                wait_for(dve, ln_ready, GB * (n - 1))
                for j in batches:
                    v.bn_stats(stats[:, half_at, j, :], src[:, GB * g + j, :]).then_inc(stats_step, 1)
                for j in batches:
                    wait_for(dve, stats_step, GB * n + j + 1)
                    v.bn_aggr(mean_var[:, half_at, j, :], stats[:, half_at, j, :]).then_inc(stats_ready, 1)

            def norm_apply(n, g, src, part=None):
                half_at = n % 2
                batches = range(GB) if part is None else range(2 * part, 2 * part + 2)
                wait_for(dve, ln_inv_ready, n + 1 + (part or 0))
                wait_for(dve, stats_ready, GB * n + batches[-1] + 1)
                for j in batches:
                    b = GB * g + j
                    v.tensor_scalar(x_raw[:, b, :], src[:, b, :], mean_var[:, half_at, j, 0:1],
                                    ln_inv[:, half_at, j:j + 1], ALU.subtract, ALU.mult).then_inc(ln_ready, 1)

            def x_over_rms(g):
                wait_for(dve, rms_ready, g + 1)
                for b in range(GB * g, GB * g + GB):
                    v.tensor_scalar(acc[:, b, :], x_raw[:, b, :], rms_inv[:, b:b + 1], None, ALU.mult
                                    ).then_inc(x_normed, 1)

            def x_low(g, banks, high_ready, ready):
                dve.wait_ge(got_small, 16)
                for dc in range(DC):
                    cols = slice(GT * g, GT * g + GT)
                    dve.wait_ge(high_ready, dc + 1)
                    v.scalar_tensor_tensor(xt_lo[:, dc, cols], banks[dc][:, :], sm[:, 0, dc:dc + 1],
                                           xt_hi[:, dc, cols].bitcast(F32), ALU.mult, ALU.subtract).then_inc(ready, 1)

            x_over_rms(0)
            lora_low(0)
            x_low(0, (ring[0], ring[3]), blk_mid, blk_free)
            sum_weights(0, 0, 1, 2, w_raw[:, 0, :], got_w, 16)
            sum_weights(1, 1, 2, 3, w_raw[:, 1, :], got_w, 16)
            dve.wait_ge(w_hi_ready, 1)
            low(flat3(wqk[0][1][:, :, :]), w_sum[:, 0, :], flat3(wqk[0][0][:, :, :])).then_inc(w_ready, 1)
            x_over_rms(1)
            dve.wait_ge(got_cst, 16)
            slot(0, 0, 0)
            x_low(1, wo_bank, xt1_hi_ready, xt1_ready)
            slot(1, 0, 1)
            slot(2, 0, 2)
            slot(3, 0, 3)
            dve.wait_ge(xt1_full, DC)
            v.tensor_scalar(acc[:, :, :], x_raw[:, :, :], 2.0, None, ALU.mult).then_inc(acc_added, 1)
            with dve.Fori(1, PAIRS - 1) as pair:
                for c in range(4):
                    slot(4 * pair + c, pair, c)
            dve.wait_ge(decay_exp, 1)
            v.tensor_scalar(decay[:, :], decay[:, :], -1.0, None, ALU.mult).then_inc(tables_step, 1)
            for c in range(DC):
                v.memset(decay_tab[c][:, :, :], 0.0).then_inc(tables_step, 1)
            dve.wait_ge(tables_step, 1 + DC)
            for c in range(DC):
                v.tensor_scalar(decay_tab[c][:, :, :], decay_tab[c][:, :, :], decay[:, c:c + 1], None, ALU.add
                                ).then_inc(tables_step, 1)
            dve.wait_ge(tables_step, 1 + 2 * DC)
            for c in range(DC):
                v.memset(decay_tab[c][:, :, 0:1], FORGET).then_inc(tables_step, 1)
            v.memset(k_first[:, :, 0:1], NO_STATE).then_inc(exts_set, 1)
            for t in (keep, add_k, add_v):
                v.memset(t[:, :, 0:1], 0.0).then_inc(exts_set, 1)

            for s in range(UNITS - 4, UNITS):
                slot(s, s // 4, s % 4)

            def scan_top(n):
                wait_for(dve, k_copied, n + 1)
                wait_for(dve, out_gap_ready, n - 1)
                wait_for(dve, state_gap_ready, n - 1)
                v.tensor_tensor_scan(flat(top[n % 2]), flat(decay_tab[n % DC]), flat(k_ext[n % 2]), NO_STATE,
                                     ALU.add, ALU.max).then_inc(top_ready, 1)

            def make_state_gap(n):
                c = n % DC
                wait_for(dve, top_ready, n + 1)
                wait_for(dve, keep_arg, n - 1)
                wait_for(dve, add_k_arg, n - 1)
                v.scalar_tensor_tensor(state_gap[n], top[n % 2][:, :, 0:T], decay[:, c:c + 1],
                                       k_ext[n % 2][:, :, 1:], ALU.add, ALU.subtract).then_inc(state_gap_ready, 1)

            def make_out_gap(n):
                c = n % DC
                wait_for(dve, top_ready, n + 1)
                wait_for(dve, e_old_arg, n - 1)
                wait_for(dve, e_new_arg, n - 1)
                v.scalar_tensor_tensor(out_gap[n % 2][:, :, :], k_ext[n % 2][:, :, 1:], sm[:, 2, c:c + 1],
                                       top[n % 2][:, :, 0:T], ALU.add, ALU.subtract).then_inc(out_gap_ready, 1)

            def arg_keep(n):
                wait_for(dve, state_gap_ready, n + 1)
                wait_for(dve, aa_ready, n)
                wait_for(dve, bb_ready, n)
                v.tensor_scalar(keep[:, :, 1:], state_gap[n], 0.0, None, ALU.min).then_inc(keep_arg, 1)

            def scan_bb(n):
                wait_for(dve, keep_ready, n + 1)
                wait_for(dve, add_k_ready, n + 1)
                wait_for(dve, den_old_ready, n)
                v.tensor_tensor_scan(flat(bb), flat(keep), flat(add_k), 0.0, ALU.mult, ALU.add).then_inc(bb_ready, 1)

            def scan_aa(n):
                wait_for(dve, keep_ready, n + 1)
                wait_for(dve, add_v_ready, n + 1)
                wait_for(dve, num_old_ready, n)
                v.tensor_tensor_scan(flat(aa), flat(keep), flat(add_v), 0.0, ALU.mult, ALU.add).then_inc(aa_ready, 1)

            def invert_den(n):
                wait_for(dve, den_ready, n + 1)
                wait_for(dve, y_ready, n)
                v.reciprocal(den_inv[:, :, :], den[:, :, :]).then_inc(den_inv_ready, 1)

            def add_den(n):
                wait_for(dve, den_old_ready, n + 1)
                wait_for(dve, e_new_ready, n + 1)
                v.tensor_tensor(den[:, :, :], den[:, :, :], e_new[n % 2][:, :, :], ALU.add).then_inc(den_ready, 1)

            def add_num(n):
                wait_for(dve, num_old_ready, n + 1)
                wait_for(dve, new_v_ready, n + 1)
                v.tensor_tensor(num[:, :, :], num[:, :, :], new_v[:, :, :], ALU.add).then_inc(num_ready, 1)

            def make_y(n):
                g, c = n // DC, n % DC
                wait_for(dve, num_ready, n + 1)
                wait_for(dve, den_inv_ready, n + 1)
                wait_for(dve, y_full, 2 * g)
                v.tensor_tensor(y_t[c][:, :, :], num[:, :, :], den_inv[:, :, :], ALU.mult).then_inc(y_ready, 1)

            def add_y(g):
                for j, bank in enumerate((s_bank, to_bank)):
                    part = flat3(x_raw[:, GB * g + 2 * j:GB * g + 2 * j + 2, :])
                    wait_for(dve, y_full, 2 * g + j + 1)
                    v.tensor_tensor(part, bank[:, :], part, ALU.add).then_inc(y_added, 1)
                dve.wait_ge(y_added, 2 * g + 2)

            def x2_low(g):
                for c, bank in enumerate((s_bank, to_bank)):
                    cols = slice(GT * g, GT * g + GT)
                    wait_for(dve, x2t_hi, DC * g + c + 1)
                    low(xt_lo[:, c, cols], bank[:, :], xt_hi[:, c, cols]).then_inc(x2t_ready, 1)

            def ffn(g, between):
                for ib in range(IB):
                    n = IB * g + ib
                    wait_for(dve, tanh_ready, n + 1)
                    wait_for(dve, inner_ready, n - 1)
                    v.scalar_tensor_tensor(flat(gated[n % 2]), flat3(th[n % 2]), 1.0, ring[2 * (n % 2)][:, :],
                                           ALU.add, ALU.mult).then_inc(gate_used, 1)
                    wait_for(dve, gate_used, n + 1)
                    wait_for(dve, up_full, n + 1)
                    v.tensor_tensor(flat(gated[n % 2]), ring[2 * (n % 2) + 1][:, :], flat(gated[n % 2]), ALU.mult
                                    ).then_inc(up_used, 1)
                    for step, chunk in between[ib]:
                        step(chunk)

            def second_stats(g):
                norm_stats(2 * g + 1, g, x_raw)

            def second_apply(g):
                norm_apply(2 * g + 1, g, x_raw)

            def third_stats(g):
                norm_stats(4 + g, g, x_raw)

            def third_apply(g):
                norm_apply(4 + g, g, x_raw)

            def add_down_0(j):
                add_down(0, j)

            def add_down(g, j):
                if j == 0:
                    wait_for(dve, down_half_full, g + 1)
                else:
                    wait_for(dve, down_full, IB * (g + 1))
                part = flat3(x_raw[:, GB * g + 2 * j:GB * g + 2 * j + 2, :])
                v.scalar_tensor_tensor(part, wo_bank[j][:, :], 0.5, part, ALU.mult, ALU.add
                                       ).then_inc(down_added, 1)
                dve.wait_ge(down_added, 2 * g + j + 1)

            mask_scores(UNITS - 1, 1)
            add_to_acc(UNITS - 3, PAIRS - 1, 0)
            dve.wait_ge(acc_added, 1 + 4 * (PAIRS - 1) + 2)
            norm_stats(0, 0, acc)
            dve.wait_ge(w_ready, 4 * PAIRS)
            v.memset(k_second[:, :, 0:1], NO_STATE).then_inc(exts_set, 1)
            invert_sums(UNITS - 1)
            low_out(UNITS - 2)
            norm_apply(0, 0, acc)
            dve.wait_ge(tables_step, 1 + 3 * DC)
            dve.wait_ge(exts_set, 5)
            dve.wait_ge(got_v, 16)
            dve.wait_ge(ln_ready, GB)
            scan_top(0)
            make_state_gap(0)
            arg_keep(0)
            make_out_gap(0)
            low_out(UNITS - 1)
            scan_top(1)
            make_state_gap(1)
            scan_bb(0)
            make_out_gap(1)
            scan_aa(0)
            arg_keep(1)
            add_den(0)
            invert_den(0)
            scan_bb(1)
            scan_aa(1)
            add_num(0)
            make_y(0)
            add_den(1)
            invert_den(1)
            make_y(1)
            add_to_acc(UNITS - 1, PAIRS - 1, 1)
            add_y(0)
            second_stats(0)
            dve.wait_ge(acc_added, 1 + 4 * PAIRS)
            norm_stats(2, 1, acc)
            second_apply(0)
            norm_apply(2, 1, acc)
            x2_low(0)
            scan_top(2)
            make_state_gap(2)
            arg_keep(2)
            make_out_gap(2)
            ffn(0, [[(scan_top, 3), (scan_bb, 2)], [(scan_aa, 2), (make_state_gap, 3), (arg_keep, 3)],
                    [(make_out_gap, 3), (invert_den, 2)], [(scan_bb, 3)], [(scan_aa, 3)],
                    [(add_den, 3), (invert_den, 3), (add_num, 3), (make_y, 3)], [(add_y, 1), (second_stats, 1)],
                    [(second_apply, 1)]])
            x2_low(1)
            ffn(1, [[(add_down_0, 0), (add_down_0, 1)], [(third_stats, 0)], [], [(third_apply, 0)], [], [], [], []])
            n = GROUPS * IB - 1
            dve.wait_ge(inner_hi_ready, n + 1)
            dve.wait_ge(inner_ready, n)
            low(flat(inner_parts[n % 2][1]), flat(gated[n % 2]), flat(inner_parts[n % 2][0])).then_inc(inner_ready, 1)
            for part in range(2):
                add_down(1, part)
                norm_stats(5, 1, x_raw, range(2 * part, 2 * part + 2))
            for part in range(2):
                norm_apply(5, 1, x_raw, part)

        @block.gpsimd
        def _(pool):
            gp = nc.gpsimd

            def flat3(t):
                return t.rearrange("p a b -> p (a b)")

            def sine(p, c, m):
                s = 4 * p + c
                wait_for(pool, blk_mid, mid_at(p, (BLK_Q, BLK_K)[m][c]) + 1)
                gp.tensor_tensor(turned[m][:, :, :], turned[m][:, :, :],
                                 rope_sin[m].unsqueeze(1).to_broadcast([P, GB, T]), ALU.mult).then_inc(turned_ready, 1)

            def low_weights(n, parity, dst, high):
                wait_for(pool, w_hi_ready, n + 1)
                gp.tensor_tensor(dst, w_sum[:, parity, :], high.bitcast(F32), ALU.subtract).then_inc(w_ready, 1)

            def normalise(u, par):
                wait_for(pool, inv_ready, u + 1)
                gp.tensor_tensor(prob[par][:, :, :], prob[par][:, :, :],
                                 row_inv[:, :].unsqueeze(2).to_broadcast([P, GB, T]), ALU.mult
                                 ).then_inc(prob_ready, 1)

            def slot(s, p, c):
                static = isinstance(s, int)
                active = not static or s < UNITS
                if active and c == 0 and (not static or p > 0):
                    low_weights(4 * p + 1, 1, flat3(wqk[1][1][:, :, :]), flat3(wqk[1][0][:, :, :]))
                if c == 3 and (not static or p + 1 < PAIRS):
                    low_weights(4 * p + 4, 0, flat3(wqk[0][1][:, :, :]), flat3(wqk[0][0][:, :, :]))
                if active:
                    sine(p, c, 0)
                    sine(p, c, 1)
                if active and c == 1:
                    wait_for(pool, got_knots, 16 * (p + 1))
                    wait_for(pool, got_tab, 48 * (p + 1))
                    wait_for(pool, coef_ready, p)
                    gp.tensor_tensor(coef[:, :, :], spline_tab[:, :, :],
                                     knot_rows[:, :].unsqueeze(1).to_broadcast([96, 2, CHUNK]), ALU.mult
                                     ).then_inc(coef_made, 1)
                if not static or 0 <= s - 1 < UNITS:
                    normalise(s - 1, (c + 1) % 2)
                if active and c == 0:
                    low_weights(4 * p + 2, 0, flat3(wv[1][:, :, :]), flat3(wv[0][:, :, :]))
                if active and c == 1:
                    wait_for(pool, coef_hi_ready, p + 1)
                    gp.tensor_tensor(flat3(coef_lo[:, :, :]), flat3(coef[:, :, :]),
                                     flat3(coef_hi[:, :, :]).bitcast(F32), ALU.subtract).then_inc(coef_ready, 1)
                if active and c == 2:
                    low_weights(4 * p + 3, 1, flat3(wo[1][:, :, :]), flat3(wo[0][:, :, :]))

            gp.memset(half[:, :], -0.5).then_inc(half_set, 1)
            pool.wait_ge(half_set, 1)

            def rms_inverse(g):
                cols = slice(GB * g, GB * g + GB)
                pool.wait_ge(squared, GB * (g + 1))
                gp.tensor_scalar(mean_sq[:, cols], sum_sq[:, cols], 1.0 / D, RMS_EPS, ALU.mult, ALU.add
                                 ).then_inc(rms_step, 1)
                pool.wait_ge(rms_step, g + 1)
                gp.tensor_tensor(rms_inv[:, cols], mean_sq[:, cols], half[:, cols], ALU.pow).then_inc(rms_ready, 1)

            rms_inverse(0)
            pool.wait_ge(rms_ready, 1)
            pool.wait_ge(la_hi_ready, 1)
            gp.tensor_tensor(la[64:96, :, :], la_raw[64:96, :, :], la[64:96, :, :].bitcast(F32), ALU.subtract
                             ).then_inc(la_ready, 1)
            pool.wait_ge(la_ready, 1)
            pool.wait_ge(w_ready, 1)
            low_weights(1, 1, flat3(wqk[1][1][:, :, :]), flat3(wqk[1][0][:, :, :]))
            rms_inverse(1)
            pool.wait_ge(got_cst, 16)

            for s in range(4):
                slot(s, 0, s)
            with pool.Fori(1, PAIRS - 1) as pair:
                for c in range(4):
                    slot(4 * pair + c, pair, c)
            for s in range(UNITS - 4, UNITS):
                slot(s, s // 4, s % 4)

            def norm_inverse(n, part=None):
                half_at = n % 2
                at = slice(0, GB) if part is None else slice(2 * part, 2 * part + 2)
                count = n + 1 + (part or 0)
                wait_for(pool, stats_ready, GB * n + at.stop)
                wait_for(pool, ln_ready, GB * (n - 1))
                gp.tensor_scalar(var_eps[:, half_at, at], mean_var[:, half_at, at, 1], LN_EPS, None, ALU.add
                                 ).then_inc(ln_step, 1)
                wait_for(pool, ln_step, count)
                gp.tensor_tensor(ln_inv[:, half_at, at], var_eps[:, half_at, at], half[:, at], ALU.pow
                                 ).then_inc(ln_inv_ready, 1)

            def v_part(n):
                g, c = n // DC, n % DC
                return v_t[:, c, GT * g:GT * g + GT].rearrange("p (b t) -> p b t", b=GB)

            def make_add_v(n):
                wait_for(pool, add_k_ready, n + 1)
                wait_for(pool, aa_ready, n)
                gp.tensor_tensor(add_v[:, :, 1:], add_k[:, :, 1:], v_part(n), ALU.mult).then_inc(add_v_ready, 1)

            def old_den(n):
                wait_for(pool, bb_ready, n + 1)
                wait_for(pool, e_old_ready, n + 1)
                wait_for(pool, den_inv_ready, n)
                gp.tensor_tensor(den[:, :, :], e_old[n % 2][:, :, :], bb[:, :, 0:T], ALU.mult
                                 ).then_inc(den_old_ready, 1)

            def old_num(n):
                wait_for(pool, aa_ready, n + 1)
                wait_for(pool, e_old_ready, n + 1)
                wait_for(pool, y_ready, n)
                gp.tensor_tensor(num[:, :, :], e_old[n % 2][:, :, :], aa[:, :, 0:T], ALU.mult
                                 ).then_inc(num_old_ready, 1)

            def make_new_v(n):
                wait_for(pool, e_new_ready, n + 1)
                wait_for(pool, num_ready, n)
                gp.tensor_tensor(new_v[:, :, :], e_new[n % 2][:, :, :], v_part(n), ALU.mult).then_inc(new_v_ready, 1)

            def add_den(n):
                wait_for(pool, den_old_ready, n + 1)
                wait_for(pool, e_new_ready, n + 1)
                gp.tensor_tensor(den[:, :, :], den[:, :, :], e_new[n % 2][:, :, :], ALU.add).then_inc(den_ready, 1)

            def add_num(n):
                wait_for(pool, num_old_ready, n + 1)
                wait_for(pool, new_v_ready, n + 1)
                gp.tensor_tensor(num[:, :, :], num[:, :, :], new_v[:, :, :], ALU.add).then_inc(num_ready, 1)

            def make_y(n):
                g, c = n // DC, n % DC
                wait_for(pool, num_ready, n + 1)
                wait_for(pool, den_inv_ready, n + 1)
                wait_for(pool, y_full, 2 * g)
                gp.tensor_tensor(y_t[c][:, :, :], num[:, :, :], den_inv[:, :, :], ALU.mult).then_inc(y_ready, 1)

            def ffn(g, between):
                for ib in range(IB):
                    n = IB * g + ib
                    for step, chunk in between[ib]:
                        step(chunk)
                    if n < GROUPS * IB - 1:
                        wait_for(pool, inner_hi_ready, n + 1)
                        hi, lo = inner_parts[n % 2]
                        gp.tensor_tensor(lo[:, :, :], gated[n % 2][:, :, :], hi[:, :, :].bitcast(F32), ALU.subtract
                                         ).then_inc(inner_ready, 1)

            norm_inverse(0)
            normalise(UNITS - 1, 1)
            pool.wait_ge(got_v, 16)
            make_add_v(0)
            old_den(0)
            old_num(0)
            make_add_v(1)
            pool.wait_ge(ot_full, UNITS)
            make_new_v(0)
            old_den(1)
            old_num(1)
            make_new_v(1)
            add_num(1)
            norm_inverse(1)
            norm_inverse(2)
            ffn(0, [[(make_add_v, 2), (old_den, 2)], [(add_den, 2), (old_num, 2)], [(make_new_v, 2), (add_num, 2)],
                    [(make_add_v, 3), (make_y, 2)], [(old_den, 3)],
                    [(old_num, 3), (make_new_v, 3)], [], [(norm_inverse, 3)]])
            ffn(1, [[], [], [(norm_inverse, 4)], [], [], [], [], []])
            norm_inverse(5, 0)
            norm_inverse(5, 1)


def spline_tables():
    import numpy as np

    knots_n = max(16, int(INTER * D / 128.9))
    t = np.linspace(0.0, knots_n - 1.0, D * INTER, dtype=np.float64)
    interval = np.clip(np.floor(t).astype(np.int64), 0, knots_n - 2).reshape(COLUMNS, P)
    j = np.arange(COLUMNS)
    base = 127 * (j // P) + j % P - 2
    first = interval[:, 0]
    second = (interval != first[:, None]).T.astype(np.int32)
    catmull = 0.5 * np.array([[0, -1, 2, -1], [2, 0, -5, 3], [0, 1, 4, -3], [0, 0, -1, 1]], np.float64)
    table = np.zeros((32, 2, COLUMNS))
    for side in (0, 1):
        a = t.reshape(COLUMNS, P)[:, 64] - first - side
        s = 64 * t[1]
        powers = np.zeros((4, 4, COLUMNS))
        powers[0, 0] = 1
        powers[1, 0], powers[1, 1] = a, s
        powers[2, 0], powers[2, 1], powers[2, 2] = a ** 2, 2 * a * s, s * s
        powers[3, 0], powers[3, 1], powers[3, 2], powers[3, 3] = a ** 3, 3 * a ** 2 * s, 3 * a * s * s, s ** 3
        for k in range(4):
            kk = np.clip(first + side - 1 + k, 0, knots_n - 1) - base
            co = np.einsum("m,mrj->rj", catmull[k], powers)
            ok = (kk >= 0) & (kk < 6)
            for r in range(5):
                np.add.at(table[:, side], (np.where(ok, kk * 5 + r, 31), j), np.where(ok, co[min(r, 3)], 0))
    q = (np.arange(P) - 64) / 64.0
    mantissa, exponent = np.frexp(q ** 3)
    high = np.ldexp(np.rint(mantissa * 4096) / 4096, exponent)
    phi = np.zeros((32, P))
    for kk in range(6):
        phi[5 * kk:5 * kk + 5] = [q ** 0, q, q * q, high, q ** 3 - high]
    return table.astype(np.float32), second, phi.astype(np.float32)


def constant_tables(phi):
    import numpy as np

    half = DH // 2
    theta = (1.0 / 10000.0 ** (np.arange(half) / half)).astype(np.float32)
    angle = (np.arange(T, dtype=np.float32)[:, None] * theta[None, :]).astype(np.float64).T
    cos = np.concatenate([np.cos(angle), np.cos(angle)])
    sin = np.concatenate([-np.sin(angle), np.sin(angle)])
    consts = np.zeros((P, 9, P), np.float32)
    scale = DH ** -0.5
    consts[:, 0] = np.eye(P)
    consts[:, 2], consts[:, 3], consts[:, 4], consts[:, 5] = cos * scale, sin * scale, cos, sin
    i, j = np.arange(T)[:, None], np.arange(T)[None, :]
    consts[:, 1] = np.where((j <= i) & (j >= i - WINDOW + 1), 0.0, MASKED)
    for w in range(3):
        consts[32 * w:32 * w + 32, 6 + w] = phi
    return consts


def lay_out(inputs):
    import numpy as np

    a = {k.replace("L0_", "").replace("attn_", ""): np.asarray(v) for k, v in inputs.items()}
    f = np.float32
    table, second, phi = spline_tables()
    arrays = {"x": a["x"], "ctx_t": np.ascontiguousarray(a["ctx_2048"].reshape(B * T, D).T)}
    arrays["small"] = np.ascontiguousarray(np.stack(
        [a["norm_w"], a["xtime_decay"], a["xtime_first"]]).reshape(3, DC, P).transpose(2, 0, 1))
    arrays["consts"] = constant_tables(phi)

    lora_a = np.zeros((32, 4, D), f)
    lora_a[0:16, 0], lora_a[16:32, 1], lora_a[0:16, 2] = a["qA"], a["kA"], a["vA"]
    lora_a[0:16, 3] = a["oB"].T
    arrays["lora_a"] = lora_a.reshape(32, 4 * D)
    lora_b = np.zeros((PAIRS + 1, 32, 3, 2 * DH), f)
    by_pair = lambda m: m.reshape(RANK, PAIRS, 2 * DH).transpose(1, 0, 2)
    lora_b[:PAIRS, 0:16, 0], lora_b[:PAIRS, 16:32, 0] = by_pair(a["qB"].T), by_pair(a["kB"].T)
    lora_b[:PAIRS, 0:16, 1] = by_pair(a["vB"].T)
    lora_b[1:, 0:16, 2] = by_pair(a["oA"])
    arrays["lora_b"] = lora_b.reshape(PAIRS + 1, 32, 3 * 2 * DH)

    w_qkv = np.zeros((PAIRS, P, 3, 512), f)
    q = a["wq"].reshape(PAIRS, 2, DH, DC, P).transpose(0, 4, 1, 3, 2)
    k = a["wk"].reshape(PAIRS, 2, DH, DC, P).transpose(0, 4, 1, 3, 2)
    w_qkv[:, :, 0:2, 0:256] = q.reshape(PAIRS, P, 2, 256)
    w_qkv[:, :, 0:2, 256:512] = k.reshape(PAIRS, P, 2, 256)
    v = a["wv"].reshape(PAIRS, 2 * DH, DC, P).transpose(0, 3, 2, 1)
    w_qkv[:, :, 2] = v.reshape(PAIRS, P, 512)
    arrays["w_qkv"] = w_qkv.reshape(PAIRS, P, 3 * 512)
    arrays["w_o"] = np.ascontiguousarray(
        a["wo"].reshape(D, PAIRS, 2, DH).transpose(1, 3, 2, 0)).reshape(PAIRS, DH, 512)

    knots = np.zeros((3, 32, 16, P), f)
    for w, name in enumerate(("ffn_gate_cp", "ffn_up_cp", "ffn_down_cp")):
        padded = np.pad(a[name], (2, 8))
        for kk in range(6):
            for jb in range(16):
                knots[w, 5 * kk:5 * kk + 5, jb] = padded[127 * jb + kk:127 * jb + kk + P]
    arrays["knots"] = np.ascontiguousarray(
        knots.reshape(96, PAIRS, CHUNK).transpose(1, 0, 2))
    arrays["spline"] = np.ascontiguousarray(
        table.reshape(32, 2, PAIRS, CHUNK).transpose(2, 0, 1, 3)).reshape(PAIRS, 32, 2 * CHUNK)
    arrays["piece"] = np.ascontiguousarray(second.reshape(P, PAIRS, CHUNK).transpose(1, 0, 2))
    return arrays


def kernel(**inputs):
    import numpy as _np
    import concourse.bacc as _bacc
    from concourse import mybir as _mybir
    from concourse.bass_utils import run_bass_kernel_spmd as _run

    nc = _bacc.Bacc("TRN2", target_bir_lowering=False, num_devices=1)
    arrays, args = {}, []
    for name, a in lay_out(inputs).items():
        a = _np.ascontiguousarray(a)
        arrays[f"in_{name}_dram"] = a
        args.append(nc.dram_tensor(f"in_{name}_dram", a.shape, _mybir.dt.from_np(a.dtype), kind="ExternalInput").ap())
    args.append(nc.dram_tensor("out_0_dram", (B, T, D), F32, kind="ExternalOutput").ap())
    decoder_layer(nc, *args)
    r = _run(nc, [arrays], core_ids=[0])
    return r.results[0]["out_0_dram"]
```
